# Optimizing a Trainium2 kernel written in Bass

```python
import numpy as np
import jax
import jax.numpy as jnp

def _softmax(x, axis=-1):
    return jax.nn.softmax(x, axis=axis)

def _gelu(x):
    return jax.nn.gelu(x, approximate=True)

def _silu(x):
    return jax.nn.silu(x)

def _sigmoid(x):
    return jax.nn.sigmoid(x)

def _layernorm(x, axis=-1, eps=1e-05):
    m = jnp.mean(x, axis=axis, keepdims=True)
    v = jnp.var(x, axis=axis, keepdims=True)
    return (x - m) / jnp.sqrt(v + eps)

def _scatter_add(tgt, idx, src, axis=0):
    return tgt.at[idx].add(src)

def _segment_sum(src, seg, n):
    return jax.ops.segment_sum(src, seg, n)
kernel_name = 'mk_pixart_seq_d2_seqx_r2_b9030a'

def setup_inputs(seed: int=0):
    np.random.seed(seed)
    _w = jnp.asarray

    def _rec_inputs():
        import jax
        import jax.numpy as jnp
        _rk = jax.random.key(seed)
        x = -0.0003929 + 0.9999 * jax.random.normal(jax.random.fold_in(_rk, 1), (8, 224, 512), jnp.float32)
        _lenS = 224 - jax.random.randint(jax.random.fold_in(_rk, 7), (8,), 0, max(1, 224 // 4) + 1, jnp.int32)
        _lenS2 = 750 - jax.random.randint(jax.random.fold_in(_rk, 8), (8,), 0, max(1, 750 // 4) + 1, jnp.int32)
        cond_1024 = 0.00782532 + 1.00527 * jax.random.normal(jax.random.fold_in(_rk, 11), (8, 512), jnp.float32)
        _ctx_1024P = jax.random.normal(jax.random.fold_in(_rk, 12), (8, 16, 512), jnp.float32)
        _ctx_1024c = jax.random.dirichlet(jax.random.fold_in(_rk, 512), 0.3 * jnp.ones((16,), jnp.float32), (8, 750))
        _ctx_1024t = jnp.einsum('bsk,bkd->bsd', _ctx_1024c, _ctx_1024P)
        _ctx_1024t = _ctx_1024t * jax.lax.rsqrt(jnp.mean(jnp.square(_ctx_1024t)) + 1e-12) * 0.953939
        ctx_1024 = -0.000761806 + 0.999296 * (_ctx_1024t + 0.3 * jax.random.normal(jax.random.fold_in(_rk, 612), (8, 750, 512), jnp.float32))
        return (x, cond_1024, ctx_1024)
    x, cond_1024, ctx_1024 = _rec_inputs()

    def _L0_xcond_setup():
        import jax, jax.numpy as jnp
        import numpy as np
        H = 512
        RH = 2 * H
        E = 3
        B, T, P = (8, 1024, 64)
        LN_EPS = 1e-05

        def _layer_norm(x, gamma, beta):
            mu = jnp.mean(x, axis=-1, keepdims=True)
            var = jnp.mean(jnp.square(x - mu), axis=-1, keepdims=True)
            return (x - mu) * jax.lax.rsqrt(var + LN_EPS) * gamma + beta
        key = jax.random.key(seed)
        ks = jax.random.split(key, 24)
        s = lambda fan_in: 1.0 / np.sqrt(fan_in)
        inp = {'mix_hidden_states': jax.random.normal(ks[0], (B, T, H), jnp.float32), 'global_anchor': jax.random.normal(ks[1], (B, H), jnp.float32), 'prototype_bank': jax.random.normal(ks[2], (B, P, H), jnp.float32), 'ln_gamma': jnp.ones((H,), jnp.float32), 'ln_beta': jnp.zeros((H,), jnp.float32), 'Wq': jax.random.normal(ks[3], (H, H), jnp.float32) * s(H), 'Wk': jax.random.normal(ks[4], (H, H), jnp.float32) * s(H), 'Wv': jax.random.normal(ks[5], (H, H), jnp.float32) * s(H), 'router_W': jax.random.normal(ks[6], (3 * H, E), jnp.float32) * s(3 * H), 'router_b': jnp.zeros((E,), jnp.float32), 'e_w1': jax.random.normal(ks[7], (E, 3 * H, RH), jnp.float32) * s(3 * H), 'e_b1': jnp.zeros((E, RH), jnp.float32), 'e_w2': jax.random.normal(ks[8], (E, RH, H), jnp.float32) * s(RH), 'e_b2': jnp.zeros((E, H), jnp.float32), 'gate_w1': jax.random.normal(ks[9], (3 * H, H), jnp.float32) * s(3 * H), 'gate_b1': jnp.zeros((H,), jnp.float32), 'gate_w2': jax.random.normal(ks[10], (H, H), jnp.float32) * s(H), 'gate_b2': jnp.zeros((H,), jnp.float32), 'out_w': jax.random.normal(ks[11], (H, H), jnp.float32) * s(H), 'out_b': jnp.zeros((H,), jnp.float32)}
        return inp
    _L0_xcond_all = _L0_xcond_setup()
    _L0_xcond_in = {k: v for k, v in _L0_xcond_all.items() if k in ('ln_gamma', 'ln_beta', 'Wq', 'Wk', 'Wv', 'router_W', 'router_b', 'e_w1', 'e_b1', 'e_w2', 'e_b2', 'gate_w1', 'gate_b1', 'gate_w2', 'gate_b2', 'out_w', 'out_b')}
    del _L0_xcond_all

    def _L1_xcond_setup():
        import jax, jax.numpy as jnp
        import numpy as np
        LN_EPS = 1e-06

        def _ln(x):
            mu = jnp.mean(x, axis=-1, keepdims=True)
            var = jnp.var(x, axis=-1, keepdims=True)
            return (x - mu) * jax.lax.rsqrt(var + LN_EPS)
        key = jax.random.key(seed)
        H, NH = (512, 16)
        B, N, S = (4, 512, 77)
        MLP = int(H * 4.0)
        ks = jax.random.split(key, 20)
        s = 1.0 / np.sqrt(H)
        return {'x': jax.random.normal(ks[0], (B, N, H), jnp.float32), 'c': jax.random.normal(ks[1], (B, H), jnp.float32), 'context': jax.random.normal(ks[2], (B, S, H), jnp.float32), 'W_mod': jax.random.normal(ks[3], (H, 6 * H), jnp.float32) * s, 'b_mod': jnp.zeros((6 * H,), jnp.float32), 'W_qkv': jax.random.normal(ks[4], (H, 3 * H), jnp.float32) * s, 'b_qkv': jnp.zeros((3 * H,), jnp.float32), 'W_proj': jax.random.normal(ks[5], (H, H), jnp.float32) * s, 'b_proj': jnp.zeros((H,), jnp.float32), 'W_qc': jax.random.normal(ks[6], (H, H), jnp.float32) * s, 'b_qc': jnp.zeros((H,), jnp.float32), 'W_kvc': jax.random.normal(ks[7], (H, 2 * H), jnp.float32) * s, 'b_kvc': jnp.zeros((2 * H,), jnp.float32), 'W_cproj': jax.random.normal(ks[8], (H, H), jnp.float32) * s, 'b_cproj': jnp.zeros((H,), jnp.float32), 'W_mlp1': jax.random.normal(ks[9], (H, MLP), jnp.float32) * s, 'b_mlp1': jnp.zeros((MLP,), jnp.float32), 'W_mlp2': jax.random.normal(ks[10], (MLP, H), jnp.float32) * (1.0 / np.sqrt(MLP)), 'b_mlp2': jnp.zeros((H,), jnp.float32)}
    _L1_xcond_all = _L1_xcond_setup()
    _L1_xcond_in = {k: v for k, v in _L1_xcond_all.items() if k in ('W_mod', 'b_mod', 'W_qkv', 'b_qkv', 'W_proj', 'b_proj', 'W_qc', 'b_qc', 'W_kvc', 'b_kvc', 'W_cproj', 'b_cproj', 'W_mlp1', 'b_mlp1', 'W_mlp2', 'b_mlp2')}
    del _L1_xcond_all
    return {'x': x, 'cond_1024': cond_1024, 'ctx_1024': ctx_1024, 'L0_xcond_ln_gamma': _L0_xcond_in['ln_gamma'], 'L0_xcond_ln_beta': _L0_xcond_in['ln_beta'], 'L0_xcond_Wq': _L0_xcond_in['Wq'], 'L0_xcond_Wk': _L0_xcond_in['Wk'], 'L0_xcond_Wv': _L0_xcond_in['Wv'], 'L0_xcond_router_W': _L0_xcond_in['router_W'], 'L0_xcond_router_b': _L0_xcond_in['router_b'], 'L0_xcond_e_w1': _L0_xcond_in['e_w1'], 'L0_xcond_e_b1': _L0_xcond_in['e_b1'], 'L0_xcond_e_w2': _L0_xcond_in['e_w2'], 'L0_xcond_e_b2': _L0_xcond_in['e_b2'], 'L0_xcond_gate_w1': _L0_xcond_in['gate_w1'], 'L0_xcond_gate_b1': _L0_xcond_in['gate_b1'], 'L0_xcond_gate_w2': _L0_xcond_in['gate_w2'], 'L0_xcond_gate_b2': _L0_xcond_in['gate_b2'], 'L0_xcond_out_w': _L0_xcond_in['out_w'], 'L0_xcond_out_b': _L0_xcond_in['out_b'], 'L1_xcond_W_mod': _L1_xcond_in['W_mod'], 'L1_xcond_b_mod': _L1_xcond_in['b_mod'], 'L1_xcond_W_qkv': _L1_xcond_in['W_qkv'], 'L1_xcond_b_qkv': _L1_xcond_in['b_qkv'], 'L1_xcond_W_proj': _L1_xcond_in['W_proj'], 'L1_xcond_b_proj': _L1_xcond_in['b_proj'], 'L1_xcond_W_qc': _L1_xcond_in['W_qc'], 'L1_xcond_b_qc': _L1_xcond_in['b_qc'], 'L1_xcond_W_kvc': _L1_xcond_in['W_kvc'], 'L1_xcond_b_kvc': _L1_xcond_in['b_kvc'], 'L1_xcond_W_cproj': _L1_xcond_in['W_cproj'], 'L1_xcond_b_cproj': _L1_xcond_in['b_cproj'], 'L1_xcond_W_mlp1': _L1_xcond_in['W_mlp1'], 'L1_xcond_b_mlp1': _L1_xcond_in['b_mlp1'], 'L1_xcond_W_mlp2': _L1_xcond_in['W_mlp2'], 'L1_xcond_b_mlp2': _L1_xcond_in['b_mlp2']}

def reference(x, cond_1024, ctx_1024, L0_xcond_ln_gamma, L0_xcond_ln_beta, L0_xcond_Wq, L0_xcond_Wk, L0_xcond_Wv, L0_xcond_router_W, L0_xcond_router_b, L0_xcond_e_w1, L0_xcond_e_b1, L0_xcond_e_w2, L0_xcond_e_b2, L0_xcond_gate_w1, L0_xcond_gate_b1, L0_xcond_gate_w2, L0_xcond_gate_b2, L0_xcond_out_w, L0_xcond_out_b, L1_xcond_W_mod, L1_xcond_b_mod, L1_xcond_W_qkv, L1_xcond_b_qkv, L1_xcond_W_proj, L1_xcond_b_proj, L1_xcond_W_qc, L1_xcond_b_qc, L1_xcond_W_kvc, L1_xcond_b_kvc, L1_xcond_W_cproj, L1_xcond_b_cproj, L1_xcond_W_mlp1, L1_xcond_b_mlp1, L1_xcond_W_mlp2, L1_xcond_b_mlp2):
    import jax
    import jax.numpy as jnp

    def _L0_xcond_ref(mix_hidden_states, global_anchor, prototype_bank, ln_gamma, ln_beta, Wq, Wk, Wv, router_W, router_b, e_w1, e_b1, e_w2, e_b2, gate_w1, gate_b1, gate_w2, gate_b2, out_w, out_b):
        import jax, jax.numpy as jnp
        import numpy as np
        H = 512
        RH = 2 * H
        E = 3
        B, T, P = (8, 1024, 64)
        LN_EPS = 1e-05

        def _layer_norm(x, gamma, beta):
            mu = jnp.mean(x, axis=-1, keepdims=True)
            var = jnp.mean(jnp.square(x - mu), axis=-1, keepdims=True)
            return (x - mu) * jax.lax.rsqrt(var + LN_EPS) * gamma + beta
        x = mix_hidden_states
        nx = _layer_norm(x, ln_gamma, ln_beta)
        q = nx @ Wq
        k = prototype_bank @ Wk
        v = prototype_bank @ Wv
        scores = jnp.einsum('bth,bph->btp', q, k) * H ** (-0.5)
        weights = jax.nn.softmax(scores, axis=-1)
        evidence = jnp.einsum('btp,bph->bth', weights, v)
        anchor = jnp.broadcast_to(global_anchor[:, None, :], nx.shape)
        combined = jnp.concatenate([nx, evidence, anchor], axis=-1)
        router_logits = combined @ router_W + router_b
        router_probs = jax.nn.softmax(router_logits, axis=-1)
        h = jax.nn.silu(jnp.einsum('btc,ecr->bter', combined, e_w1) + e_b1)
        expert_out = jnp.einsum('bter,erh->bteh', h, e_w2) + e_b2
        routed = jnp.sum(expert_out * router_probs[..., None], axis=-2)
        g = jax.nn.sigmoid(jax.nn.silu(combined @ gate_w1 + gate_b1) @ gate_w2 + gate_b2)
        refined_delta = g * (routed @ out_w + out_b)
        return x + refined_delta

    def _L1_xcond_ref(x, c, context, W_mod, b_mod, W_qkv, b_qkv, W_proj, b_proj, W_qc, b_qc, W_kvc, b_kvc, W_cproj, b_cproj, W_mlp1, b_mlp1, W_mlp2, b_mlp2):
        import jax, jax.numpy as jnp
        import numpy as np
        LN_EPS = 1e-06

        def _ln(x):
            mu = jnp.mean(x, axis=-1, keepdims=True)
            var = jnp.var(x, axis=-1, keepdims=True)
            return (x - mu) * jax.lax.rsqrt(var + LN_EPS)
        B, N, H = x.shape
        NH = 16
        hd = H // NH
        scale = hd ** (-0.5)
        c_proj = jax.nn.silu(c) @ W_mod + b_mod
        shift_a, scale_a, gate_a, shift_m, scale_m, gate_m = jnp.split(c_proj, 6, axis=-1)

        def modulate(t, shift, sc):
            return t * (1 + sc[:, None]) + shift[:, None]
        x_norm = modulate(_ln(x), shift_a, scale_a)
        qkv = x_norm @ W_qkv + b_qkv
        q, k, v = jnp.split(qkv, 3, axis=-1)
        q = q.reshape(B, N, NH, hd).transpose(0, 2, 1, 3)
        k = k.reshape(B, N, NH, hd).transpose(0, 2, 1, 3)
        v = v.reshape(B, N, NH, hd).transpose(0, 2, 1, 3)
        attn_w = jax.nn.softmax(jnp.einsum('bhqd,bhkd->bhqk', q, k) * scale, axis=-1)
        attn_out = jnp.einsum('bhqk,bhkd->bhqd', attn_w, v)
        attn_out = attn_out.transpose(0, 2, 1, 3).reshape(B, N, H)
        attn_out = attn_out @ W_proj + b_proj
        x = x + gate_a[:, None] * attn_out
        S = context.shape[1]
        q_c = _ln(x) @ W_qc + b_qc
        kv_c = _ln(context) @ W_kvc + b_kvc
        k_c, v_c = jnp.split(kv_c, 2, axis=-1)
        q_c = q_c.reshape(B, N, NH, hd).transpose(0, 2, 1, 3)
        k_c = k_c.reshape(B, S, NH, hd).transpose(0, 2, 1, 3)
        v_c = v_c.reshape(B, S, NH, hd).transpose(0, 2, 1, 3)
        c_attn_w = jax.nn.softmax(jnp.einsum('bhqd,bhsd->bhqs', q_c, k_c) * scale, axis=-1)
        c_attn_out = jnp.einsum('bhqs,bhsd->bhqd', c_attn_w, v_c)
        c_attn_out = c_attn_out.transpose(0, 2, 1, 3).reshape(B, N, H)
        c_attn_out = c_attn_out @ W_cproj + b_cproj
        x = x + c_attn_out
        x_norm2 = modulate(_ln(x), shift_m, scale_m)
        h = jax.nn.gelu(x_norm2 @ W_mlp1 + b_mlp1)
        h = h @ W_mlp2 + b_mlp2
        x = x + gate_m[:, None] * h
        return x
    x = _L0_xcond_ref(x, cond_1024, ctx_1024, L0_xcond_ln_gamma, L0_xcond_ln_beta, L0_xcond_Wq, L0_xcond_Wk, L0_xcond_Wv, L0_xcond_router_W, L0_xcond_router_b, L0_xcond_e_w1, L0_xcond_e_b1, L0_xcond_e_w2, L0_xcond_e_b2, L0_xcond_gate_w1, L0_xcond_gate_b1, L0_xcond_gate_w2, L0_xcond_gate_b2, L0_xcond_out_w, L0_xcond_out_b)
    x = _L1_xcond_ref(x, cond_1024, ctx_1024, L1_xcond_W_mod, L1_xcond_b_mod, L1_xcond_W_qkv, L1_xcond_b_qkv, L1_xcond_W_proj, L1_xcond_b_proj, L1_xcond_W_qc, L1_xcond_b_qc, L1_xcond_W_kvc, L1_xcond_b_kvc, L1_xcond_W_cproj, L1_xcond_b_cproj, L1_xcond_W_mlp1, L1_xcond_b_mlp1, L1_xcond_W_mlp2, L1_xcond_b_mlp2)
    return x

_drawn_inputs = setup_inputs


def setup_inputs(seed=0):
    import zlib

    import numpy as np

    out = dict(_drawn_inputs(seed))
    spreads = {'L0_xcond_ln_gamma': (1.0, 0.6),
     'L0_xcond_ln_beta': (0.0, 0.649),
     'L0_xcond_router_b': (0.0, 0.8),
     'L0_xcond_e_b1': (0.0, 0.417),
     'L0_xcond_e_b2': (0.0, 0.1),
     'L0_xcond_gate_b1': (0.0, 0.8),
     'L0_xcond_gate_b2': (0.0, 0.8),
     'L0_xcond_out_b': (0.0, 0.1),
     'L1_xcond_b_mod': (0.0, 0.1),
     'L1_xcond_b_qkv': (0.0, 0.1),
     'L1_xcond_b_proj': (0.0, 0.1),
     'L1_xcond_b_qc': (0.0, 0.529),
     'L1_xcond_b_kvc': (0.0, 0.1),
     'L1_xcond_b_cproj': (0.0, 0.1),
     'L1_xcond_b_mlp1': (0.0, 0.1),
     'L1_xcond_b_mlp2': (0.0, 0.1)}
    factors = {}
    for name, (base, spread) in spreads.items():
        noise = np.random.default_rng([zlib.crc32(name.encode()), seed]).standard_normal(out[name].shape)
        drawn = base * np.exp(spread * noise) if base else spread * noise
        out[name] = jnp.asarray(drawn.astype(out[name].dtype))
    for name, factor in factors.items():
        out[name] = (out[name] * factor).astype(out[name].dtype)
    return out
```

```python
import concourse.bass as bass
from concourse import mybir
from contextlib import ExitStack

FP32 = mybir.dt.float32
F32R = mybir.dt.float32r
ALU = mybir.AluOpType
ACT = mybir.ActivationFunctionType
AX = mybir.AxisListType

B, T, D, S = 8, 224, 512, 750
R = B * T
P = 128
KD = D // P
QT = T // 2
GROUP = 2 * T
NG = R // GROUP
TPG = GROUP // QT
KC, KCH = S // 6, 6
HALF = S // 2
HALF_E, S_E = HALF + HALF % 2, S + 2
NH, HD = 16, 32
E, HID = 3, 1024
HCH = HID // P
MLP = 2048
SCALE0, SCALE1 = float(D) ** -0.5, float(HD) ** -0.5
EPS0, EPS1 = 1e-5, 1e-6


def three_passes(nc, out, lhs_hi, lhs_lo, rhs_hi, rhs_lo, first, last):
    nc.tensor.matmul(out, lhs_lo, rhs_hi, start=first, stop=False)
    nc.tensor.matmul(out, lhs_hi, rhs_lo, start=False, stop=False)
    return nc.tensor.matmul(out, lhs_hi, rhs_hi, start=False, stop=last)


def batches(eng, step):
    step(0, 0, True, True)
    step(1, 1, True, True)
    with eng.Fori(1, B // 2 - 1) as i:
        for par in range(2):
            step(2 * i + par, par, True, True)
    step(B - 2, 0, True, False)
    step(B - 1, 1, False, False)


def after_first(eng, b, sem, value):
    if not isinstance(b, int) or b > 0:
        eng.wait_ge(sem, value)


def conditioning(nc, dram, const):
    ident, vecs, mod, anchor = const["ident"], const["vecs"], const["mod"], const["anchor"]
    NM = 6 * KD
    NA = (E + 1) * HCH - HCH // 2
    names = [("b_mod", 24), ("e_b1", 24), ("gate_b1", 4), ("ln_gamma", 4), ("ln_beta", 4), ("b_qkv", 12),
             ("b_qc", 4), ("b_kvc", 8), ("b_mlp1", 16)]
    with ExitStack() as ctx:
        sb = lambda name, shape, dt=FP32: ctx.enter_context(nc.sbuf_tensor("cd_" + name, shape, dt))
        sem = lambda name: ctx.enter_context(nc.semaphore("cd_" + name))
        rows = sb("rows", [VECS, P])
        cond = sb("cond", [B, D])
        silu = sb("silu", [B, D])
        condT = sb("condT", [P, KD, B])
        siluT = sb("siluT", [P, KD, B])
        w_mod = sb("w_mod", [P, KD, 6 * D])
        w_e1 = sb("w_e1", [P, E, KD, HID])
        w_g1 = sb("w_g1", [P, KD, D])
        w_r = sb("w_r", [P, KD, E])
        r_bias = sb("r_bias", [E, 1])
        g_bias = sb("g_bias", [B, 2, D])
        gates = sb("gates", [B, 2, D])
        w_q, w_k = sb("w_q", [P, KD, D]), sb("w_k", [P, KD, D])
        wt_hi = sb("wt_hi", [P, 2, KD, D], F32R)
        wt_lo = sb("wt_lo", [P, 2, KD, D], F32R)
        w_qk = sb("w_qk", [P, KD, D])
        ps = ctx.enter_context(nc.psum_tensor("cd_ps", [P, 6, 512], FP32))
        ps_f = ctx.enter_context(nc.psum_tensor("cd_ps_f", [P, 2, 512], FP32))
        qk_loaded = [sem("q_loaded"), sem("k_loaded")]
        wt_tr, wt_hi_done, wt_lo_done, fold_mm, fold_done = sem("wt_tr"), sem("wt_hi_done"), sem("wt_lo_done"), sem("fold_mm"), sem("fold_done")
        vec_loaded, small_loaded, mod_loaded = sem("vec_loaded"), sem("small_loaded"), sem("mod_loaded")
        anchor_loaded, ident_done = sem("anchor_loaded"), sem("ident_done")
        silu_done, tr_done, copied, mod_mm, mod_done = sem("silu_done"), sem("tr_done"), sem("copied"), sem("mod_mm"), sem("mod_done")
        stored = sem("stored")
        block = ctx.enter_context(nc.Block())

        @block.sync
        def _(sp):
            for i, (w, name) in enumerate(((w_q, "Wq"), (w_k, "Wk"))):
                sp.dma_start(w[:, :, :], dram[name].rearrange("(k p) n -> p k n", p=P)).then_inc(qk_loaded[i], 16)
            n = 0
            for name, k in names:
                sp.dma_start(rows[n:n + k, :], dram["rows_" + name]).then_inc(vec_loaded, 16)
                n += k
            sp.dma_start(cond[:, :], dram["cond"]).then_inc(small_loaded, 16)
            sp.dma_start(w_mod[:, :, :], dram["W_mod"].rearrange("(k p) n -> p k n", p=P)).then_inc(mod_loaded, 16)
            sp.wait_ge(fold_done, KD)
            sp.dma_start(dram["W_qk"].rearrange("(k p) n -> p k n", p=P), w_qk[:, :, :]).then_inc(stored, 16)
            sp.wait_ge(mod_done, 5)
            sp.dma_start(dram["gates"], gates[:, :, :]).then_inc(stored, 16)
            sp.wait_ge(stored, 32)

        @block.gpsimd
        def _(pool):
            nc.gpsimd.memset(ident[:, :], 0.0).then_inc(ident_done, 1)
            pool.wait_ge(ident_done, 1)
            nc.gpsimd.affine_select(out=ident[:, :], in_=ident[:, :], compare_op=ALU.not_equal, fill=1.0, base=0,
                                    pattern=[[-1, P]], channel_multiplier=1).then_inc(ident_done, 1)

        @block.scalar
        def _(act):
            for e in range(E):
                act.dma_start(w_e1[:, e, :, :], dram["e_w1"][e, 2 * D:, :].rearrange("(k p) n -> p k n", p=P)).then_inc(anchor_loaded, 16)
            act.dma_start(w_g1[:, :, :], dram["gate_w1"][2 * D:, :].rearrange("(k p) n -> p k n", p=P)).then_inc(anchor_loaded, 16)
            act.dma_start(w_r[:, :, :], dram["router_W"][2 * D:, :].rearrange("(k p) n -> p k n", p=P)).then_inc(anchor_loaded, 16)
            act.dma_start(r_bias[:, :], dram["router_b"].rearrange("(e o) -> e o", o=1)).then_inc(anchor_loaded, 16)
            for i, part in enumerate((2, 5)):
                act.dma_start(g_bias[:, i, :], dram["b_mod"][part * D:(part + 1) * D].partition_broadcast(B)).then_inc(anchor_loaded, 16)
            for n in range(2 * KD):
                act.wait_ge(wt_tr, n + 1)
                nc.scalar.activation(wt_hi[:, n // KD, n % KD, :], ps_f[:, n % 2, :], ACT.Copy).then_inc(wt_hi_done, 1)
            act.wait_ge(small_loaded, 16)
            nc.scalar.activation(silu[:, :], cond[:, :], ACT.Silu).then_inc(silu_done, 1)

        @block.vector
        def _(dve):
            for n in range(2 * KD):
                dve.wait_ge(wt_hi_done, n + 1)
                nc.vector.tensor_tensor(wt_lo[:, n // KD, n % KD, :], ps_f[:, n % 2, :],
                                        wt_hi[:, n // KD, n % KD, :].bitcast(FP32), ALU.subtract).then_inc(wt_lo_done, 1)
            for n in range(KD):
                dve.wait_ge(fold_mm, n + 1)
                nc.vector.tensor_scalar(w_qk[:, n, :], ps_f[:, n % 2, :], SCALE0, None, ALU.mult).then_inc(fold_done, 1)
            dve.wait_ge(tr_done, 1)
            nc.vector.tensor_copy(vecs["all"][:, :], ps[:, 0, 0:VECS]).then_inc(copied, 1)
            dve.wait_ge(tr_done, 2)
            nc.vector.tensor_copy(condT[:, :, :], ps[:, 1, 0:KD * B].rearrange("p (k b) -> p k b", k=KD)).then_inc(copied, 1)
            nc.vector.tensor_copy(siluT[:, :, :], ps[:, 1, 64:64 + KD * B].rearrange("p (k b) -> p k b", k=KD)).then_inc(copied, 1)
            dve.wait_ge(mod_mm, 1)
            dve.wait_ge(copied, 1)
            for name, k in (("b_qkv", KD), ("b_qc", KD)):
                last = nc.vector.tensor_scalar(vecs[name][:, 0:k], vecs[name][:, 0:k], SCALE1, None, ALU.mult)
            last.then_inc(mod_done, 1)
            wide = lambda v, n: v.unsqueeze(2).to_broadcast([P, n, B])
            nc.vector.tensor_tensor(mod[:, :, :], ps[:, 2, 0:NM * B].rearrange("p (n b) -> p n b", b=B),
                                    wide(vecs["b_mod"], NM), ALU.add).then_inc(mod_done, 1)
            dve.wait_ge(mod_done, 2)
            for part in (1, 4):
                last = nc.vector.tensor_scalar(mod[:, part * KD:(part + 1) * KD, :], mod[:, part * KD:(part + 1) * KD, :],
                                               1.0, None, ALU.add)
            last.then_inc(mod_done, 1)
            dve.wait_ge(mod_mm, 2)
            dve.wait_ge(anchor_loaded, 128)
            nc.vector.tensor_tensor(gates[:, 0, :], ps[:B, 3, :], g_bias[:, 0, :], ALU.add).then_inc(mod_done, 1)
            nc.vector.tensor_tensor(gates[:, 1, :], ps[:B, 4, :], g_bias[:, 1, :], ALU.add).then_inc(mod_done, 1)
            dve.wait_ge(mod_mm, 3)
            nc.vector.tensor_tensor(anchor[:, :, :], ps[:, 5, 0:NA * B].rearrange("p (n b) -> p n b", b=B),
                                    wide(vecs["hidden"], NA), ALU.add).then_inc(mod_done, 1)
            nc.vector.tensor_scalar(const["router_anchor"][:, :], ps[:E, 5, 256:256 + B], r_bias[:, :], None, ALU.add).then_inc(mod_done, 1)

        @block.tensor
        def _(pe):
            pe.wait_ge(ident_done, 2)
            for n in range(2 * KD):
                if n % KD == 0:
                    pe.wait_ge(qk_loaded[n // KD], 16)
                if n >= 2:
                    pe.wait_ge(wt_lo_done, n - 1)
                w = (w_q, w_k)[n // KD]
                for k in range(KD):
                    last = nc.tensor.transpose(ps_f[:, n % 2, k * P:(k + 1) * P], w[:, k, n % KD * P:(n % KD + 1) * P], ident[:, :])
                last.then_inc(wt_tr, 1)
            pe.wait_ge(wt_lo_done, 2 * KD)
            for n in range(KD):
                if n >= 2:
                    pe.wait_ge(fold_done, n - 1)
                i = slice(n * P, (n + 1) * P)
                for k in range(KD):
                    last = three_passes(nc, ps_f[:, n % 2, :], wt_hi[:, 0, k, i], wt_lo[:, 0, k, i], wt_hi[:, 1, k, :],
                                        wt_lo[:, 1, k, :], k == 0, k == KD - 1)
                last.then_inc(fold_mm, 1)
            pe.wait_ge(vec_loaded, 16 * len(names))
            nc.tensor.transpose(ps[:, 0, 0:VECS], rows[:, :], ident[:VECS, :VECS]).then_inc(tr_done, 1)
            pe.wait_ge(small_loaded, 16)
            pe.wait_ge(silu_done, 1)
            for k in range(KD):
                nc.tensor.transpose(ps[:, 1, k * B:(k + 1) * B], cond[:, k * P:(k + 1) * P], ident[:B, :B])
                last = nc.tensor.transpose(ps[:, 1, 64 + k * B:64 + (k + 1) * B], silu[:, k * P:(k + 1) * P], ident[:B, :B])
            last.then_inc(tr_done, 1)
            pe.wait_ge(copied, 3)
            pe.wait_ge(mod_loaded, 16)
            for n in range(NM):
                for k in range(KD):
                    last = nc.tensor.matmul(ps[:, 2, n * B:(n + 1) * B], w_mod[:, k, n * P:(n + 1) * P], siluT[:, k, :],
                                            start=k == 0, stop=k == KD - 1)
            last.then_inc(mod_mm, 1)
            for i, part in enumerate((2, 5)):
                for k in range(KD):
                    last = nc.tensor.matmul(ps[:B, 3 + i, :], siluT[:, k, :], w_mod[:, k, part * D:(part + 1) * D],
                                            start=k == 0, stop=k == KD - 1)
            last.then_inc(mod_mm, 1)
            pe.wait_ge(anchor_loaded, 128)
            for n in range(NA):
                for k in range(KD):
                    if n < E * HCH:
                        w = w_e1[:, n // HCH, k, n % HCH * P:(n % HCH + 1) * P]
                    else:
                        w = w_g1[:, k, (n - E * HCH) * P:(n - E * HCH + 1) * P]
                    nc.tensor.matmul(ps[:, 5, n * B:(n + 1) * B], w, condT[:, k, :], start=k == 0, stop=k == KD - 1)
            for k in range(KD):
                last = nc.tensor.matmul(ps[:E, 5, 256:256 + B], w_r[:, k, :], condT[:, k, :], start=k == 0, stop=k == KD - 1)
            last.then_inc(mod_mm, 1)


def context_kv(nc, dram, const):
    ident, vecs = const["ident"], const["vecs"]
    ctx_view = dram["ctx"].rearrange("b (p c) d -> b p c d", c=KCH)
    w_view = dram["W_kvc"].rearrange("(k p) n -> p k n", p=P)
    NCK = 2 * KD
    NC = NCK + KCH
    T0 = KCH
    with ExitStack() as ctx:
        sb = lambda name, shape, dt=FP32: ctx.enter_context(nc.sbuf_tensor("kv_" + name, shape, dt))
        sem = lambda name: ctx.enter_context(nc.semaphore("kv_" + name))
        w_raw = sb("w_raw", [P, KD, 2 * D])
        w_hi, w_lo = sb("w_hi", [P, KD, 2 * D], F32R), sb("w_lo", [P, KD, 2 * D], F32R)
        raw = [sb(f"raw{i}", [KC, KCH, D]) for i in range(2)]
        xn = sb("xn", [KC, KCH, D])
        stats = sb("stats", [KC, KCH, 6])
        moments = sb("moments", [KC, KCH, 2])
        rstd = sb("rstd", [KC, KCH])
        power, eps_tile = sb("power", [KC, KCH]), sb("eps_tile", [KC, KCH])
        spare = sb("spare", [KC, 1])
        xt_hi = [sb(f"xt_hi{i}", [P, KD, S_E], F32R) for i in range(2)]
        xt_lo = [sb(f"xt_lo{i}", [P, KD, S_E], F32R) for i in range(2)]
        k_hi = sb("k_hi", [P, KD, S], F32R)
        k_lo = sb("k_lo", [P, KD, S], F32R)
        v_sb = sb("v_sb", [KC, KCH, D])
        ps_t = ctx.enter_context(nc.psum_tensor("kv_ps_t", [P, 4, 512], FP32))
        ps_m = ctx.enter_context(nc.psum_tensor("kv_ps_m", [P, 4, 512], FP32))
        w_loaded = [sem(f"w_loaded{k}") for k in range(KD)]
        w_hi_done, w_split = sem("w_hi_done"), sem("w_split")
        raw_loaded = [sem("raw_loaded0"), sem("raw_loaded1")]
        stats_done, aggr_done, rstd_done = sem("stats_done"), sem("aggr_done"), sem("rstd_done")
        rstd_add = sem("rstd_add")
        xn_done, tr_done, xt_hi_done, xt_lo_done = sem("xn_done"), sem("tr_done"), sem("xt_hi_done"), sem("xt_lo_done")
        mm_done, k_hi_done, k_lo_done, v_done = sem("mm_done"), sem("k_hi_done"), sem("k_lo_done"), sem("v_done")
        padded = sem("padded")
        k_stored, v_stored = sem("k_stored"), sem("v_stored")
        block = ctx.enter_context(nc.Block())

        @block.sync
        def _(sp):
            def load(b, par):
                sp.dma_start(raw[par][:, :, :], ctx_view[b, :, :, :]).then_inc(raw_loaded[par], 16)

            load(0, 0)
            for k in range(KD):
                sp.dma_start(w_raw[:, k, :], w_view[:, k, :]).then_inc(w_loaded[k], 16)
            load(1, 1)

            def step(b, par, has_next, has_second):
                if has_second:
                    sp.wait_ge(xn_done, KCH * (b + 1))
                    load(b + 2, par)
                sp.wait_ge(k_lo_done, NCK * (b + 1))
                sp.dma_start(dram["kT_hi"][b, :, :].rearrange("(k p) s -> p k s", p=P), k_hi[:, :, :].bitcast(FP32)).then_inc(k_stored, 16)
                sp.dma_start(dram["kT_lo"][b, :, :].rearrange("(k p) s -> p k s", p=P), k_lo[:, :, :].bitcast(FP32)).then_inc(k_stored, 16)
                sp.wait_ge(v_done, KCH * (b + 1))
                sp.dma_start(dram["v_c"][b, :, :, :], v_sb[:, :, :]).then_inc(v_stored, 16)

            batches(sp, step)
            sp.wait_ge(k_stored, 32 * B)
            sp.wait_ge(v_stored, 16 * B)

        @block.gpsimd
        def _(pool):
            nc.gpsimd.memset(power[:, :], -0.5).then_inc(rstd_add, 1)
            nc.gpsimd.memset(eps_tile[:, :], EPS1).then_inc(rstd_add, 1)
            pool.wait_ge(rstd_add, 2)
            for t in (*xt_hi, *xt_lo):
                nc.gpsimd.memset(t[:, :, S:].bitcast(FP32), 0.0).then_inc(padded, 1)

            def step(b):
                pool.wait_ge(aggr_done, b + 1)
                after_first(pool, b, xn_done, KCH * b)
                nc.gpsimd.tensor_tensor(rstd[:, :], moments[:, :, 1], eps_tile[:, :], ALU.add).then_inc(rstd_add, 1)
                pool.wait_ge(rstd_add, b + 3)
                nc.gpsimd.tensor_tensor(rstd[:, :], rstd[:, :], power[:, :], ALU.pow).then_inc(rstd_done, 1)

            step(0)
            with pool.Fori(1, B) as b:
                step(b)

        @block.vector
        def _(dve):
            def statistics(b, par):
                dve.wait_ge(raw_loaded[par], 16 * (b // 2) + 16 if isinstance(b, int) else 8 * (b - par) + 16)
                if not isinstance(b, int) or b > 0:
                    dve.wait_ge(xn_done, KCH * b)
                for c in range(KCH):
                    nc.vector.bn_stats(stats[:, c, :], raw[par][:, c, :]).then_inc(stats_done, 1)
                dve.wait_ge(stats_done, KCH * (b + 1))
                nc.vector.memset(spare[:, :], 0.0)
                for c in range(KCH):
                    last = nc.vector.bn_aggr(moments[:, c, :], stats[:, c, :])
                last.then_inc(aggr_done, 1)

            def normalise(b, par):
                dve.wait_ge(rstd_done, b + 1)
                after_first(dve, b, tr_done, NCK * b)
                for c in range(KCH):
                    nc.vector.tensor_scalar(xn[:, c, :], raw[par][:, c, :], moments[:, c, 0:1], rstd[:, c:c + 1],
                                            ALU.subtract, ALU.mult).then_inc(xn_done, 1)

            def transposed_lo(b, par, s):
                half, f = s // KD, s % KD
                cols = slice(half * HALF, (half + 1) * HALF)
                dve.wait_ge(xt_hi_done, NCK * b + s + 1)
                nc.vector.tensor_tensor(xt_lo[par][:, f, cols], ps_t[:, s % 4, 0:HALF],
                                        xt_hi[par][:, f, cols].bitcast(FP32), ALU.subtract).then_inc(xt_lo_done, 1)

            statistics(0, 0)
            normalise(0, 0)
            for k in range(KD):
                dve.wait_ge(w_hi_done, k + 1)
                nc.vector.tensor_tensor(w_lo[:, k, :], w_raw[:, k, :], w_hi[:, k, :].bitcast(FP32),
                                        ALU.subtract).then_inc(w_split, 1)
            for s in range(NCK):
                transposed_lo(0, 0, s)

            def step(b, par, has_next, has_second):
                if has_next:
                    statistics(b + 1, 1 - par)
                for s in range(NC):
                    bank = (NC * par + s) % 4
                    if has_next and s == 1:
                        normalise(b + 1, 1 - par)
                    if s < NCK:
                        half, f = s // KD, s % KD
                        cols = slice(half * HALF, (half + 1) * HALF)
                        dve.wait_ge(k_hi_done, NCK * b + s + 1)
                        nc.vector.scalar_tensor_tensor(k_lo[:, f, cols], ps_m[:, bank, 0:HALF], vecs["b_kvc"][:, f:f + 1],
                                                       k_hi[:, f, cols].bitcast(FP32), ALU.add,
                                                       ALU.subtract).then_inc(k_lo_done, 1)
                    if has_next and s >= T0:
                        transposed_lo(b + 1, 1 - par, s - T0)

            batches(dve, step)

        @block.scalar
        def _(act):
            def transposed_hi(b, par, s):
                half, f = s // KD, s % KD
                act.wait_ge(tr_done, NCK * b + s + 1)
                if not isinstance(b, int) or b > 1:
                    act.wait_ge(mm_done, NC * (b - 1))
                nc.scalar.activation(xt_hi[par][:, f, half * HALF:(half + 1) * HALF], ps_t[:, s % 4, 0:HALF],
                                     ACT.Copy).then_inc(xt_hi_done, 1)

            for k in range(KD):
                act.wait_ge(w_loaded[k], 16)
                nc.scalar.activation(w_hi[:, k, :], w_raw[:, k, :], ACT.Copy).then_inc(w_hi_done, 1)
            for s in range(NCK):
                transposed_hi(0, 0, s)

            def step(b, par, has_next, has_second):
                for s in range(NC):
                    bank = (NC * par + s) % 4
                    act.wait_ge(mm_done, NC * b + s + 1)
                    if s < NCK:
                        half, f = s // KD, s % KD
                        if s == 0 and (not isinstance(b, int) or b > 0):
                            act.wait_ge(k_stored, 32 * b)
                        nc.scalar.activation(k_hi[:, f, half * HALF:(half + 1) * HALF], ps_m[:, bank, 0:HALF],
                                             ACT.Identity, bias=vecs["b_kvc"][:, f:f + 1]).then_inc(k_hi_done, 1)
                    else:
                        if s == NCK and (not isinstance(b, int) or b > 0):
                            act.wait_ge(v_stored, 16 * b)
                        nc.scalar.activation(v_sb[:, s - NCK, :], ps_m[:KC, bank, :], ACT.Copy).then_inc(v_done, 1)
                    if has_next and s >= T0:
                        transposed_hi(b + 1, 1 - par, s - T0)

            batches(act, step)

        @block.tensor
        def _(pe):
            def transposes(b, s):
                half, f = s // KD, s % KD
                if s % KD == 0:
                    pe.wait_ge(xn_done, KCH * b + 3 * half + 3)
                if not isinstance(b, int) or NCK * b + s >= 4:
                    pe.wait_ge(xt_lo_done, NCK * b + s - 3)
                for j in range(3):
                    last = nc.tensor.transpose(ps_t[:, s % 4, j * KC:(j + 1) * KC],
                                               xn[:, 3 * half + j, f * P:(f + 1) * P], ident[:KC, :KC])
                last.then_inc(tr_done, 1)

            for s in range(NCK):
                transposes(0, s)
            pe.wait_ge(w_split, KD)
            pe.wait_ge(padded, 4)

            def step(b, par, has_next, has_second):
                for s in range(NC):
                    bank = (NC * par + s) % 4
                    if s < NCK:
                        half, f = s // KD, s % KD
                        if s == 0:
                            pe.wait_ge(xt_lo_done, NCK * (b + 1))
                    ago = s - 4
                    if ago >= NCK:
                        pe.wait_ge(v_done, KCH * b + ago - NCK + 1)
                    elif ago >= 0:
                        pe.wait_ge(k_lo_done, NCK * b + ago + 1)
                    elif not isinstance(b, int) or b > 0:
                        pe.wait_ge(v_done, KCH * b + ago + 1)
                    for k in range(KD):
                        if s < NCK:
                            cols, out = slice(half * HALF, half * HALF + HALF_E), ps_m[:, bank, 0:HALF_E]
                            w = slice(f * P, (f + 1) * P)
                            last = three_passes(nc, out, w_hi[:, k, w], w_lo[:, k, w], xt_hi[par][:, k, cols],
                                                xt_lo[par][:, k, cols], k == 0, k == KD - 1)
                        else:
                            c = slice((s - NCK) * KC, (s - NCK + 1) * KC)
                            last = three_passes(nc, ps_m[:KC, bank, :], xt_hi[par][:, k, c], xt_lo[par][:, k, c],
                                                w_hi[:, k, D:], w_lo[:, k, D:], k == 0, k == KD - 1)
                    last.then_inc(mm_done, 1)
                    if has_next and s >= T0:
                        transposes(b + 1, s - T0)

            batches(pe, step)


def project(nc, dram, const, tag, source, eps, weights, affine, fm, rm, keep, queries=0):
    ident = const["ident"]
    x_view = dram[source].rearrange("(b j p) d -> b p j d", p=QT, j=2)
    width = weights.shape[1]
    w_view = weights.rearrange("(k p) n -> p k n", p=P)
    NF = len(fm)
    NR = 2 if rm is not None else 0
    NC = NF + NR
    NW = (queries > 0) + (width > queries)
    T0 = NC - KD
    with ExitStack() as ctx:
        sb = lambda name, shape, dt=FP32: ctx.enter_context(nc.sbuf_tensor(f"{tag}_{name}", shape, dt))
        sem = lambda name: ctx.enter_context(nc.semaphore(f"{tag}_{name}"))
        w_raw = sb("w_raw", [P, KD, width])
        w_hi, w_lo = sb("w_hi", [P, KD, width], F32R), sb("w_lo", [P, KD, width], F32R)
        raw = [sb(f"raw{i}", [QT, 2, D]) for i in range(2)]
        xn = [sb(f"xn{i}", [QT, 2, D]) for i in range(2)]
        stats, moments = sb("stats", [QT, 2, 6]), sb("moments", [QT, 2, 2])
        rstd, power, eps_tile = sb("rstd", [QT, 2]), sb("power", [QT, 2]), sb("eps_tile", [QT, 2])
        spare = sb("spare", [QT, 1])
        xt = sb("xt", [P, KD, T])
        xt_hi = [sb(f"xt_hi{i}", [P, KD, T], F32R) for i in range(2)]
        xt_lo = [sb(f"xt_lo{i}", [P, KD, T], F32R) for i in range(2)]
        f_hi, f_lo = sb("f_hi", [P, NF, T], F32R), sb("f_lo", [P, NF, T], F32R)
        r_sb = sb("r_sb", [QT, 2, D])
        ps_t = ctx.enter_context(nc.psum_tensor(tag + "_ps_t", [P, KD, 512], FP32))
        ps_m = ctx.enter_context(nc.psum_tensor(tag + "_ps_m", [P, 4, 512], FP32))
        w_loaded = [sem(f"w_loaded{k}") for k in range(KD)]
        w_hi_done, w_split = sem("w_hi_done"), sem("w_split")
        raw_loaded = [sem("raw_loaded0"), sem("raw_loaded1")]
        stats_done, aggr_done, rstd_add, rstd_done = sem("stats_done"), sem("aggr_done"), sem("rstd_add"), sem("rstd_done")
        xn_done, tr_done, xt_done, xt_hi_done, xt_lo_done = sem("xn_done"), sem("tr_done"), sem("xt_done"), sem("xt_hi_done"), sem("xt_lo_done")
        mm_done, f_hi_done, f_lo_done, r_done = sem("mm_done"), sem("f_hi_done"), sem("f_lo_done"), sem("r_done")
        kept = [sem("kept0"), sem("kept1")]
        stored = sem("stored")
        NS = 16 * (2 * NF + NR // 2)
        block = ctx.enter_context(nc.Block())

        @block.sync
        def _(sp):
            def load(b, par):
                sp.dma_start(raw[par][:, :, :], x_view[b, :, :, :]).then_inc(raw_loaded[par], 16)

            load(0, 0)
            for k in range(KD):
                sp.dma_start(w_raw[:, k, :], w_view[:, k, :]).then_inc(w_loaded[k], 16)
            load(1, 1)

            def step(b, par, has_next, has_second):
                rows = bass.ds(T * b, T)
                if has_second:
                    sp.wait_ge(xn_done, 2 * (b + 1))
                    load(b + 2, par)
                if keep is not None:
                    sp.wait_ge(xt_lo_done, KD * (b + 1))
                    for part, name in ((xt_hi, keep + "_hi"), (xt_lo, keep + "_lo")):
                        sp.dma_start(dram[name][0:KD, :, rows].rearrange("k p r -> p k r"),
                                     part[par][:, :, :].bitcast(FP32)).then_inc(kept[par], 16)
                sp.wait_ge(f_lo_done, NF * (b + 1))
                for n, (_, _, name, chunk) in enumerate(fm):
                    for part, suffix in ((f_hi, "_hi"), (f_lo, "_lo")):
                        sp.dma_start(dram[name + suffix][chunk, :, rows], part[:, n, :].bitcast(FP32)).then_inc(stored, 16)
                if NR:
                    sp.wait_ge(r_done, 2 * (b + 1))
                    sp.dma_start(dram["v_s"][rows, :].rearrange("(j p) d -> p j d", p=QT), r_sb[:, :, :]).then_inc(stored, 16)

            batches(sp, step)
            sp.wait_ge(stored, NS * B)
            if keep is not None:
                sp.wait_ge(kept[0], 16 * B)
                sp.wait_ge(kept[1], 16 * B)

        @block.gpsimd
        def _(pool):
            nc.gpsimd.memset(power[:, :], -0.5).then_inc(rstd_add, 1)
            nc.gpsimd.memset(eps_tile[:, :], eps).then_inc(rstd_add, 1)
            pool.wait_ge(rstd_add, 2)

            def step(b):
                pool.wait_ge(aggr_done, b + 1)
                after_first(pool, b, xn_done, 2 * b)
                nc.gpsimd.tensor_tensor(rstd[:, :], moments[:, :, 1], eps_tile[:, :], ALU.add).then_inc(rstd_add, 1)
                pool.wait_ge(rstd_add, b + 3)
                nc.gpsimd.tensor_tensor(rstd[:, :], rstd[:, :], power[:, :], ALU.pow).then_inc(rstd_done, 1)

            step(0)
            with pool.Fori(1, B) as b:
                step(b)

        @block.vector
        def _(dve):
            def normalise(b, par):
                dve.wait_ge(raw_loaded[par], 16 * (b // 2) + 16 if isinstance(b, int) else 8 * (b - par) + 16)
                after_first(dve, b, rstd_done, b)
                for j in range(2):
                    nc.vector.bn_stats(stats[:, j, :], raw[par][:, j, :]).then_inc(stats_done, 1)
                dve.wait_ge(stats_done, 2 * (b + 1))
                after_first(dve, b, xn_done, 2 * b)
                nc.vector.memset(spare[:, :], 0.0)
                for j in range(2):
                    last = nc.vector.bn_aggr(moments[:, j, :], stats[:, j, :])
                last.then_inc(aggr_done, 1)
                dve.wait_ge(rstd_done, b + 1)
                if not isinstance(b, int) or b > 1:
                    dve.wait_ge(tr_done, KD * (b - 1))
                for j in range(2):
                    nc.vector.tensor_scalar(xn[par][:, j, :], raw[par][:, j, :], moments[:, j, 0:1], rstd[:, j:j + 1],
                                            ALU.subtract, ALU.mult).then_inc(xn_done, 1)

            def transposed(b, par, f):
                dve.wait_ge(xt_done, KD * b + f + 1)
                if f == 0:
                    if not isinstance(b, int) or b > 1:
                        dve.wait_ge(mm_done, NC * (b - 1))
                        if keep is not None:
                            dve.wait_ge(kept[par], 16 * (b - par) if not isinstance(b, int) else 32 * (b // 2))
                nc.vector.tensor_copy(xt_hi[par][:, f, :], xt[:, f, :]).then_inc(xt_hi_done, 1)
                dve.wait_ge(xt_hi_done, KD * b + f + 1)
                nc.vector.tensor_tensor(xt_lo[par][:, f, :], xt[:, f, :], xt_hi[par][:, f, :].bitcast(FP32),
                                        ALU.subtract).then_inc(xt_lo_done, 1)

            normalise(0, 0)
            for k in range(KD):
                dve.wait_ge(w_hi_done, NW * (k + 1))
                if queries:
                    nc.vector.scalar_tensor_tensor(w_lo[:, k, 0:queries], w_raw[:, k, 0:queries], SCALE1, w_hi[:, k, 0:queries].bitcast(FP32),
                                                   ALU.mult, ALU.subtract).then_inc(w_split, 1)
                if width > queries:
                    nc.vector.tensor_tensor(w_lo[:, k, queries:], w_raw[:, k, queries:], w_hi[:, k, queries:].bitcast(FP32),
                                            ALU.subtract).then_inc(w_split, 1)
            for f in range(KD):
                transposed(0, 0, f)

            def step(b, par, has_next, has_second):
                if has_next:
                    normalise(b + 1, 1 - par)
                for s in range(NC):
                    bank = (NC * par + s) % 4
                    if s < NF:
                        dve.wait_ge(f_hi_done, NF * b + s + 1)
                        nc.vector.scalar_tensor_tensor(f_lo[:, s, :], ps_m[:, bank, 0:T], fm[s][1],
                                                       f_hi[:, s, :].bitcast(FP32), ALU.add, ALU.subtract).then_inc(f_lo_done, 1)
                    if has_next and s >= T0:
                        transposed(b + 1, 1 - par, s - T0)

            batches(dve, step)

        @block.scalar
        def _(act):
            def transposed(b, par, f):
                act.wait_ge(tr_done, KD * b + f + 1)
                after_first(act, b, xt_lo_done, KD * (b - 1) + f + 1)
                scale, shift, per_batch = affine(f)
                if per_batch:
                    scale, shift = scale[:, bass.ds(b, 1)], shift[:, bass.ds(b, 1)]
                nc.scalar.activation(xt[:, f, :], ps_t[:, f, 0:T], ACT.Identity, bias=shift, scale=scale).then_inc(xt_done, 1)

            for k in range(KD):
                act.wait_ge(w_loaded[k], 16)
                if queries:
                    nc.scalar.activation(w_hi[:, k, 0:queries], w_raw[:, k, 0:queries], ACT.Copy, scale=SCALE1).then_inc(w_hi_done, 1)
                if width > queries:
                    nc.scalar.activation(w_hi[:, k, queries:], w_raw[:, k, queries:], ACT.Copy).then_inc(w_hi_done, 1)
            for f in range(KD):
                transposed(0, 0, f)

            def step(b, par, has_next, has_second):
                for s in range(NC):
                    bank = (NC * par + s) % 4
                    act.wait_ge(mm_done, NC * b + s + 1)
                    if s == 0:
                        after_first(act, b, stored, NS * b)
                    if s < NF:
                        nc.scalar.activation(f_hi[:, s, :], ps_m[:, bank, 0:T], ACT.Identity, bias=fm[s][1]).then_inc(f_hi_done, 1)
                    else:
                        nc.scalar.activation(r_sb[:, s - NF, :], ps_m[:QT, bank, :], ACT.Copy).then_inc(r_done, 1)
                    if has_next and s >= T0:
                        transposed(b + 1, 1 - par, s - T0)

            batches(act, step)

        @block.tensor
        def _(pe):
            def transposes(b, par, f):
                if f == 0:
                    pe.wait_ge(xn_done, 2 * (b + 1))
                after_first(pe, b, xt_done, KD * (b - 1) + f + 1)
                for j in range(2):
                    last = nc.tensor.transpose(ps_t[:, f, j * QT:(j + 1) * QT], xn[par][:, j, f * P:(f + 1) * P], ident[:QT, :QT])
                last.then_inc(tr_done, 1)

            for f in range(KD):
                transposes(0, 0, f)
            pe.wait_ge(w_split, NW * KD)

            def step(b, par, has_next, has_second):
                pe.wait_ge(xt_lo_done, KD * (b + 1))
                for s in range(NC):
                    bank = (NC * par + s) % 4
                    ago = (s - 4) % NC
                    done, each = (f_lo_done, NF) if ago < NF else (r_done, NR)
                    nth = ago + 1 if ago < NF else ago - NF + 1
                    if s >= 4:
                        pe.wait_ge(done, each * b + nth)
                    else:
                        after_first(pe, b, done, each * (b - 1) + nth)
                    for k in range(KD):
                        if s < NF:
                            w = slice(fm[s][0], fm[s][0] + P)
                            last = three_passes(nc, ps_m[:, bank, 0:T], w_hi[:, k, w], w_lo[:, k, w], xt_hi[par][:, k, :],
                                                xt_lo[par][:, k, :], k == 0, k == KD - 1)
                        else:
                            r = slice((s - NF) * QT, (s - NF + 1) * QT)
                            last = three_passes(nc, ps_m[:QT, bank, :], xt_hi[par][:, k, r], xt_lo[par][:, k, r],
                                                w_hi[:, k, rm:rm + D], w_lo[:, k, rm:rm + D], k == 0, k == KD - 1)
                    last.then_inc(mm_done, 1)
                    if has_next and s >= T0:
                        transposes(b + 1, 1 - par, s - T0)

            batches(pe, step)


def project_scores0(nc, dram, const):
    gamma, beta = const["vecs"]["ln_gamma"], const["vecs"]["ln_beta"]
    project(nc, dram, const, "u", "x0", EPS0, dram["W_qk"], lambda f: (gamma[:, f:f + 1], beta[:, f:f + 1], False),
            [(n * P, 0.0, "u", n) for n in range(KD)], None, "comb")


def project_qkv(nc, dram, const):
    mod, bias = const["mod"], const["vecs"]["b_qkv"]
    project(nc, dram, const, "qkv", "x1", EPS1, dram["W_qkv"], lambda f: (mod[:, KD + f, :], mod[:, f, :], True),
            [(n * P, bias[:, n:n + 1], ("q", "k")[n // KD], n % KD) for n in range(2 * KD)], 2 * D, None, D)


def project_qc(nc, dram, const):
    bias = const["vecs"]["b_qc"]
    project(nc, dram, const, "qc", "x2", EPS1, dram["W_qc"], lambda f: (1.0, 0.0, False),
            [(n * P, bias[:, n:n + 1], "qc", n) for n in range(KD)], None, None, D)


def attention0(nc, dram, const):
    ident = const["ident"]
    ctx_view = dram["ctx"].rearrange("b (p c) d -> b p c d", c=KCH)
    w_view = dram["Wv"].rearrange("(k p) n -> p k n", p=P)
    NT = 2 * KD
    NP = KCH // 2
    NM = NP + 2 * KD
    with ExitStack() as ctx:
        sb = lambda name, shape, dt=FP32: ctx.enter_context(nc.sbuf_tensor("a0_" + name, shape, dt))
        sem = lambda name: ctx.enter_context(nc.semaphore("a0_" + name))
        w_raw = sb("w_raw", [P, KD, D])
        w_hi, w_lo = sb("w_hi", [P, KD, D], F32R), sb("w_lo", [P, KD, D], F32R)
        raw = [sb(f"raw{i}", [KC, KCH, D]) for i in range(2)]
        u_hi = [sb(f"u_hi{i}", [P, KD, T], F32R) for i in range(2)]
        u_lo = [sb(f"u_lo{i}", [P, KD, T], F32R) for i in range(2)]
        c_hi, c_lo = sb("c_hi", [KC, KCH, D], F32R), sb("c_lo", [KC, KCH, D], F32R)
        ct_hi = [sb(f"ct_hi{i}", [P, KD, S_E], F32R) for i in range(2)]
        ct_lo = [sb(f"ct_lo{i}", [P, KD, S_E], F32R) for i in range(2)]
        prob = sb("prob", [QT, 2, S])
        neg_max, total, recip = sb("neg_max", [QT, 2]), sb("total", [QT, 2]), sb("recip", [QT, 2])
        pt_hi, pt_lo = sb("pt_hi", [KC, KCH, T], F32R), sb("pt_lo", [KC, KCH, T], F32R)
        e_hi, e_lo = sb("e_hi", [P, KD, T], F32R), sb("e_lo", [P, KD, T], F32R)
        ev_hi, ev_lo = sb("ev_hi", [P, KD, T], F32R), sb("ev_lo", [P, KD, T], F32R)
        ps_s = ctx.enter_context(nc.psum_tensor("a0_ps_s", [P, 2, 2, 512], FP32))
        ps_t = ctx.enter_context(nc.psum_tensor("a0_ps_t", [P, 2, 512], FP32))
        ps_m = ctx.enter_context(nc.psum_tensor("a0_ps_m", [P, 2, 512], FP32))
        padded = sem("padded")
        w_loaded, w_hi_done, w_split = sem("w_loaded"), sem("w_hi_done"), sem("w_split")
        raw_loaded = [sem("raw_loaded0"), sem("raw_loaded1")]
        u_loaded = [sem("u_loaded0"), sem("u_loaded1")]
        tr_done, ct_hi_done, ct_lo_done = sem("tr_done"), sem("ct_hi_done"), sem("ct_lo_done")
        c_hi_done, c_lo_done = sem("c_hi_done"), sem("c_lo_done")
        s_done, max_done, exp_done = sem("s_done"), sem("max_done"), sem("exp_done")
        recip_done, p_done = sem("recip_done"), sem("p_done")
        mm_done, m_hi_done, m_lo_done, stored = sem("mm_done"), sem("m_hi_done"), sem("m_lo_done"), sem("stored")
        block = ctx.enter_context(nc.Block())

        def fill(n, part):
            if n < NP:
                return (pt_hi, pt_lo)[part][:, 2 * n:2 * n + 2, :], KC, 2 * T
            if n < NP + KD:
                return (e_hi, e_lo)[part][:, n - NP, :], P, T
            return (ev_hi, ev_lo)[part][:, n - NP - KD, :], P, T

        def times(b, par):
            return 16 * (b // 2) + 16 if isinstance(b, int) else 8 * (b - par) + 16

        @block.sync
        def _(sp):
            def load(b, par):
                rows = bass.ds(T * b, T)
                sp.dma_start(raw[par][:, :, :], ctx_view[b, :, :, :]).then_inc(raw_loaded[par], 16)
                for part, name in ((u_hi, "u_hi"), (u_lo, "u_lo")):
                    sp.dma_start(part[par][:, :, :].bitcast(FP32), dram[name][:, :, rows].rearrange("k p r -> p k r")).then_inc(u_loaded[par], 16)

            load(0, 0)
            sp.dma_start(w_raw[:, :, :], w_view).then_inc(w_loaded, 16)
            load(1, 1)

            def step(b, par, has_next, has_second):
                rows = bass.ds(T * b, T)
                if has_second:
                    sp.wait_ge(mm_done, NM * b + NP + 1)
                    load(b + 2, par)
                sp.wait_ge(m_lo_done, NM * (b + 1))
                for part, name in ((ev_hi, "comb_hi"), (ev_lo, "comb_lo")):
                    sp.dma_start(dram[name][KD:, :, rows].rearrange("k p r -> p k r"), part[:, :, :].bitcast(FP32)).then_inc(stored, 16)

            batches(sp, step)
            sp.wait_ge(stored, 32 * B)

        @block.gpsimd
        def _(pool):
            for t in (*ct_hi, *ct_lo):
                nc.gpsimd.memset(t[:, :, S:].bitcast(FP32), 0.0).then_inc(padded, 1)

            def step(b, par, has_next, has_second):
                for c in range(KCH):
                    pool.wait_ge(c_hi_done, KCH * b + c + 1)
                    nc.gpsimd.tensor_tensor(c_lo[:, c, :], raw[par][:, c, :], c_hi[:, c, :].bitcast(FP32),
                                            ALU.subtract).then_inc(c_lo_done, 1)

            batches(pool, step)

        @block.vector
        def _(dve):
            def transposed(b, par, s):
                cols = slice(s // KD * HALF, (s // KD + 1) * HALF)
                dve.wait_ge(ct_hi_done, NT * b + s + 1)
                nc.vector.tensor_tensor(ct_lo[par][:, s % KD, cols], ps_t[:, s % 2, 0:HALF],
                                        ct_hi[par][:, s % KD, cols].bitcast(FP32), ALU.subtract).then_inc(ct_lo_done, 1)

            dve.wait_ge(w_hi_done, 1)
            nc.vector.tensor_tensor(w_lo[:, :, :], w_raw[:, :, :], w_hi[:, :, :].bitcast(FP32), ALU.subtract).then_inc(w_split, 1)
            for s in range(NT):
                transposed(0, 0, s)

            def step(b, par, has_next, has_second):
                for q in range(2):
                    dve.wait_ge(s_done, 2 * b + q + 1)
                    after_first(dve, b, exp_done, 2 * b)
                    nc.vector.tensor_reduce(neg_max[:, q:q + 1], ps_s[:QT, q, :, 0:HALF], AX.XY, ALU.max, negate=True).then_inc(max_done, 1)
                if has_next:
                    for s in range(NT // 2):
                        transposed(b + 1, 1 - par, s)
                for q in range(2):
                    dve.wait_ge(exp_done, 2 * b + q + 1)
                    after_first(dve, b, p_done, 2 * b)
                    nc.vector.reciprocal(recip[:, q:q + 1], total[:, q:q + 1]).then_inc(recip_done, 1)
                    dve.wait_ge(recip_done, 2 * b + q + 1)
                    nc.vector.tensor_scalar(prob[:, q, :], prob[:, q, :], recip[:, q:q + 1], None, ALU.mult).then_inc(p_done, 1)
                if has_next:
                    for s in range(NT // 2, NT):
                        transposed(b + 1, 1 - par, s)
                for n in range(NM):
                    hi, rows, cols = fill(n, 0)
                    lo, _, _ = fill(n, 1)
                    dve.wait_ge(m_hi_done, NM * b + n + 1)
                    src = ps_m[:rows, (NM * par + n) % 2, 0:cols]
                    if n < NP:
                        src = src.rearrange("p (c r) -> p c r", c=2)
                    nc.vector.tensor_tensor(lo, src, hi.bitcast(FP32), ALU.subtract).then_inc(m_lo_done, 1)

            batches(dve, step)

        @block.scalar
        def _(act):
            def transposed(b, par, s):
                act.wait_ge(tr_done, NT * b + s + 1)
                nc.scalar.activation(ct_hi[par][:, s % KD, s // KD * HALF:(s // KD + 1) * HALF], ps_t[:, s % 2, 0:HALF],
                                     ACT.Copy).then_inc(ct_hi_done, 1)

            def split_context(b, par):
                act.wait_ge(raw_loaded[par], times(b, par))
                after_first(act, b, mm_done, NM * b)
                after_first(act, b, c_lo_done, KCH * b)
                for c in range(KCH):
                    nc.scalar.activation(c_hi[:, c, :], raw[par][:, c, :], ACT.Copy).then_inc(c_hi_done, 1)

            act.wait_ge(w_loaded, 16)
            nc.scalar.activation(w_hi[:, :, :], w_raw[:, :, :], ACT.Copy).then_inc(w_hi_done, 1)
            for s in range(NT):
                transposed(0, 0, s)
            split_context(0, 0)

            def step(b, par, has_next, has_second):
                for q in range(2):
                    act.wait_ge(max_done, 2 * b + q + 1)
                    if q == 0:
                        after_first(act, b, mm_done, NM * (b - 1) + NP)
                        after_first(act, b, recip_done, 2 * b)
                        after_first(act, b, p_done, 2 * b)
                    nc.scalar.activation(prob[:, q, :].rearrange("p (h s) -> p h s", h=2), ps_s[:QT, q, :, 0:HALF], ACT.Exp,
                                         bias=neg_max[:, q:q + 1], accum_out=total[:, q:q + 1]).then_inc(exp_done, 1)
                    if has_next:
                        for s in range(q * NT // 2, (q + 1) * NT // 2):
                            transposed(b + 1, 1 - par, s)
                for n in range(NM):
                    hi, rows, cols = fill(n, 0)
                    act.wait_ge(mm_done, NM * b + n + 1)
                    if n == NP + KD:
                        after_first(act, b, stored, 32 * b)
                    src = ps_m[:rows, (NM * par + n) % 2, 0:cols]
                    if n < NP:
                        src = src.rearrange("p (c r) -> p c r", c=2)
                    nc.scalar.activation(hi, src, ACT.Copy).then_inc(m_hi_done, 1)
                if has_next:
                    split_context(b + 1, 1 - par)

            batches(act, step)

        @block.tensor
        def _(pe):
            def transposes(b, par, s):
                if s == 0:
                    pe.wait_ge(raw_loaded[par], times(b, par))
                if not isinstance(b, int) or NT * b + s >= 2:
                    pe.wait_ge(ct_lo_done, NT * b + s - 1)
                half, f = s // KD, s % KD
                for j in range(3):
                    last = nc.tensor.transpose(ps_t[:, s % 2, j * KC:(j + 1) * KC],
                                               raw[par][:, 3 * half + j, f * P:(f + 1) * P], ident[:KC, :KC])
                last.then_inc(tr_done, 1)

            for s in range(NT):
                transposes(0, 0, s)
            pe.wait_ge(padded, 4)

            def step(b, par, has_next, has_second):
                pe.wait_ge(u_loaded[par], 2 * times(b, par))
                for q in range(2):
                    after_first(pe, b, exp_done, 2 * (b - 1) + q + 1)
                    for half in range(2):
                        if q == half == 0:
                            pe.wait_ge(ct_lo_done, NT * (b + 1))
                        rows, cols = slice(q * QT, (q + 1) * QT), slice(half * HALF, half * HALF + HALF_E)
                        for k in range(KD):
                            last = three_passes(nc, ps_s[:QT, q, half, 0:HALF_E], u_hi[par][:, k, rows], u_lo[par][:, k, rows],
                                                ct_hi[par][:, k, cols], ct_lo[par][:, k, cols], k == 0, k == KD - 1)
                    last.then_inc(s_done, 1)
                if has_next:
                    for s in range(NT):
                        transposes(b + 1, 1 - par, s)
                for n in range(NM):
                    bank = (NM * par + n) % 2
                    if not isinstance(b, int) or NM * b + n >= 2:
                        pe.wait_ge(m_lo_done, NM * b + n - 1)
                    if n < NP:
                        if n == 0:
                            pe.wait_ge(p_done, 2 * (b + 1))
                        for c in range(2):
                            for q in range(2):
                                cols = slice((2 * n + c) * KC, (2 * n + c + 1) * KC)
                                last = nc.tensor.transpose(ps_m[:KC, bank, c * T + q * QT:c * T + (q + 1) * QT],
                                                           prob[:, q, cols], ident[:QT, :QT])
                    elif n < NP + KD:
                        if n == NP:
                            pe.wait_ge(m_lo_done, NM * b + NP)
                            pe.wait_ge(c_lo_done, KCH * (b + 1))
                        f = slice((n - NP) * P, (n - NP + 1) * P)
                        for c in range(KCH):
                            last = three_passes(nc, ps_m[:, bank, 0:T], c_hi[:, c, f], c_lo[:, c, f], pt_hi[:, c, :],
                                                pt_lo[:, c, :], c == 0, c == KCH - 1)
                    else:
                        if n == NP + KD:
                            pe.wait_ge(w_split, 1)
                            pe.wait_ge(m_lo_done, NM * b + NP + KD)
                        f = slice((n - NP - KD) * P, (n - NP - KD + 1) * P)
                        for k in range(KD):
                            last = three_passes(nc, ps_m[:, bank, 0:T], w_hi[:, k, f], w_lo[:, k, f], e_hi[:, k, :],
                                                e_lo[:, k, :], k == 0, k == KD - 1)
                    last.then_inc(mm_done, 1)

            batches(pe, step)


RT = R // P


class HiddenUnits:

    def __init__(self, nc, ctx, tag, ki):
        sb = lambda name, shape, dt=FP32: ctx.enter_context(nc.sbuf_tensor(f"{tag}_{name}", shape, dt))
        sem = lambda name: ctx.enter_context(nc.semaphore(f"{tag}_{name}"))
        self.nc, self.ki, self.width = nc, ki, ki * P + D
        self.x_hi, self.x_lo = sb("x_hi", [P, ki, R], F32R), sb("x_lo", [P, ki, R], F32R)
        self.acc = sb("acc", [P, RT, D])
        self.w_raw = sb("w_raw", [P, self.width])
        self.w_hi = [sb(f"w_hi{i}", [P, self.width], F32R) for i in range(2)]
        self.w_lo = [sb(f"w_lo{i}", [P, self.width], F32R) for i in range(2)]
        self.h = [sb(f"h{i}", [P, GROUP]) for i in range(2)]
        self.h_hi = [sb(f"h_hi{i}", [P, R // 2], F32R) for i in range(2)]
        self.h_lo = [sb(f"h_lo{i}", [P, R // 2], F32R) for i in range(2)]
        self.ps_h = ctx.enter_context(nc.psum_tensor(tag + "_ps_h", [P, NG, 512], FP32))
        self.ps_y = ctx.enter_context(nc.psum_tensor(tag + "_ps_y", [P, 4, 512], FP32))
        self.w_loaded = [sem("w1_loaded"), sem("w2_loaded")]
        self.w_hi_done, self.w_lo_done = sem("w_hi_done"), sem("w_lo_done")
        self.h_mm, self.h_done, self.h_hi_done, self.h_lo_done = sem("h_mm"), sem("h_done"), sem("h_hi_done"), sem("h_lo_done")
        self.y_mm, self.y_done, self.acc_ready = sem("y_mm"), sem("y_done"), sem("acc_ready")

    def load(self, sp, n, w1, w2):
        after_first(sp, n, self.w_lo_done, n)
        sp.dma_start(self.w_raw[:, 0:self.ki * P].rearrange("p (k n) -> p k n", n=P),
                     w1.rearrange("(k p) n -> p k n", p=P)).then_inc(self.w_loaded[0], 16)
        sp.dma_start(self.w_raw[:, self.ki * P:], w2).then_inc(self.w_loaded[1], 16)

    def split_hi(self, act, n, slot):
        for s in self.w_loaded:
            act.wait_ge(s, 16 * (n + 1))
        if not isinstance(n, int) or n > 1:
            act.wait_ge(self.y_mm, RT * (n - 1))
        self.nc.scalar.activation(self.w_hi[slot][:, :], self.w_raw[:, :], ACT.Copy).then_inc(self.w_hi_done, 1)

    def split_lo(self, pool, n, slot):
        pool.wait_ge(self.w_hi_done, n + 1)
        self.nc.gpsimd.tensor_tensor(self.w_lo[slot][:, :], self.w_raw[:, :], self.w_hi[slot][:, :].bitcast(FP32),
                                     ALU.subtract).then_inc(self.w_lo_done, 1)

    def activate(self, act, n, func, bias, group):
        nc = self.nc
        act.wait_ge(self.h_mm, NG * n + group + 1)
        if not isinstance(n, int) or NG * n + group >= 2:
            act.wait_ge(self.h_lo_done, NG * n + group - 1)
        for j in range(2):
            cols = slice(j * T, (j + 1) * T)
            last = nc.scalar.activation(self.h[group % 2][:, cols], self.ps_h[:, group, cols], func, bias=bias(2 * group + j))
        last.then_inc(self.h_done, 1)

    def split_h(self, dve, n, group):
        nc, half = self.nc, group // 2
        cols = slice(group % 2 * GROUP, (group % 2 + 1) * GROUP)
        dve.wait_ge(self.h_done, NG * n + group + 1)
        after_first(dve, n, self.y_mm, RT * (n - 1) + RT // 2 * (half + 1))
        nc.vector.tensor_copy(self.h_hi[half][:, cols], self.h[group % 2][:, :]).then_inc(self.h_hi_done, 1)
        dve.wait_ge(self.h_hi_done, NG * n + group + 1)
        nc.vector.tensor_tensor(self.h_lo[half][:, cols], self.h[group % 2][:, :], self.h_hi[half][:, cols].bitcast(FP32),
                                ALU.subtract).then_inc(self.h_lo_done, 1)

    def accumulate(self, dve, n, tile, weight, par):
        nc = self.nc
        dve.wait_ge(self.y_mm, RT * n + tile + 1)
        after_first(dve, n, self.y_done, RT * (n - 1) + tile + 1)
        nc.vector.scalar_tensor_tensor(self.acc[:, tile, :], self.ps_y[:, (RT * par + tile) % 4, :], weight,
                                       self.acc[:, tile, :], ALU.mult, ALU.add).then_inc(self.y_done, 1)

    def multiply(self, pe, n, slot, par, x_ready=None):
        nc, ki = self.nc, self.ki
        w_hi, w_lo = self.w_hi[slot], self.w_lo[slot]
        pe.wait_ge(self.w_lo_done, n + 1)
        for g in range(NG):
            if x_ready is not None:
                x_ready(g)
            after_first(pe, n, self.h_done, NG * (n - 1) + g + 1)
            cols = slice(g * GROUP, (g + 1) * GROUP)
            for k in range(ki):
                w = slice(k * P, (k + 1) * P)
                last = three_passes(nc, self.ps_h[:, g, 0:GROUP], w_hi[:, w], w_lo[:, w], self.x_hi[:, k, cols],
                                    self.x_lo[:, k, cols], k == 0, k == ki - 1)
            last.then_inc(self.h_mm, 1)
        for i in range(RT):
            half, j = i // (RT // 2), i % (RT // 2)
            if j == 0:
                pe.wait_ge(self.h_lo_done, NG * n + 2 * (half + 1))
            if not isinstance(n, int) or RT * n + i >= 4:
                pe.wait_ge(self.y_done, RT * n + i - 3)
            r = slice(j * P, (j + 1) * P)
            three_passes(nc, self.ps_y[:, (RT * par + i) % 4, :], self.h_hi[half][:, r], self.h_lo[half][:, r],
                         w_hi[:, ki * P:], w_lo[:, ki * P:], True, True).then_inc(self.y_mm, 1)


def mixture(nc, dram, const):
    ident, anchor = const["ident"], const["anchor"]
    KI = 2 * KD
    EU, GU = E * HCH, D // P
    with ExitStack() as ctx:
        sb = lambda name, shape, dt=FP32: ctx.enter_context(nc.sbuf_tensor("mx_" + name, shape, dt))
        sem = lambda name: ctx.enter_context(nc.semaphore("mx_" + name))
        u = HiddenUnits(nc, ctx, "mx", KI)
        b2 = sb("b2", [P, E + 1, D])
        logits = u.acc[0:E, :, :].rearrange("e i d -> e (i d)")[:, 0:R]
        prob = sb("prob", [P, RT, E])
        top, total, recip = sb("top", [P, RT]), sb("total", [P, RT]), sb("recip", [P, RT])
        x_loaded = [sem(f"x_loaded{g}") for g in range(NG)]
        r_zeroed, r_loaded, b2_loaded = sem("r_zeroed"), sem("r_loaded"), sem("b2_loaded")
        r_hi_done, r_lo_done = sem("r_hi_done"), sem("r_lo_done")
        l_mm, l_done, l_tr, soft, soft_exp = sem("l_mm"), sem("l_done"), sem("l_tr"), sem("soft"), sem("soft_exp")
        routed_stored, stored = [sem("routed_stored0"), sem("routed_stored1")], sem("stored")
        block = ctx.enter_context(nc.Block())
        r_raw = u.w_raw[:, 0:KI * P].rearrange("p (k n) -> p k n", n=P)
        r_hi, r_lo = u.w_hi[1][:, 0:KI * P], u.w_lo[1][:, 0:KI * P]
        H = RT // 2

        def expert_units(eng, unit):
            unit(0, 0, 0, 0)
            unit(0, 1, 1, 1)
            with eng.Fori(1, HCH // 2) as i:
                for slot in range(2):
                    unit(0, 2 * i + slot, 2 * i + slot, slot)
            with eng.Fori(1, E) as e:
                with eng.Fori(0, HCH // 2) as i:
                    for slot in range(2):
                        unit(e, 2 * i + slot, e * HCH + 2 * i + slot, slot)

        def gate_units(eng, unit, first=0):
            for k in range(first, 2):
                unit(k, EU + k, k)
            with eng.Fori(1, GU // 2) as i:
                for slot in range(2):
                    unit(2 * i + slot, 2 * i + slot + EU, slot)

        def chunk(k):
            return bass.ds(k * P, P)

        @block.sync
        def _(sp):
            sp.wait_ge(r_zeroed, 1)
            sp.dma_start(r_raw[:, :, 0:E], dram["router_W"][0:2 * D, :].rearrange("(k p) n -> p k n", p=P)).then_inc(r_loaded, 16)
            for g in range(NG):
                rows = slice(g * GROUP, (g + 1) * GROUP)
                for part, name in ((u.x_hi, "comb_hi"), (u.x_lo, "comb_lo")):
                    sp.dma_start(part[:, :, rows].bitcast(FP32), dram[name][:, :, rows].rearrange("k p r -> p k r")).then_inc(x_loaded[g], 16)
                if g == 0:
                    sp.wait_ge(r_lo_done, 1)
                    u.load(sp, 0, dram["e_w1"][0, 0:2 * D, 0:P], dram["e_w2"][0, 0:P, :])
            for e in range(E):
                sp.dma_start(b2[:, e, :], dram["e_b2"][e].partition_broadcast(P)).then_inc(b2_loaded, 16)
            sp.dma_start(b2[:, E, :], dram["gate_b2"].partition_broadcast(P)).then_inc(b2_loaded, 16)
            expert_units(sp, lambda e, k, n, slot: None if isinstance(n, int) and n == 0 else
                         u.load(sp, n, dram["e_w1"][e, 0:2 * D, chunk(k)], dram["e_w2"][e, chunk(k), :]))
            gate = lambda k, n, slot: u.load(sp, n, dram["gate_w1"][0:2 * D, chunk(k)], dram["gate_w2"][chunk(k), :])
            gate(0, EU, 0)
            for h in range(2):
                tiles = slice(h * H, (h + 1) * H)
                sp.wait_ge(u.y_done, RT * (EU - 1) + H * (h + 1))
                sp.dma_start(dram["routed"].rearrange("(i p) d -> p i d", p=P)[:, tiles, :], u.acc[:, tiles, :]).then_inc(routed_stored[h], 16)
            gate_units(sp, gate, first=1)
            for h in range(2):
                tiles = slice(h * H, (h + 1) * H)
                sp.wait_ge(u.y_done, RT * (EU + GU - 1) + H * (h + 1))
                sp.dma_start(dram["gate"].rearrange("(i p) d -> p i d", p=P)[:, tiles, :], u.acc[:, tiles, :]).then_inc(stored, 16)
            sp.wait_ge(stored, 32)

        @block.gpsimd
        def _(pool):
            nc.gpsimd.memset(r_raw, 0.0).then_inc(r_zeroed, 1)
            pool.wait_ge(r_hi_done, 1)
            nc.gpsimd.tensor_tensor(r_lo, u.w_raw[:, 0:KI * P], r_hi.bitcast(FP32), ALU.subtract).then_inc(r_lo_done, 1)
            expert_units(pool, lambda e, k, n, slot: u.split_lo(pool, n, slot))
            gate_units(pool, lambda k, n, slot: u.split_lo(pool, n, slot))

        @block.scalar
        def _(act):
            act.wait_ge(r_loaded, 16)
            nc.scalar.activation(r_hi, u.w_raw[:, 0:KI * P], ACT.Copy).then_inc(r_hi_done, 1)
            for g in range(NG):
                act.wait_ge(l_mm, g + 1)
                for j in range(2):
                    last = nc.scalar.activation(logits[:, g * GROUP + j * T:g * GROUP + (j + 1) * T], u.ps_h[:E, g, j * T:(j + 1) * T], ACT.Identity,
                                                bias=const["router_anchor"][:, 2 * g + j:2 * g + j + 1])
                last.then_inc(l_done, 1)
                if g == 0:
                    u.split_hi(act, 0, 0)
            act.wait_ge(soft, 2)
            nc.scalar.activation(prob[:, :, :], prob[:, :, :], ACT.Exp).then_inc(soft_exp, 1)

            def expert(e, k, n, slot):
                if not isinstance(n, int) or n > 0:
                    u.split_hi(act, n, slot)
                for g in range(NG):
                    u.activate(act, n, ACT.Silu, lambda b: anchor[:, bass.ds(e * HCH + k, 1), b], g)

            def gate(k, n, slot):
                u.split_hi(act, n, slot)
                for g in range(NG):
                    u.activate(act, n, ACT.Silu, lambda b: anchor[:, bass.ds(k + EU, 1), b], g)

            expert_units(act, expert)
            gate_units(act, gate)

        @block.vector
        def _(dve):
            dve.wait_ge(l_tr, 1)
            raw = u.ps_y[:, 0, 0:4 * RT].rearrange("p (i e) -> p i e", e=4)[:, :, 0:E]
            wide = lambda v: v.unsqueeze(2).to_broadcast([P, RT, E])
            nc.vector.tensor_reduce(top[:, :], raw, AX.X, ALU.max).then_inc(soft, 1)
            dve.wait_ge(soft, 1)
            nc.vector.tensor_tensor(prob[:, :, :], raw, wide(top[:, :]), ALU.subtract).then_inc(soft, 1)
            dve.wait_ge(soft_exp, 1)
            nc.vector.tensor_reduce(total[:, :], prob[:, :, :], AX.X, ALU.add).then_inc(soft, 1)
            dve.wait_ge(soft, 3)
            nc.vector.reciprocal(recip[:, :], total[:, :]).then_inc(soft, 1)
            dve.wait_ge(soft, 4)
            nc.vector.tensor_tensor(prob[:, :, :], prob[:, :, :], wide(recip[:, :]), ALU.mult).then_inc(soft, 1)
            dve.wait_ge(soft, 5)
            dve.wait_ge(b2_loaded, 16 * (E + 1))
            for g in range(NG):
                u.split_h(dve, 0, g)
            for e in range(E):
                for i in range(RT):
                    if e == 0:
                        nc.vector.tensor_scalar(u.acc[:, i, :], b2[:, e, :], prob[:, i, e:e + 1], None, ALU.mult).then_inc(u.acc_ready, 1)
                    else:
                        dve.wait_ge(u.acc_ready, RT * (e - 1) + i + 1)
                        nc.vector.scalar_tensor_tensor(u.acc[:, i, :], b2[:, e, :], prob[:, i, e:e + 1], u.acc[:, i, :],
                                                       ALU.mult, ALU.add).then_inc(u.acc_ready, 1)
            dve.wait_ge(u.acc_ready, E * RT)

            def expert(e, k, n, slot):
                for g in range(NG):
                    if not isinstance(n, int) or n > 0:
                        u.split_h(dve, n, g)
                for i in range(RT):
                    w = prob[:, i, e:e + 1] if isinstance(e, int) else prob[:, i, bass.ds(e, 1)]
                    u.accumulate(dve, n, i, w, slot)

            def gate(k, n, slot):
                for g in range(NG):
                    u.split_h(dve, n, g)
                for i in range(RT):
                    u.accumulate(dve, n, i, 1.0, slot)

            expert_units(dve, expert)
            for i in range(RT):
                dve.wait_ge(routed_stored[i // H], 16)
                nc.vector.tensor_copy(u.acc[:, i, :], b2[:, E, :]).then_inc(u.acc_ready, 1)
            dve.wait_ge(u.acc_ready, (E + 1) * RT)
            gate_units(dve, gate)

        @block.tensor
        def _(pe):
            pe.wait_ge(r_lo_done, 1)
            for g in range(NG):
                pe.wait_ge(x_loaded[g], 32)
                cols = slice(g * GROUP, (g + 1) * GROUP)
                for k in range(KI):
                    w = slice(k * P, (k + 1) * P)
                    last = three_passes(nc, u.ps_h[:, g, 0:GROUP], r_hi[:, w], r_lo[:, w], u.x_hi[:, k, cols],
                                        u.x_lo[:, k, cols], k == 0, k == KI - 1)
                last.then_inc(l_mm, 1)
            pe.wait_ge(l_done, NG)
            for i in range(RT):
                last = nc.tensor.transpose(u.ps_y[:, 0, 4 * i:4 * i + E], logits[:, i * P:(i + 1) * P], ident[:E, :E])
            last.then_inc(l_tr, 1)
            pe.wait_ge(soft, 2)
            expert_units(pe, lambda e, k, n, slot: u.multiply(pe, n, slot, slot))
            gate_units(pe, lambda k, n, slot: u.multiply(pe, n, slot, slot))


def residual(nc, dram, const):
    ident = const["ident"]
    rows_of = lambda name: dram[name].rearrange("(b j p) d -> b p j d", p=QT, j=2)
    with ExitStack() as ctx:
        sb = lambda name, shape, dt=FP32: ctx.enter_context(nc.sbuf_tensor("rs_" + name, shape, dt))
        sem = lambda name: ctx.enter_context(nc.semaphore("rs_" + name))
        w_raw = sb("w_raw", [P, KD, D])
        w_hi, w_lo = sb("w_hi", [P, KD, D], F32R), sb("w_lo", [P, KD, D], F32R)
        bias = sb("bias", [QT, D])
        routed = [sb(f"routed{i}", [QT, 2, D]) for i in range(2)]
        gate = [sb(f"gate{i}", [QT, 2, D]) for i in range(2)]
        x = [sb(f"x{i}", [QT, 2, D]) for i in range(2)]
        r_hi = [sb(f"r_hi{i}", [P, KD, T], F32R) for i in range(2)]
        r_lo = [sb(f"r_lo{i}", [P, KD, T], F32R) for i in range(2)]
        y = [sb(f"y{i}", [QT, 2, D]) for i in range(2)]
        ps_t = ctx.enter_context(nc.psum_tensor("rs_ps_t", [P, KD, 512], FP32))
        ps_m = ctx.enter_context(nc.psum_tensor("rs_ps_m", [P, 4, 512], FP32))
        w_loaded, bias_loaded, w_hi_done, w_split = sem("w_loaded"), sem("bias_loaded"), sem("w_hi_done"), sem("w_split")
        routed_loaded = [sem("routed_loaded0"), sem("routed_loaded1")]
        side_loaded = [sem("side_loaded0"), sem("side_loaded1")]
        tr_done, r_hi_done, r_lo_done, mm_done = sem("tr_done"), sem("r_hi_done"), sem("r_lo_done"), sem("mm_done")
        gate_done, y_done, gated, y_added, stored = sem("gate_done"), sem("y_done"), sem("gated"), sem("y_added"), [sem("stored0"), sem("stored1")]
        block = ctx.enter_context(nc.Block())

        def nth(b, par, n=16):
            return n * (b // 2 + 1) if isinstance(b, int) else n // 2 * (b - par) + n

        @block.sync
        def _(sp):
            def load(b, par):
                sp.dma_start(routed[par][:, :, :], rows_of("routed")[b, :, :, :]).then_inc(routed_loaded[par], 16)
                sp.dma_start(gate[par][:, :, :], rows_of("gate")[b, :, :, :]).then_inc(side_loaded[par], 16)
                sp.dma_start(x[par][:, :, :], rows_of("x0")[b, :, :, :]).then_inc(side_loaded[par], 16)

            sp.dma_start(w_raw[:, :, :], dram["out_w"].rearrange("(k p) n -> p k n", p=P)).then_inc(w_loaded, 16)
            load(0, 0)
            sp.dma_start(bias[:, :], dram["out_b"].partition_broadcast(QT)).then_inc(bias_loaded, 16)
            load(1, 1)

            def step(b, par, has_next, has_second):
                sp.wait_ge(y_added, b + 1)
                sp.dma_start(rows_of("x1")[b, :, :, :], y[par][:, :, :]).then_inc(stored[par], 16)
                if has_second:
                    load(b + 2, par)

            batches(sp, step)
            for s in stored:
                sp.wait_ge(s, 16 * B // 2)

        @block.scalar
        def _(act):
            act.wait_ge(w_loaded, 16)
            nc.scalar.activation(w_hi[:, :, :], w_raw[:, :, :], ACT.Copy).then_inc(w_hi_done, 1)

            def step(b, par, has_next, has_second):
                for f in range(KD):
                    act.wait_ge(tr_done, KD * b + f + 1)
                    if f == 0 and (not isinstance(b, int) or b > 1):
                        act.wait_ge(mm_done, 2 * (b - 1))
                    nc.scalar.activation(r_hi[par][:, f, :], ps_t[:, f, 0:T], ACT.Copy).then_inc(r_hi_done, 1)
                act.wait_ge(side_loaded[par], nth(b, par, 32))
                nc.scalar.activation(gate[par][:, :, :], gate[par][:, :, :], ACT.Sigmoid).then_inc(gate_done, 1)

            batches(act, step)

        @block.vector
        def _(dve):
            dve.wait_ge(w_hi_done, 1)
            nc.vector.tensor_tensor(w_lo[:, :, :], w_raw[:, :, :], w_hi[:, :, :].bitcast(FP32), ALU.subtract).then_inc(w_split, 1)
            dve.wait_ge(bias_loaded, 16)

            def step(b, par, has_next, has_second):
                for f in range(KD):
                    dve.wait_ge(r_hi_done, KD * b + f + 1)
                    nc.vector.tensor_tensor(r_lo[par][:, f, :], ps_t[:, f, 0:T], r_hi[par][:, f, :].bitcast(FP32),
                                            ALU.subtract).then_inc(r_lo_done, 1)
                if not isinstance(b, int) or b > 1:
                    dve.wait_ge(stored[par], nth(b, par) - 16)
                for q in range(2):
                    dve.wait_ge(mm_done, 2 * b + q + 1)
                    nc.vector.tensor_tensor(y[par][:, q, :], ps_m[:QT, 2 * par + q, :], bias[:, :], ALU.add).then_inc(y_done, 1)
                dve.wait_ge(y_done, 2 * (b + 1))
                dve.wait_ge(gate_done, b + 1)
                nc.vector.tensor_tensor(y[par][:, :, :], y[par][:, :, :], gate[par][:, :, :], ALU.mult).then_inc(gated, 1)

            batches(dve, step)

        @block.gpsimd
        def _(pool):
            def step(b, par, has_next, has_second):
                pool.wait_ge(gated, b + 1)
                pool.wait_ge(side_loaded[par], nth(b, par, 32))
                nc.gpsimd.tensor_tensor(y[par][:, :, :], y[par][:, :, :], x[par][:, :, :], ALU.add).then_inc(y_added, 1)

            batches(pool, step)

        @block.tensor
        def _(pe):
            def transposes(b, par):
                pe.wait_ge(routed_loaded[par], nth(b, par))
                for f in range(KD):
                    after_first(pe, b, r_lo_done, KD * (b - 1) + f + 1)
                    for j in range(2):
                        last = nc.tensor.transpose(ps_t[:, f, j * QT:(j + 1) * QT], routed[par][:, j, f * P:(f + 1) * P], ident[:QT, :QT])
                    last.then_inc(tr_done, 1)

            transposes(0, 0)
            pe.wait_ge(w_split, 1)

            def step(b, par, has_next, has_second):
                if has_next:
                    transposes(b + 1, 1 - par)
                pe.wait_ge(r_lo_done, KD * (b + 1))
                if not isinstance(b, int) or b > 1:
                    pe.wait_ge(y_done, 2 * (b - 1))
                for q in range(2):
                    for k in range(KD):
                        r = slice(q * QT, (q + 1) * QT)
                        last = three_passes(nc, ps_m[:QT, 2 * par + q, :], r_hi[par][:, k, r], r_lo[par][:, k, r],
                                            w_hi[:, k, :], w_lo[:, k, :], k == 0, k == KD - 1)
                    last.then_inc(mm_done, 1)

            batches(pe, step)


def attention1(nc, dram, const, tag, chunks, kc, halves, q_name, k_parts, v_of, v_bias, w_name, b_name, gate, source, target, lag):
    ident = const["ident"]
    keys = chunks * kc
    HN = keys // halves
    HN_E = HN + HN % 2
    NS = 4 // halves
    NPB = 2 * NS
    NP = chunks // 2
    HPB = P // HD
    GPB = NH // HPB
    TAIL = lag + 5
    rows_of = lambda name: dram[name].rearrange("(b j p) d -> b p j d", p=QT, j=2)
    with ExitStack() as ctx:
        sb = lambda name, shape, dt=FP32: ctx.enter_context(nc.sbuf_tensor(f"{tag}_{name}", shape, dt))
        sem = lambda name: ctx.enter_context(nc.semaphore(f"{tag}_{name}"))
        w_raw = sb("w_raw", [P, KD, D])
        w_hi, w_lo = sb("w_hi", [P, KD, D], F32R), sb("w_lo", [P, KD, D], F32R)
        b_out = sb("b_out", [QT, D])
        pick = sb("pick", [HPB, P])
        q4 = [sb(f"q4_{i}", [P, HPB, T], F32R) for i in range(2)]
        k4 = [sb(f"k4_{i}", [P, HPB, keys + 2], F32R) for i in range(2)]
        v = [sb(f"v{i}", [kc, chunks, D]) for i in range(2)]
        x = [sb(f"x{i}", [QT, 2, D]) for i in range(2)]
        factor = [sb(f"factor{i}", [QT, D]) for i in range(2)]
        neg_max = sb("neg_max", [QT, NPB])
        total, recip = sb("total", [QT, 2, 2, HPB]), sb("recip", [QT, 2, HPB])
        prob = sb("prob", [QT, NPB, keys])
        pt = [sb(f"pt{i}", [kc, HPB, chunks, T]) for i in range(2)]
        recip_t, recip_wide = sb("recip_t", [HPB, T]), sb("recip_wide", [P, T])
        a = sb("a", [P, T])
        a_hi, a_lo = sb("a_hi", [P, GPB, T], F32R), sb("a_lo", [P, GPB, T], F32R)
        y = sb("y", [QT, 2, D])
        ps_s = ctx.enter_context(nc.psum_tensor(tag + "_ps_s", [P, NS, halves, 512], FP32))
        ps_t = ctx.enter_context(nc.psum_tensor(tag + "_ps_t", [P, 2, 512], FP32))
        ps_o = ctx.enter_context(nc.psum_tensor(tag + "_ps_o", [P, 2, 512], FP32))
        w_loaded, w_hi_done, w_split, side_loaded = sem("w_loaded"), sem("w_hi_done"), sem("w_split"), [sem("side_loaded0"), sem("side_loaded1")]
        padded = sem("padded")
        bias_loaded, pick_done = sem("bias_loaded"), sem("pick_done")
        qk_loaded = [sem("qk_loaded0"), sem("qk_loaded1")]
        v_loaded = [sem("v_loaded0"), sem("v_loaded1")]
        s_done, max_done, exp_done, tr_done = sem("s_done"), sem("max_done"), sem("exp_done"), sem("tr_done")
        pt_done = [sem("pt_done_dve"), sem("pt_done_act")]
        recip_done, rt_done, rt_copied, wide_done, wide_copied = sem("recip_done"), sem("rt_done"), sem("rt_copied"), sem("wide_done"), sem("wide_copied")
        pv_done, a_done, a_hi_done, a_lo_done = sem("pv_done"), sem("a_done"), sem("a_hi_done"), sem("a_lo_done")
        y_mm, y_done, y_gated, y_added, stored = sem("y_mm"), sem("y_done"), sem("y_gated"), sem("y_added"), sem("stored")
        block = ctx.enter_context(nc.Block())

        def slots(eng, slot):
            for b in range(2):
                for h in range(NH):
                    slot(b, b, h)
            with eng.Fori(1, B // 2) as i:
                for par in range(2):
                    for h in range(NH):
                        slot(2 * i + par, par, h)
            for h in range(NH, NH + TAIL):
                slot(B - 1, 1, h)

        def exists(b, h):
            return not isinstance(b, int) or 0 <= NH * b + h < NH * B

        def group_ends(b, h):
            return h % HPB == HPB - 1 and exists(b, h)

        def wait(eng, s, b, per_batch, more):
            if not isinstance(b, int) or per_batch * b + more > 0:
                eng.wait_ge(s, per_batch * b + more)

        def every_second(b, par, n):
            return n * (b // 2 + 1) if isinstance(b, int) else n // 2 * (b - par) + n

        @block.sync
        def _(sp):
            def step(b, par):
                if not isinstance(b, int) or b > 1:
                    sp.wait_ge(pv_done, GPB * (b - 1))
                    sp.wait_ge(y_added, b - 1)
                sp.dma_start(v[par][:, :, :], v_of(b)).then_inc(v_loaded[par], 16)
                rows, keys_of = bass.ds(T * b, T), [k_parts(part, b) for part in range(2)]
                for g in range(GPB):
                    wait(sp, s_done, b, 2 * NH, 2 * HPB * (g - 1))
                    if g == 0:
                        sp.dma_start(x[par][:, :, :], rows_of(source)[b, :, :, :]).then_inc(side_loaded[par], 16)
                        if gate is not None:
                            sp.dma_start(factor[par][:, :], dram["gates"][b, gate, :].partition_broadcast(QT)).then_inc(side_loaded[par], 16)
                    for strip in range(4):
                        part = slice(strip * HD, (strip + 1) * HD)
                        heads = slice(g * P, (g + 1) * P)
                        q = dram[q_name + ("_hi", "_lo")[strip % 2]].rearrange("k p r -> (k p) r")[heads, rows]
                        k = keys_of[strip // 2][heads, :]
                        sp.dma_start(q4[g % 2][part, :, :].bitcast(FP32), q.rearrange("(h d) r -> d h r", d=HD)).then_inc(qk_loaded[g % 2], 16)
                        sp.dma_start(k4[g % 2][part, :, 0:keys].bitcast(FP32), k.rearrange("(h d) s -> d h s", d=HD)).then_inc(qk_loaded[g % 2], 16)
                    if isinstance(b, int) and b == 0 and g == 1:
                        sp.dma_start(w_raw[:, :, :], dram[w_name].rearrange("(k p) n -> p k n", p=P)).then_inc(w_loaded, 16)
                        sp.dma_start(b_out[:, :], dram[b_name].partition_broadcast(QT)).then_inc(bias_loaded, 16)
                if not isinstance(b, int) or b > 0:
                    sp.wait_ge(y_added, b)
                    sp.dma_start(rows_of(target)[b - 1, :, :, :], y[:, :, :]).then_inc(stored, 16)

            step(0, 0)
            step(1, 1)
            with sp.Fori(1, B // 2) as i:
                step(2 * i, 0)
                step(2 * i + 1, 1)
            sp.wait_ge(y_added, B)
            sp.dma_start(rows_of(target)[B - 1, :, :, :], y[:, :, :]).then_inc(stored, 16)
            sp.wait_ge(stored, 16 * B)

        @block.gpsimd
        def _(pool):
            nc.gpsimd.memset(pick[:, :], 1.0).then_inc(pick_done, 1)
            for t in k4:
                nc.gpsimd.memset(t[:, :, keys:].bitcast(FP32), 0.0).then_inc(padded, 1)
            pool.wait_ge(pick_done, 1)
            nc.gpsimd.affine_select(out=pick[:, :], in_=pick[:, :], compare_op=ALU.is_ge, fill=0.0, base=0,
                                    pattern=[[1, P]], channel_multiplier=-HD).then_inc(pick_done, 1)
            pool.wait_ge(pick_done, 2)
            nc.gpsimd.affine_select(out=pick[:, :], in_=pick[:, :], compare_op=ALU.is_ge, fill=0.0, base=HD - 1,
                                    pattern=[[-1, P]], channel_multiplier=HD).then_inc(pick_done, 1)

            def slot(b, par, h):
                old = h - lag - 4
                if old % NH == NH - 1 and exists(b, old):
                    done, side = b + (old + 1) // NH, (par + old // NH) % 2
                    n_side = 32 if gate is not None else 16
                    pool.wait_ge(y_done, 2 * done)
                    pool.wait_ge(side_loaded[side], every_second(b + old // NH, side, n_side))
                    if gate is not None:
                        nc.gpsimd.tensor_tensor(y[:, :, :], y[:, :, :], factor[side][:, :].unsqueeze(1).to_broadcast([QT, 2, D]),
                                                ALU.mult).then_inc(y_gated, 1)
                        pool.wait_ge(y_gated, done)
                    nc.gpsimd.tensor_tensor(y[:, :, :], y[:, :, :], x[side][:, :, :], ALU.add).then_inc(y_added, 1)

            slots(pool, slot)

        def emptied_by(b, h, n):
            fill = NP * h + n
            return fill % 2, fill // 2 + 1

        def empty(eng, own, b, par, h):
            for n in range(NP):
                which, nth = emptied_by(b, h, n)
                if which != own:
                    continue
                eng.wait_ge(tr_done, NP * NH * b + NP * h + n + 1)
                group = h // HPB
                wait(eng, pv_done, b, GPB, group - 1)
                out = pt[group % 2][:, h % HPB, 2 * n:2 * n + 2, :]
                src = ps_t[:kc, own, 0:2 * T].rearrange("p (c r) -> p c r", c=2)
                if own == 0:
                    nc.vector.tensor_copy(out, src).then_inc(pt_done[0], 1)
                else:
                    nc.scalar.activation(out, src, ACT.Copy).then_inc(pt_done[1], 1)

        @block.vector
        def _(dve):
            def slot(b, par, h):
                old = h - lag - 4
                if old % NH == NH - 1 and exists(b, old):
                    done = b + (old + 1) // NH
                    wait(dve, stored, done, 16, -16)
                    for q in range(2):
                        dve.wait_ge(y_mm, 2 * done - 1 + q)
                        nc.vector.tensor_tensor(y[:, q, :], ps_o[:QT, q, :], b_out[:, :], ALU.add).then_inc(y_done, 1)
                if h < NH:
                    for q in range(2):
                        n = 2 * h + q
                        dve.wait_ge(s_done, 2 * NH * b + n + 1)
                        wait(dve, exp_done, b, 2 * NH, n + 1 - NPB)
                        nc.vector.tensor_reduce(neg_max[:, n % NPB:n % NPB + 1], ps_s[:QT, n % NS, :, 0:HN], AX.XY, ALU.max,
                                                negate=True).then_inc(max_done, 1)
                old = h - lag
                if group_ends(b, old):
                    dve.wait_ge(exp_done, 2 * NH * b + 2 * (old + 1))
                    wait(dve, rt_done, b, GPB, old // HPB)
                    nc.vector.reciprocal(recip[:, :, :], total[:, old // HPB % 2, :, :]).then_inc(recip_done, 1)
                if exists(b, old):
                    empty(dve, 0, b, par, old)
                old = h - lag - 2
                if group_ends(b, old):
                    g = old // HPB
                    dve.wait_ge(pv_done, GPB * b + g + 1)
                    dve.wait_ge(wide_copied, GPB * b + g + 1)
                    wait(dve, a_lo_done, b, GPB, g)
                    nc.vector.tensor_tensor(a[:, :], ps_o[:, 0, 0:T], recip_wide[:, :], ALU.mult).then_inc(a_done, 1)
                    dve.wait_ge(a_hi_done, GPB * b + g + 1)
                    nc.vector.scalar_tensor_tensor(a_lo[:, g % GPB, :], a[:, :], v_bias[:, g % GPB:g % GPB + 1],
                                                   a_hi[:, g % GPB, :].bitcast(FP32), ALU.add, ALU.subtract).then_inc(a_lo_done, 1)
                if isinstance(b, int) and b == 0 and h == 0:
                    dve.wait_ge(w_hi_done, 1)
                    nc.vector.tensor_tensor(w_lo[:, :, :], w_raw[:, :, :], w_hi[:, :, :].bitcast(FP32), ALU.subtract).then_inc(w_split, 1)
                    dve.wait_ge(bias_loaded, 16)

            slots(dve, slot)

        @block.scalar
        def _(act):
            def slot(b, par, h):
                if h < NH:
                    for q in range(2):
                        n = 2 * h + q
                        g = h // HPB
                        act.wait_ge(max_done, 2 * NH * b + n + 1)
                        wait(act, tr_done, b, NP * NH, NP * (h + 1 - NS))
                        wait(act, recip_done, b, GPB, g - 1)
                        nc.scalar.activation(prob[:, n % NPB, :].rearrange("p (h s) -> p h s", h=halves),
                                             ps_s[:QT, n % NS, :, 0:HN], ACT.Exp, bias=neg_max[:, n % NPB:n % NPB + 1],
                                             accum_out=total[:, g % 2, q, h % HPB:h % HPB + 1]).then_inc(exp_done, 1)
                old = h - lag
                if exists(b, old):
                    empty(act, 1, b, par, old)
                if group_ends(b, old):
                    act.wait_ge(rt_done, GPB * b + old // HPB + 1)
                    nc.scalar.activation(recip_t[:, :], ps_o[:HPB, 1, 0:T], ACT.Copy).then_inc(rt_copied, 1)
                old = h - lag - 1
                if group_ends(b, old):
                    g = old // HPB
                    act.wait_ge(wide_done, GPB * b + g + 1)
                    wait(act, a_done, b, GPB, g)
                    nc.scalar.activation(recip_wide[:, :], ps_o[:, 1, 0:T], ACT.Copy).then_inc(wide_copied, 1)
                old = h - lag - 2
                if group_ends(b, old):
                    g = old // HPB
                    act.wait_ge(a_done, GPB * b + g + 1)
                    wait(act, y_mm, b + old // NH, 2, 0)
                    nc.scalar.activation(a_hi[:, g % GPB, :], a[:, :], ACT.Identity, bias=v_bias[:, g % GPB:g % GPB + 1]).then_inc(a_hi_done, 1)
                if isinstance(b, int) and b == 0 and h == 0:
                    act.wait_ge(w_loaded, 16)
                    nc.scalar.activation(w_hi[:, :, :], w_raw[:, :, :], ACT.Copy).then_inc(w_hi_done, 1)

            slots(act, slot)

        @block.tensor
        def _(pe):
            pe.wait_ge(pick_done, 3)
            pe.wait_ge(padded, 2)

            def slot(b, par, h):
                if h < NH:
                    g, j = h // HPB, h % HPB
                    if j == 0:
                        pe.wait_ge(qk_loaded[g % 2], 128 * (GPB // 2) * b + 128 * (g // 2 + 1))
                    for q in range(2):
                        n = 2 * h + q
                        wait(pe, exp_done, b, 2 * NH, n + 1 - NS)
                        for half in range(halves):
                            last = nc.tensor.matmul(ps_s[:QT, n % NS, half, 0:HN_E], q4[g % 2][:, j, q * QT:(q + 1) * QT],
                                                    k4[g % 2][:, j, half * HN:half * HN + HN_E], start=True, stop=True)
                        last.then_inc(s_done, 1)
                old = h - lag
                if exists(b, old):
                    for n in range(NP):
                        which, nth = emptied_by(b, old, n)
                        wait(pe, pt_done[which], b, NP * NH // 2, nth - 1)
                        if n == 0:
                            wait(pe, exp_done, b, 2 * NH, 2 * (old + 1))
                        for c in range(2):
                            for q in range(2):
                                cols = slice((2 * n + c) * kc, (2 * n + c + 1) * kc)
                                last = nc.tensor.transpose(ps_t[:kc, which, c * T + q * QT:c * T + (q + 1) * QT],
                                                           prob[:, (2 * old + q) % NPB, cols], ident[:QT, :QT])
                        last.then_inc(tr_done, 1)
                if group_ends(b, old):
                    g = old // HPB
                    pe.wait_ge(recip_done, GPB * b + g + 1)
                    wait(pe, wide_copied, b, GPB, g)
                    if g % GPB == 0:
                        wait(pe, y_done, b + g // GPB, 2, 0)
                    for q in range(2):
                        last = nc.tensor.transpose(ps_o[:HPB, 1, q * QT:(q + 1) * QT], recip[:, q, :], ident[:QT, :QT])
                    last.then_inc(rt_done, 1)
                old = h - lag - 1
                if group_ends(b, old):
                    g = old // HPB
                    pe.wait_ge(rt_copied, GPB * b + g + 1)
                    nc.tensor.matmul(ps_o[:, 1, 0:T], pick[:, :], recip_t[:, :], start=True, stop=True).then_inc(wide_done, 1)
                    for which in range(2):
                        pe.wait_ge(pt_done[which], NP * NH // 2 * b + NP * HPB // 2 * (g + 1))
                    if g % GPB == 0:
                        side = (par + g // GPB) % 2
                        pe.wait_ge(v_loaded[side], every_second(b + g // GPB, side, 16))
                    wait(pe, a_done, b, GPB, g)
                    side = (par + g // GPB) % 2
                    for c in range(chunks):
                        for j in range(HPB):
                            cols = slice((g % GPB * HPB + j) * HD, (g % GPB * HPB + j + 1) * HD)
                            last = nc.tensor.matmul(ps_o[j * HD:(j + 1) * HD, 0, 0:T], v[side][:, c, cols], pt[g % 2][:, j, c, :],
                                                    start=c == 0, stop=c == chunks - 1)
                    last.then_inc(pv_done, 1)
                old = h - lag - 3
                if old % NH == NH - 1 and exists(b, old):
                    pe.wait_ge(a_lo_done, GPB * (b + (old + 1) // NH))
                    if isinstance(b, int):
                        pe.wait_ge(w_split, 1)
                    for q in range(2):
                        for k in range(KD):
                            r = slice(q * QT, (q + 1) * QT)
                            last = three_passes(nc, ps_o[:QT, q, :], a_hi[:, k, r], a_lo[:, k, r], w_hi[:, k, :], w_lo[:, k, :],
                                                k == 0, k == KD - 1)
                        last.then_inc(y_mm, 1)

            slots(pe, slot)


def self_attention(nc, dram, const):
    keys = lambda part, b: dram[("k_hi", "k_lo")[part]].rearrange("k p r -> (k p) r")[:, bass.ds(T * b, T)]
    values = lambda b: dram["v_s"][bass.ds(T * b, T), :].rearrange("(c p) d -> p c d", p=QT)
    attention1(nc, dram, const, "sa", 2, QT, 1, "q", keys, values, const["vecs"]["b_qkv"][:, 2 * KD:3 * KD], "W_proj", "b_proj",
               0, "x1", "x2", 2)


def cross_attention(nc, dram, const):
    keys = lambda part, b: dram[("kT_hi", "kT_lo")[part]][b, :, :]
    attention1(nc, dram, const, "ca", KCH, KC, 2, "qc", keys, lambda b: dram["v_c"][b, :, :, :],
               const["vecs"]["b_kvc"][:, KD:2 * KD], "W_cproj", "b_cproj", None, "x2", "x3", 1)


def mlp(nc, dram, const):
    ident, mod = const["ident"], const["mod"]
    NU = MLP // P
    N_SIDE = 1 + RT + sum(T * b % P > 0 for b in range(B))
    x_view = dram["x3"].rearrange("(b j p) d -> b p j d", p=QT, j=2)
    by_tile = lambda name: dram[name].rearrange("(i p) d -> p i d", p=P)
    with ExitStack() as ctx:
        sb = lambda name, shape, dt=FP32: ctx.enter_context(nc.sbuf_tensor("ml_" + name, shape, dt))
        sem = lambda name: ctx.enter_context(nc.semaphore("ml_" + name))
        u = HiddenUnits(nc, ctx, "ml", KD)
        raw = [sb(f"raw{i}", [QT, 2, D]) for i in range(2)]
        xn = [sb(f"xn{i}", [QT, 2, D]) for i in range(2)]
        stats, moments = sb("stats", [QT, 2, 6]), sb("moments", [QT, 2, 2])
        rstd, power, eps_tile = sb("rstd", [QT, 2]), sb("power", [QT, 2]), sb("eps_tile", [QT, 2])
        spare = sb("spare", [QT, 1])
        xt = sb("xt", [P, KD, T])
        b2 = sb("b2", [P, D])
        bias = sb("bias", [P, 2])
        x3 = sb("x3", [P, RT, D])
        factor = sb("factor", [P, RT, D])
        raw_loaded = [sem("raw_loaded0"), sem("raw_loaded1")]
        stats_done, aggr_done, rstd_add, rstd_done = sem("stats_done"), sem("aggr_done"), sem("rstd_add"), sem("rstd_done")
        xn_done, tr_done, xt_done, xt_hi_done, xt_lo_done = sem("xn_done"), sem("tr_done"), sem("xt_done"), sem("xt_hi_done"), sem("xt_lo_done")
        bias_done = sem("bias_done")
        side_loaded, b2_loaded, scaled, summed, stored = sem("side_loaded"), sem("b2_loaded"), sem("scaled"), sem("summed"), sem("stored")
        block = ctx.enter_context(nc.Block())

        def units(eng, unit):
            unit(0, 0)
            unit(1, 1)
            with eng.Fori(1, NU // 2) as i:
                for slot in range(2):
                    unit(2 * i + slot, slot)

        @block.sync
        def _(sp):
            def load(b, par):
                sp.dma_start(raw[par][:, :, :], x_view[b, :, :, :]).then_inc(raw_loaded[par], 16)

            weights = lambda n, slot: u.load(sp, n, dram["W_mlp1"][:, bass.ds(n * P, P)], dram["W_mlp2"][bass.ds(n * P, P), :])
            load(0, 0)
            load(1, 1)
            weights(0, 0)
            sp.dma_start(b2[:, :], dram["b_mlp2"].partition_broadcast(P)).then_inc(b2_loaded, 16)

            def step(b, par, has_next, has_second):
                if has_second:
                    sp.wait_ge(xn_done, 2 * (b + 1))
                    load(b + 2, par)

            batches(sp, step)
            n_side = 1
            sp.dma_start(x3[:, :, :], by_tile("x3")).then_inc(side_loaded, 16)
            for i in range(RT):
                at = i * P
                while at < (i + 1) * P:
                    b = at // T
                    end = min((i + 1) * P, (b + 1) * T)
                    sp.dma_start(factor[at - i * P:end - i * P, i, :], dram["gates"][b, 1, :].partition_broadcast(end - at)).then_inc(side_loaded, 16)
                    n_side += 1
                    at = end
            assert n_side == N_SIDE
            units(sp, lambda n, slot: None if isinstance(n, int) and n == 0 else weights(n, slot))
            for i in range(RT):
                sp.wait_ge(summed, i + 1)
                sp.dma_start(by_tile("y")[:, i, :], u.acc[:, i, :]).then_inc(stored, 16)
            sp.wait_ge(stored, 16 * RT)

        @block.gpsimd
        def _(pool):
            nc.gpsimd.memset(power[:, :], -0.5).then_inc(rstd_add, 1)
            nc.gpsimd.memset(eps_tile[:, :], EPS1).then_inc(rstd_add, 1)
            pool.wait_ge(rstd_add, 2)

            def step(b):
                pool.wait_ge(aggr_done, b + 1)
                after_first(pool, b, xn_done, 2 * b)
                nc.gpsimd.tensor_tensor(rstd[:, :], moments[:, :, 1], eps_tile[:, :], ALU.add).then_inc(rstd_add, 1)
                pool.wait_ge(rstd_add, b + 3)
                nc.gpsimd.tensor_tensor(rstd[:, :], rstd[:, :], power[:, :], ALU.pow).then_inc(rstd_done, 1)

            step(0)
            u.split_lo(pool, 0, 0)
            with pool.Fori(1, B) as b:
                step(b)
            units(pool, lambda n, slot: None if isinstance(n, int) and n == 0 else u.split_lo(pool, n, slot))

        @block.vector
        def _(dve):
            def normalise(b, par):
                dve.wait_ge(raw_loaded[par], 16 * (b // 2) + 16 if isinstance(b, int) else 8 * (b - par) + 16)
                after_first(dve, b, rstd_done, b)
                for j in range(2):
                    nc.vector.bn_stats(stats[:, j, :], raw[par][:, j, :]).then_inc(stats_done, 1)
                dve.wait_ge(stats_done, 2 * (b + 1))
                after_first(dve, b, xn_done, 2 * b)
                nc.vector.memset(spare[:, :], 0.0)
                for j in range(2):
                    last = nc.vector.bn_aggr(moments[:, j, :], stats[:, j, :])
                last.then_inc(aggr_done, 1)
                dve.wait_ge(rstd_done, b + 1)
                if not isinstance(b, int) or b > 1:
                    dve.wait_ge(tr_done, KD * (b - 1))
                for j in range(2):
                    nc.vector.tensor_scalar(xn[par][:, j, :], raw[par][:, j, :], moments[:, j, 0:1], rstd[:, j:j + 1],
                                            ALU.subtract, ALU.mult).then_inc(xn_done, 1)

            def step(b, par, has_next, has_second):
                if has_next:
                    normalise(b + 1, 1 - par)
                cols = bass.ds(T * b, T)
                for f in range(KD):
                    dve.wait_ge(xt_done, KD * b + f + 1)
                    nc.vector.tensor_copy(u.x_hi[:, f, cols], xt[:, f, :]).then_inc(xt_hi_done, 1)
                    dve.wait_ge(xt_hi_done, KD * b + f + 1)
                    nc.vector.tensor_tensor(u.x_lo[:, f, cols], xt[:, f, :], u.x_hi[:, f, cols].bitcast(FP32),
                                            ALU.subtract).then_inc(xt_lo_done, 1)

            normalise(0, 0)
            batches(dve, step)
            dve.wait_ge(b2_loaded, 16)
            for i in range(RT):
                nc.vector.tensor_copy(u.acc[:, i, :], b2[:, :]).then_inc(u.acc_ready, 1)
            dve.wait_ge(u.acc_ready, RT)

            def unit(n, slot):
                for g in range(NG):
                    u.split_h(dve, n, g)
                for i in range(RT):
                    u.accumulate(dve, n, i, 1.0, slot)

            units(dve, unit)
            dve.wait_ge(side_loaded, 16 * N_SIDE)
            for i in range(RT):
                dve.wait_ge(u.y_done, RT * (NU - 1) + i + 1)
                nc.vector.tensor_tensor(u.acc[:, i, :], u.acc[:, i, :], factor[:, i, :], ALU.mult).then_inc(scaled, 1)
                dve.wait_ge(scaled, i + 1)
                nc.vector.tensor_tensor(u.acc[:, i, :], u.acc[:, i, :], x3[:, i, :], ALU.add).then_inc(summed, 1)

        @block.scalar
        def _(act):
            def transposed(b, f):
                act.wait_ge(tr_done, KD * b + f + 1)
                after_first(act, b, xt_lo_done, KD * (b - 1) + f + 1)
                one = bass.ds(b, 1)
                nc.scalar.activation(xt[:, f, :], u.ps_y[:, f, 0:T], ACT.Identity, bias=mod[:, 3 * KD + f, one],
                                     scale=mod[:, 4 * KD + f, one]).then_inc(xt_done, 1)

            for f in range(KD):
                transposed(0, f)
            u.split_hi(act, 0, 0)
            with act.Fori(1, B) as b:
                for f in range(KD):
                    transposed(b, f)

            def unit(n, slot):
                if not isinstance(n, int) or n > 0:
                    u.split_hi(act, n, slot)
                nc.scalar.activation(bias[:, slot:slot + 1], const["vecs"]["b_mlp1"][:, bass.ds(n, 1)], ACT.Copy).then_inc(bias_done, 1)
                act.wait_ge(bias_done, n + 1)
                for g in range(NG):
                    u.activate(act, n, ACT.Gelu_apprx_tanh, lambda b: bias[:, slot:slot + 1], g)

            units(act, unit)

        @block.tensor
        def _(pe):
            def step(b, par, has_next, has_second):
                pe.wait_ge(xn_done, 2 * (b + 1))
                for f in range(KD):
                    after_first(pe, b, xt_done, KD * (b - 1) + f + 1)
                    for j in range(2):
                        last = nc.tensor.transpose(u.ps_y[:, f, j * QT:(j + 1) * QT], xn[par][:, j, f * P:(f + 1) * P], ident[:QT, :QT])
                    last.then_inc(tr_done, 1)

            batches(pe, step)
            pe.wait_ge(xt_lo_done, KD * B)
            units(pe, lambda n, slot: u.multiply(pe, n, slot, slot))


STAGES = [conditioning, context_kv, project_scores0, attention0, mixture, residual, project_qkv, self_attention,
          project_qc, cross_attention, mlp]


VECS = 100


def program(nc, io, out, stages=None):
    dram = dict(io)
    dram["out"] = out

    def scratch(name, shape, dt=FP32):
        dram[name] = nc.dram_tensor(name, shape, dt, kind="Internal").ap()

    for name in ("b_mod", "e_b1", "gate_b1", "ln_gamma", "ln_beta", "b_qkv", "b_qc", "b_kvc", "b_mlp1"):
        v = dram[name]
        dram["rows_" + name] = v.rearrange("e (k p) -> (e k) p", p=P) if name == "e_b1" else v.rearrange("(k p) -> k p", p=P)
    scratch("W_qk", (D, D))
    scratch("gates", (B, 2, D))
    for name in ("comb_hi", "comb_lo"):
        scratch(name, (2 * KD, P, R))
    for name in ("u_hi", "u_lo", "q_hi", "q_lo", "k_hi", "k_lo", "qc_hi", "qc_lo"):
        scratch(name, (KD, P, R))
    scratch("v_s", (R, D))
    scratch("routed", (R, D))
    scratch("gate", (R, D))
    for name in ("x1", "x2", "x3"):
        scratch(name, (R, D))
    scratch("kT_hi", (B, D, S))
    scratch("kT_lo", (B, D, S))
    scratch("v_c", (B, KC, KCH, D))
    dram["x0"] = dram["x"].rearrange("b t d -> (b t) d")
    dram["y"] = out.rearrange("b t d -> (b t) d")
    with ExitStack() as ctx:
        sb = lambda name, shape, dt=FP32: ctx.enter_context(nc.sbuf_tensor(name, shape, dt))
        const = {
            "ident": sb("ident", [P, P]),
            "mod": sb("mod", [P, 6 * KD, B]),
            "anchor": sb("anchor", [P, E * HCH + KD, B]),
            "router_anchor": sb("router_anchor", [E, B]),
        }
        columns = sb("columns", [P, VECS])
        vecs = {"all": columns, "hidden": columns[:, 24:52]}
        at = 0
        for name, k in (("b_mod", 24), ("e_b1", 24), ("gate_b1", 4), ("ln_gamma", 4), ("ln_beta", 4), ("b_qkv", 12),
                        ("b_qc", 4), ("b_kvc", 8), ("b_mlp1", 16)):
            vecs[name] = columns[:, at:at + k]
            at += k
        const["vecs"] = vecs
        for stage in STAGES if stages is None else stages:
            if stage is project_qkv:
                used = list(nc.released_uncleared_semaphores)
                nc.gpsimd.sem_clear(range(min(used), max(used) + 1))
                nc.all_engine_barrier()
            stage(nc, dram, const)


NAMES = {
    "x": "x", "cond": "cond_1024", "ctx": "ctx_1024", "ln_gamma": "L0_xcond_ln_gamma", "ln_beta": "L0_xcond_ln_beta",
    "Wq": "L0_xcond_Wq", "Wk": "L0_xcond_Wk", "Wv": "L0_xcond_Wv", "router_W": "L0_xcond_router_W",
    "router_b": "L0_xcond_router_b", "e_w1": "L0_xcond_e_w1", "e_b1": "L0_xcond_e_b1", "e_w2": "L0_xcond_e_w2",
    "e_b2": "L0_xcond_e_b2", "gate_w1": "L0_xcond_gate_w1", "gate_b1": "L0_xcond_gate_b1",
    "gate_w2": "L0_xcond_gate_w2", "gate_b2": "L0_xcond_gate_b2", "out_w": "L0_xcond_out_w",
    "out_b": "L0_xcond_out_b", "W_mod": "L1_xcond_W_mod", "b_mod": "L1_xcond_b_mod", "W_qkv": "L1_xcond_W_qkv",
    "b_qkv": "L1_xcond_b_qkv", "W_proj": "L1_xcond_W_proj", "b_proj": "L1_xcond_b_proj", "W_qc": "L1_xcond_W_qc",
    "b_qc": "L1_xcond_b_qc", "W_kvc": "L1_xcond_W_kvc", "b_kvc": "L1_xcond_b_kvc", "W_cproj": "L1_xcond_W_cproj",
    "b_cproj": "L1_xcond_b_cproj", "W_mlp1": "L1_xcond_W_mlp1", "b_mlp1": "L1_xcond_b_mlp1",
    "W_mlp2": "L1_xcond_W_mlp2", "b_mlp2": "L1_xcond_b_mlp2",
}


def kernel(**inputs):
    import numpy as np
    import concourse.bacc as bacc
    from concourse.bass_utils import run_bass_kernel_spmd

    nc = bacc.Bacc("TRN2", target_bir_lowering=False, num_devices=1)
    arrays, io = {}, {}
    for name, given in NAMES.items():
        a = np.ascontiguousarray(inputs[given])
        arrays["in_" + name] = a
        io[name] = nc.dram_tensor("in_" + name, a.shape, mybir.dt.from_np(a.dtype), kind="ExternalInput").ap()
    out = nc.dram_tensor("out", (B, T, D), FP32, kind="ExternalOutput").ap()
    program(nc, io, out)
    result = run_bass_kernel_spmd(nc, [arrays], core_ids=[0])
    return result.results[0]["out"]
```

```python
import concourse.bass as bass
from concourse import mybir
from contextlib import ExitStack

FP32 = mybir.dt.float32
F32R = mybir.dt.float32r
ALU = mybir.AluOpType
ACT = mybir.ActivationFunctionType
AX = mybir.AxisListType

B, T, D, S = 8, 224, 512, 750
R = B * T
P = 128
KD = D // P
QT = T // 2
GROUP = 2 * T
NG = R // GROUP
TPG = GROUP // QT
KC, KCH = S // 6, 6
HALF = S // 2
HALF_E, S_E = HALF + HALF % 2, S + 2
NH, HD = 16, 32
E, HID = 3, 1024
HCH = HID // P
MLP = 2048
SCALE0, SCALE1 = float(D) ** -0.5, float(HD) ** -0.5
EPS0, EPS1 = 1e-5, 1e-6


def three_passes(nc, out, lhs_hi, lhs_lo, rhs_hi, rhs_lo, first, last):
    nc.tensor.matmul(out, lhs_lo, rhs_hi, start=first, stop=False)
    nc.tensor.matmul(out, lhs_hi, rhs_lo, start=False, stop=False)
    return nc.tensor.matmul(out, lhs_hi, rhs_hi, start=False, stop=last)


def batches(eng, step):
    step(0, 0, True, True)
    step(1, 1, True, True)
    with eng.Fori(1, B // 2 - 1) as i:
        for par in range(2):
            step(2 * i + par, par, True, True)
    step(B - 2, 0, True, False)
    step(B - 1, 1, False, False)


def after_first(eng, b, sem, value):
    if not isinstance(b, int) or b > 0:
        eng.wait_ge(sem, value)


def conditioning(nc, dram, const):
    ident, vecs, mod, anchor = const["ident"], const["vecs"], const["mod"], const["anchor"]
    NM = 6 * KD
    NA = (E + 1) * HCH - HCH // 2
    names = [("b_mod", 24), ("e_b1", 24), ("gate_b1", 4), ("ln_gamma", 4), ("ln_beta", 4), ("b_qkv", 12),
             ("b_qc", 4), ("b_kvc", 8), ("b_mlp1", 16)]
    with ExitStack() as ctx:
        sb = lambda name, shape, dt=FP32: ctx.enter_context(nc.sbuf_tensor("cd_" + name, shape, dt))
        sem = lambda name: ctx.enter_context(nc.semaphore("cd_" + name))
        rows = sb("rows", [VECS, P])
        cond = sb("cond", [B, D])
        silu = sb("silu", [B, D])
        condT = sb("condT", [P, KD, B])
        siluT = sb("siluT", [P, KD, B])
        w_mod = sb("w_mod", [P, KD, 6 * D])
        w_e1 = sb("w_e1", [P, E, KD, HID])
        w_g1 = sb("w_g1", [P, KD, D])
        w_r = sb("w_r", [P, KD, E])
        r_bias = sb("r_bias", [E, 1])
        g_bias = sb("g_bias", [B, 2, D])
        gates = sb("gates", [B, 2, D])
        w_q, w_k = sb("w_q", [P, KD, D]), sb("w_k", [P, KD, D])
        wt_hi = sb("wt_hi", [P, 2, KD, D], F32R)
        wt_lo = sb("wt_lo", [P, 2, KD, D], F32R)
        w_qk = sb("w_qk", [P, KD, D])
        products = [(None, condT, w_e1[:, e, :, half * D:(half + 1) * D]) for e in range(E) for half in range(HID // D)]
        products += [(None, condT, w_g1)] + [(part, siluT, w_mod[:, :, part * D:(part + 1) * D]) for part in range(6)]
        row_major = sb("row_major", [B, len(products), D])
        ps = ctx.enter_context(nc.psum_tensor("cd_ps", [P, 6, 512], FP32))
        ps_f = ctx.enter_context(nc.psum_tensor("cd_ps_f", [P, 2, 512], FP32))
        qk_loaded = [sem("q_loaded"), sem("k_loaded")]
        wt_tr, wt_hi_done, wt_lo_done, fold_mm, fold_done = sem("wt_tr"), sem("wt_hi_done"), sem("wt_lo_done"), sem("fold_mm"), sem("fold_done")
        vec_loaded, small_loaded, mod_loaded = sem("vec_loaded"), sem("small_loaded"), sem("mod_loaded")
        anchor_loaded, ident_done = sem("anchor_loaded"), sem("ident_done")
        silu_done, tr_done, copied, mod_mm, mod_done = sem("silu_done"), sem("tr_done"), sem("copied"), sem("mod_mm"), sem("mod_done")
        row_mm, rows_done, gates_done = sem("row_mm"), sem("rows_done"), sem("gates_done")
        stored = sem("stored")
        block = ctx.enter_context(nc.Block())

        @block.sync
        def _(sp):
            for i, (w, name) in enumerate(((w_q, "Wq"), (w_k, "Wk"))):
                sp.dma_start(w[:, :, :], dram[name].rearrange("(k p) n -> p k n", p=P)).then_inc(qk_loaded[i], 16)
            n = 0
            for name, k in names:
                sp.dma_start(rows[n:n + k, :], dram["rows_" + name]).then_inc(vec_loaded, 16)
                n += k
            sp.dma_start(cond[:, :], dram["cond"]).then_inc(small_loaded, 16)
            sp.dma_start(w_mod[:, :, :], dram["W_mod"].rearrange("(k p) n -> p k n", p=P)).then_inc(mod_loaded, 16)
            sp.wait_ge(fold_done, KD)
            sp.dma_start(dram["W_qk"].rearrange("(k p) n -> p k n", p=P), w_qk[:, :, :]).then_inc(stored, 16)
            sp.wait_ge(gates_done, 2)
            sp.dma_start(dram["gates"], gates[:, :, :]).then_inc(stored, 16)
            sp.wait_ge(stored, 32)

        @block.gpsimd
        def _(pool):
            nc.gpsimd.memset(ident[:, :], 0.0).then_inc(ident_done, 1)
            pool.wait_ge(ident_done, 1)
            nc.gpsimd.affine_select(out=ident[:, :], in_=ident[:, :], compare_op=ALU.not_equal, fill=1.0, base=0,
                                    pattern=[[-1, P]], channel_multiplier=1).then_inc(ident_done, 1)

        @block.scalar
        def _(act):
            for e in range(E):
                act.dma_start(w_e1[:, e, :, :], dram["e_w1"][e, 2 * D:, :].rearrange("(k p) n -> p k n", p=P)).then_inc(anchor_loaded, 16)
            act.dma_start(w_g1[:, :, :], dram["gate_w1"][2 * D:, :].rearrange("(k p) n -> p k n", p=P)).then_inc(anchor_loaded, 16)
            act.dma_start(w_r[:, :, :], dram["router_W"][2 * D:, :].rearrange("(k p) n -> p k n", p=P)).then_inc(anchor_loaded, 16)
            act.dma_start(r_bias[:, :], dram["router_b"].rearrange("(e o) -> e o", o=1)).then_inc(anchor_loaded, 16)
            for i, part in enumerate((2, 5)):
                act.dma_start(g_bias[:, i, :], dram["b_mod"][part * D:(part + 1) * D].partition_broadcast(B)).then_inc(anchor_loaded, 16)
            for n in range(2 * KD):
                act.wait_ge(wt_tr, n + 1)
                nc.scalar.activation(wt_hi[:, n // KD, n % KD, :], ps_f[:, n % 2, :], ACT.Copy).then_inc(wt_hi_done, 1)
            act.wait_ge(small_loaded, 16)
            nc.scalar.activation(silu[:, :], cond[:, :], ACT.Silu).then_inc(silu_done, 1)

        @block.vector
        def _(dve):
            for n in range(2 * KD):
                dve.wait_ge(wt_hi_done, n + 1)
                nc.vector.tensor_tensor(wt_lo[:, n // KD, n % KD, :], ps_f[:, n % 2, :],
                                        wt_hi[:, n // KD, n % KD, :].bitcast(FP32), ALU.subtract).then_inc(wt_lo_done, 1)
            for n in range(KD):
                dve.wait_ge(fold_mm, n + 1)
                nc.vector.tensor_scalar(w_qk[:, n, :], ps_f[:, n % 2, :], SCALE0, None, ALU.mult).then_inc(fold_done, 1)
            dve.wait_ge(tr_done, 1)
            nc.vector.tensor_copy(vecs["all"][:, :], ps[:, 0, 0:VECS]).then_inc(copied, 1)
            dve.wait_ge(tr_done, 2)
            nc.vector.tensor_copy(condT[:, :, :], ps[:, 1, 0:KD * B].rearrange("p (k b) -> p k b", k=KD)).then_inc(copied, 1)
            nc.vector.tensor_copy(siluT[:, :, :], ps[:, 1, 64:64 + KD * B].rearrange("p (k b) -> p k b", k=KD)).then_inc(copied, 1)
            for n, (part, _, _) in enumerate(products):
                dve.wait_ge(row_mm, n + 1)
                if part in (2, 5):
                    if part == 2:
                        dve.wait_ge(anchor_loaded, 128)
                    nc.vector.tensor_tensor(gates[:, part // 3, :], ps[:B, 3 + n % 2, :], g_bias[:, part // 3, :], ALU.add).then_inc(gates_done, 1)
                nc.vector.tensor_copy(row_major[:, n, :], ps[:B, 3 + n % 2, :]).then_inc(rows_done, 1)
            dve.wait_ge(mod_mm, 2)
            dve.wait_ge(copied, 1)
            for name, k in (("b_qkv", KD), ("b_qc", KD)):
                last = nc.vector.tensor_scalar(vecs[name][:, 0:k], vecs[name][:, 0:k], SCALE1, None, ALU.mult)
            last.then_inc(mod_done, 1)
            wide = lambda v, n: v.unsqueeze(2).to_broadcast([P, n, B])
            nc.vector.tensor_tensor(mod[:, :, :], ps[:, 2, 0:NM * B].rearrange("p (n b) -> p n b", b=B),
                                    wide(vecs["b_mod"], NM), ALU.add).then_inc(mod_done, 1)
            dve.wait_ge(mod_done, 2)
            for part in (1, 4):
                last = nc.vector.tensor_scalar(mod[:, part * KD:(part + 1) * KD, :], mod[:, part * KD:(part + 1) * KD, :],
                                               1.0, None, ALU.add)
            last.then_inc(mod_done, 1)
            nc.vector.tensor_tensor(anchor[:, :, :], ps[:, 5, 0:NA * B].rearrange("p (n b) -> p n b", b=B),
                                    wide(vecs["hidden"], NA), ALU.add).then_inc(mod_done, 1)
            nc.vector.tensor_scalar(const["router_anchor"][:, :], ps[:E, 5, 256:256 + B], r_bias[:, :], None, ALU.add).then_inc(mod_done, 1)

        @block.tensor
        def _(pe):
            pe.wait_ge(ident_done, 2)
            for n in range(2 * KD):
                if n % KD == 0:
                    pe.wait_ge(qk_loaded[n // KD], 16)
                if n >= 2:
                    pe.wait_ge(wt_lo_done, n - 1)
                w = (w_q, w_k)[n // KD]
                for k in range(KD):
                    last = nc.tensor.transpose(ps_f[:, n % 2, k * P:(k + 1) * P], w[:, k, n % KD * P:(n % KD + 1) * P], ident[:, :])
                last.then_inc(wt_tr, 1)
            pe.wait_ge(wt_lo_done, 2 * KD)
            for n in range(KD):
                if n >= 2:
                    pe.wait_ge(fold_done, n - 1)
                i = slice(n * P, (n + 1) * P)
                for k in range(KD):
                    last = three_passes(nc, ps_f[:, n % 2, :], wt_hi[:, 0, k, i], wt_lo[:, 0, k, i], wt_hi[:, 1, k, :],
                                        wt_lo[:, 1, k, :], k == 0, k == KD - 1)
                last.then_inc(fold_mm, 1)
            pe.wait_ge(vec_loaded, 16 * len(names))
            nc.tensor.transpose(ps[:, 0, 0:VECS], rows[:, :], ident[:VECS, :VECS]).then_inc(tr_done, 1)
            pe.wait_ge(small_loaded, 16)
            pe.wait_ge(silu_done, 1)
            for k in range(KD):
                nc.tensor.transpose(ps[:, 1, k * B:(k + 1) * B], cond[:, k * P:(k + 1) * P], ident[:B, :B])
                last = nc.tensor.transpose(ps[:, 1, 64 + k * B:64 + (k + 1) * B], silu[:, k * P:(k + 1) * P], ident[:B, :B])
            last.then_inc(tr_done, 1)
            pe.wait_ge(copied, 3)
            pe.wait_ge(anchor_loaded, 128)
            anchors = NA // KD

            def to_columns(n):
                pe.wait_ge(rows_done, n + 1)
                bank, at = (5, n) if n < anchors else (2, n - anchors)
                for k in range(KD):
                    last = nc.tensor.transpose(ps[:, bank, (at * KD + k) * B:(at * KD + k + 1) * B], row_major[:, n, k * P:(k + 1) * P], ident[:B, :B])
                if n in (anchors - 1, len(products) - 1):
                    last.then_inc(mod_mm, 1)

            for k in range(KD):
                nc.tensor.matmul(ps[:E, 5, 256:256 + B], w_r[:, k, :], condT[:, k, :], start=k == 0, stop=k == KD - 1)
            for n, (part, left, w) in enumerate(products):
                if part == 0:
                    pe.wait_ge(mod_loaded, 16)
                if n >= 2:
                    pe.wait_ge(rows_done, n - 1)
                for k in range(KD):
                    last = nc.tensor.matmul(ps[:B, 3 + n % 2, :], left[:, k, :], w[:, k, :], start=k == 0, stop=k == KD - 1)
                last.then_inc(row_mm, 1)
                if n > 0:
                    to_columns(n - 1)
            to_columns(len(products) - 1)


def context_kv(nc, dram, const):
    ident, vecs = const["ident"], const["vecs"]
    ctx_view = dram["ctx"].rearrange("b (p c) d -> b p c d", c=KCH)
    w_view = dram["W_kvc"].rearrange("(k p) n -> p k n", p=P)
    NCK = 2 * KD
    NC = NCK + KCH
    T0 = KCH
    with ExitStack() as ctx:
        sb = lambda name, shape, dt=FP32: ctx.enter_context(nc.sbuf_tensor("kv_" + name, shape, dt))
        sem = lambda name: ctx.enter_context(nc.semaphore("kv_" + name))
        w_raw = sb("w_raw", [P, KD, 2 * D])
        w_hi, w_lo = sb("w_hi", [P, KD, 2 * D], F32R), sb("w_lo", [P, KD, 2 * D], F32R)
        raw = [sb(f"raw{i}", [KC, KCH, D]) for i in range(2)]
        xn = sb("xn", [KC, KCH, D])
        stats = sb("stats", [KC, KCH, 6])
        moments = sb("moments", [KC, KCH, 2])
        rstd = sb("rstd", [KC, KCH])
        power, eps_tile = sb("power", [KC, KCH]), sb("eps_tile", [KC, KCH])
        spare = sb("spare", [KC, 1])
        xt_hi = [sb(f"xt_hi{i}", [P, KD, S_E], F32R) for i in range(2)]
        xt_lo = [sb(f"xt_lo{i}", [P, KD, S_E], F32R) for i in range(2)]
        k_hi = sb("k_hi", [P, KD, S], F32R)
        k_lo = sb("k_lo", [P, KD, S], F32R)
        v_sb = sb("v_sb", [KC, KCH, D])
        ps_t = ctx.enter_context(nc.psum_tensor("kv_ps_t", [P, 4, 512], FP32))
        ps_m = ctx.enter_context(nc.psum_tensor("kv_ps_m", [P, 4, 512], FP32))
        w_loaded = [sem(f"w_loaded{k}") for k in range(KD)]
        w_hi_done, w_split = sem("w_hi_done"), sem("w_split")
        raw_loaded = [sem("raw_loaded0"), sem("raw_loaded1")]
        stats_done, aggr_done, rstd_done = sem("stats_done"), sem("aggr_done"), sem("rstd_done")
        rstd_add = sem("rstd_add")
        xn_done, tr_done, xt_hi_done, xt_lo_done = sem("xn_done"), sem("tr_done"), sem("xt_hi_done"), sem("xt_lo_done")
        mm_done, k_hi_done, k_lo_done, v_done = sem("mm_done"), sem("k_hi_done"), sem("k_lo_done"), sem("v_done")
        padded = sem("padded")
        k_stored, v_stored = sem("k_stored"), sem("v_stored")
        block = ctx.enter_context(nc.Block())

        @block.sync
        def _(sp):
            def load(b, par):
                sp.dma_start(raw[par][:, :, :], ctx_view[b, :, :, :]).then_inc(raw_loaded[par], 16)

            load(0, 0)
            for k in range(KD):
                sp.dma_start(w_raw[:, k, :], w_view[:, k, :]).then_inc(w_loaded[k], 16)
            load(1, 1)

            def step(b, par, has_next, has_second):
                if has_second:
                    sp.wait_ge(xn_done, KCH * (b + 1))
                    load(b + 2, par)
                sp.wait_ge(k_lo_done, NCK * (b + 1))
                sp.dma_start(dram["kT_hi"][b, :, :].rearrange("(k p) s -> p k s", p=P), k_hi[:, :, :].bitcast(FP32)).then_inc(k_stored, 16)
                sp.dma_start(dram["kT_lo"][b, :, :].rearrange("(k p) s -> p k s", p=P), k_lo[:, :, :].bitcast(FP32)).then_inc(k_stored, 16)
                sp.wait_ge(v_done, KCH * (b + 1))
                sp.dma_start(dram["v_c"][b, :, :, :], v_sb[:, :, :]).then_inc(v_stored, 16)

            batches(sp, step)
            sp.wait_ge(k_stored, 32 * B)
            sp.wait_ge(v_stored, 16 * B)

        @block.gpsimd
        def _(pool):
            nc.gpsimd.memset(power[:, :], -0.5).then_inc(rstd_add, 1)
            nc.gpsimd.memset(eps_tile[:, :], EPS1).then_inc(rstd_add, 1)
            pool.wait_ge(rstd_add, 2)
            for t in (*xt_hi, *xt_lo):
                nc.gpsimd.memset(t[:, :, S:].bitcast(FP32), 0.0).then_inc(padded, 1)

            def step(b):
                pool.wait_ge(aggr_done, b + 1)
                after_first(pool, b, xn_done, KCH * b)
                nc.gpsimd.tensor_tensor(rstd[:, :], moments[:, :, 1], eps_tile[:, :], ALU.add).then_inc(rstd_add, 1)
                pool.wait_ge(rstd_add, b + 3)
                nc.gpsimd.tensor_tensor(rstd[:, :], rstd[:, :], power[:, :], ALU.pow).then_inc(rstd_done, 1)

            step(0)
            with pool.Fori(1, B) as b:
                step(b)

        @block.vector
        def _(dve):
            def statistics(b, par):
                dve.wait_ge(raw_loaded[par], 16 * (b // 2) + 16 if isinstance(b, int) else 8 * (b - par) + 16)
                if not isinstance(b, int) or b > 0:
                    dve.wait_ge(xn_done, KCH * b)
                for c in range(KCH):
                    nc.vector.bn_stats(stats[:, c, :], raw[par][:, c, :]).then_inc(stats_done, 1)
                dve.wait_ge(stats_done, KCH * (b + 1))
                nc.vector.memset(spare[:, :], 0.0)
                for c in range(KCH):
                    last = nc.vector.bn_aggr(moments[:, c, :], stats[:, c, :])
                last.then_inc(aggr_done, 1)

            def normalise(b, par):
                dve.wait_ge(rstd_done, b + 1)
                after_first(dve, b, tr_done, NCK * b)
                for c in range(KCH):
                    nc.vector.tensor_scalar(xn[:, c, :], raw[par][:, c, :], moments[:, c, 0:1], rstd[:, c:c + 1],
                                            ALU.subtract, ALU.mult).then_inc(xn_done, 1)

            def transposed_lo(b, par, s):
                half, f = s // KD, s % KD
                cols = slice(half * HALF, (half + 1) * HALF)
                dve.wait_ge(xt_hi_done, NCK * b + s + 1)
                nc.vector.tensor_tensor(xt_lo[par][:, f, cols], ps_t[:, s % 4, 0:HALF],
                                        xt_hi[par][:, f, cols].bitcast(FP32), ALU.subtract).then_inc(xt_lo_done, 1)

            statistics(0, 0)
            normalise(0, 0)
            for k in range(KD):
                dve.wait_ge(w_hi_done, k + 1)
                nc.vector.tensor_tensor(w_lo[:, k, :], w_raw[:, k, :], w_hi[:, k, :].bitcast(FP32),
                                        ALU.subtract).then_inc(w_split, 1)
            for s in range(NCK):
                transposed_lo(0, 0, s)

            def step(b, par, has_next, has_second):
                if has_next:
                    statistics(b + 1, 1 - par)
                for s in range(NC):
                    bank = (NC * par + s) % 4
                    if has_next and s == 1:
                        normalise(b + 1, 1 - par)
                    if s < NCK:
                        half, f = s // KD, s % KD
                        cols = slice(half * HALF, (half + 1) * HALF)
                        dve.wait_ge(k_hi_done, NCK * b + s + 1)
                        nc.vector.scalar_tensor_tensor(k_lo[:, f, cols], ps_m[:, bank, 0:HALF], vecs["b_kvc"][:, f:f + 1],
                                                       k_hi[:, f, cols].bitcast(FP32), ALU.add,
                                                       ALU.subtract).then_inc(k_lo_done, 1)
                    if has_next and s >= T0:
                        transposed_lo(b + 1, 1 - par, s - T0)

            batches(dve, step)

        @block.scalar
        def _(act):
            def transposed_hi(b, par, s):
                half, f = s // KD, s % KD
                act.wait_ge(tr_done, NCK * b + s + 1)
                if not isinstance(b, int) or b > 1:
                    act.wait_ge(mm_done, NC * (b - 1))
                nc.scalar.activation(xt_hi[par][:, f, half * HALF:(half + 1) * HALF], ps_t[:, s % 4, 0:HALF],
                                     ACT.Copy).then_inc(xt_hi_done, 1)

            for k in range(KD):
                act.wait_ge(w_loaded[k], 16)
                nc.scalar.activation(w_hi[:, k, :], w_raw[:, k, :], ACT.Copy).then_inc(w_hi_done, 1)
            for s in range(NCK):
                transposed_hi(0, 0, s)

            def step(b, par, has_next, has_second):
                for s in range(NC):
                    bank = (NC * par + s) % 4
                    act.wait_ge(mm_done, NC * b + s + 1)
                    if s < NCK:
                        half, f = s // KD, s % KD
                        if s == 0 and (not isinstance(b, int) or b > 0):
                            act.wait_ge(k_stored, 32 * b)
                        nc.scalar.activation(k_hi[:, f, half * HALF:(half + 1) * HALF], ps_m[:, bank, 0:HALF],
                                             ACT.Identity, bias=vecs["b_kvc"][:, f:f + 1]).then_inc(k_hi_done, 1)
                    else:
                        if s == NCK and (not isinstance(b, int) or b > 0):
                            act.wait_ge(v_stored, 16 * b)
                        nc.scalar.activation(v_sb[:, s - NCK, :], ps_m[:KC, bank, :], ACT.Copy).then_inc(v_done, 1)
                    if has_next and s >= T0:
                        transposed_hi(b + 1, 1 - par, s - T0)

            batches(act, step)

        @block.tensor
        def _(pe):
            def transposes(b, s):
                half, f = s // KD, s % KD
                if s % KD == 0:
                    pe.wait_ge(xn_done, KCH * b + 3 * half + 3)
                if not isinstance(b, int) or NCK * b + s >= 4:
                    pe.wait_ge(xt_lo_done, NCK * b + s - 3)
                for j in range(3):
                    last = nc.tensor.transpose(ps_t[:, s % 4, j * KC:(j + 1) * KC],
                                               xn[:, 3 * half + j, f * P:(f + 1) * P], ident[:KC, :KC])
                last.then_inc(tr_done, 1)

            for s in range(NCK):
                transposes(0, s)
            pe.wait_ge(w_split, KD)
            pe.wait_ge(padded, 4)

            def step(b, par, has_next, has_second):
                for s in range(NC):
                    bank = (NC * par + s) % 4
                    if s < NCK:
                        half, f = s // KD, s % KD
                        if s == 0:
                            pe.wait_ge(xt_lo_done, NCK * (b + 1))
                    ago = s - 4
                    if ago >= NCK:
                        pe.wait_ge(v_done, KCH * b + ago - NCK + 1)
                    elif ago >= 0:
                        pe.wait_ge(k_lo_done, NCK * b + ago + 1)
                    elif not isinstance(b, int) or b > 0:
                        pe.wait_ge(v_done, KCH * b + ago + 1)
                    for k in range(KD):
                        if s < NCK:
                            cols, out = slice(half * HALF, half * HALF + HALF_E), ps_m[:, bank, 0:HALF_E]
                            w = slice(f * P, (f + 1) * P)
                            last = three_passes(nc, out, w_hi[:, k, w], w_lo[:, k, w], xt_hi[par][:, k, cols],
                                                xt_lo[par][:, k, cols], k == 0, k == KD - 1)
                        else:
                            c = slice((s - NCK) * KC, (s - NCK + 1) * KC)
                            last = three_passes(nc, ps_m[:KC, bank, :], xt_hi[par][:, k, c], xt_lo[par][:, k, c],
                                                w_hi[:, k, D:], w_lo[:, k, D:], k == 0, k == KD - 1)
                    last.then_inc(mm_done, 1)
                    if has_next and s >= T0:
                        transposes(b + 1, s - T0)

            batches(pe, step)


def project(nc, dram, const, tag, source, eps, weights, affine, fm, rm, keep, queries=0):
    ident = const["ident"]
    x_view = dram[source].rearrange("(b j p) d -> b p j d", p=QT, j=2)
    width = weights.shape[1]
    w_view = weights.rearrange("(k p) n -> p k n", p=P)
    NF = len(fm)
    NR = 2 if rm is not None else 0
    NC = NF + NR
    NW = (queries > 0) + (width > queries)
    T0 = NC - 4
    with ExitStack() as ctx:
        sb = lambda name, shape, dt=FP32: ctx.enter_context(nc.sbuf_tensor(f"{tag}_{name}", shape, dt))
        sem = lambda name: ctx.enter_context(nc.semaphore(f"{tag}_{name}"))
        w_raw = sb("w_raw", [P, KD, width])
        w_hi, w_lo = sb("w_hi", [P, KD, width], F32R), sb("w_lo", [P, KD, width], F32R)
        raw = [sb(f"raw{i}", [QT, 2, D]) for i in range(2)]
        xn = [sb(f"xn{i}", [QT, 2, D]) for i in range(2)]
        stats, moments = sb("stats", [QT, 2, 6]), sb("moments", [QT, 2, 2])
        rstd, power, eps_tile = sb("rstd", [QT, 2]), sb("power", [QT, 2]), sb("eps_tile", [QT, 2])
        spare = sb("spare", [QT, 1])
        xt = sb("xt", [P, KD, T])
        xt_hi = [sb(f"xt_hi{i}", [P, KD, T], F32R) for i in range(2)]
        xt_lo = [sb(f"xt_lo{i}", [P, KD, T], F32R) for i in range(2)]
        f_hi = [sb(f"f_hi{i}", [P, NF, T], F32R) for i in range(2)]
        f_lo = [sb(f"f_lo{i}", [P, NF, T], F32R) for i in range(2)]
        r_sb = [sb(f"r_sb{i}", [QT, 2, D]) for i in range(2)]
        ps_t = ctx.enter_context(nc.psum_tensor(tag + "_ps_t", [P, KD, 512], FP32))
        ps_m = ctx.enter_context(nc.psum_tensor(tag + "_ps_m", [P, 4, 512], FP32))
        w_loaded = [sem(f"w_loaded{k}") for k in range(KD)]
        w_hi_done, w_split = sem("w_hi_done"), sem("w_split")
        raw_loaded = [sem("raw_loaded0"), sem("raw_loaded1")]
        stats_done, aggr_done, rstd_add, rstd_done = sem("stats_done"), sem("aggr_done"), sem("rstd_add"), sem("rstd_done")
        xn_done, tr_done, xt_done, xt_hi_done, xt_lo_done = sem("xn_done"), sem("tr_done"), sem("xt_done"), sem("xt_hi_done"), sem("xt_lo_done")
        mm_done, f_hi_done, f_lo_done, r_done = sem("mm_done"), sem("f_hi_done"), sem("f_lo_done"), sem("r_done")
        kept = [sem("kept0"), sem("kept1")]
        stored = [sem("stored0"), sem("stored1")]
        NS = 16 * (2 * NF // KD + NR // 2)
        block = ctx.enter_context(nc.Block())

        def chunks_in(s):
            return [f for f in range(KD) if T0 + f // 2 == s]

        @block.sync
        def _(sp):
            def load(b, par):
                sp.dma_start(raw[par][:, :, :], x_view[b, :, :, :]).then_inc(raw_loaded[par], 16)

            load(0, 0)
            for k in range(KD):
                sp.dma_start(w_raw[:, k, :], w_view[:, k, :]).then_inc(w_loaded[k], 16)
            load(1, 1)

            def step(b, par, has_next, has_second):
                rows = bass.ds(T * b, T)
                if has_second:
                    sp.wait_ge(xn_done, 2 * (b + 1))
                    load(b + 2, par)
                if keep is not None:
                    sp.wait_ge(xt_lo_done, KD * (b + 1))
                    for part, name in ((xt_hi, keep + "_hi"), (xt_lo, keep + "_lo")):
                        sp.dma_start(dram[name][0:KD, :, rows].rearrange("k p r -> p k r"),
                                     part[par][:, :, :].bitcast(FP32)).then_inc(kept[par], 16)
                sp.wait_ge(f_lo_done, NF * (b + 1))
                for n in range(0, NF, KD):
                    for part, suffix in ((f_hi, "_hi"), (f_lo, "_lo")):
                        sp.dma_start(dram[fm[n][2] + suffix][:, :, rows].rearrange("k p r -> p k r"),
                                     part[par][:, n:n + KD, :].bitcast(FP32)).then_inc(stored[par], 16)
                if NR:
                    sp.wait_ge(r_done, 2 * (b + 1))
                    sp.dma_start(dram["v_s"][rows, :].rearrange("(j p) d -> p j d", p=QT), r_sb[par][:, :, :]).then_inc(stored[par], 16)

            batches(sp, step)
            for s in stored:
                sp.wait_ge(s, NS * B // 2)
            if keep is not None:
                sp.wait_ge(kept[0], 16 * B)
                sp.wait_ge(kept[1], 16 * B)

        @block.gpsimd
        def _(pool):
            nc.gpsimd.memset(power[:, :], -0.5).then_inc(rstd_add, 1)
            nc.gpsimd.memset(eps_tile[:, :], eps).then_inc(rstd_add, 1)
            pool.wait_ge(rstd_add, 2)

            def step(b):
                pool.wait_ge(aggr_done, b + 1)
                after_first(pool, b, xn_done, 2 * b)
                nc.gpsimd.tensor_tensor(rstd[:, :], moments[:, :, 1], eps_tile[:, :], ALU.add).then_inc(rstd_add, 1)
                pool.wait_ge(rstd_add, b + 3)
                nc.gpsimd.tensor_tensor(rstd[:, :], rstd[:, :], power[:, :], ALU.pow).then_inc(rstd_done, 1)

            step(0)
            with pool.Fori(1, B) as b:
                step(b)

        @block.vector
        def _(dve):
            def statistics(b, par):
                dve.wait_ge(raw_loaded[par], 16 * (b // 2) + 16 if isinstance(b, int) else 8 * (b - par) + 16)
                after_first(dve, b, rstd_done, b)
                for j in range(2):
                    nc.vector.bn_stats(stats[:, j, :], raw[par][:, j, :]).then_inc(stats_done, 1)
                dve.wait_ge(stats_done, 2 * (b + 1))
                after_first(dve, b, xn_done, 2 * b)
                nc.vector.memset(spare[:, :], 0.0)
                for j in range(2):
                    last = nc.vector.bn_aggr(moments[:, j, :], stats[:, j, :])
                last.then_inc(aggr_done, 1)

            def normalise(b, par):
                dve.wait_ge(rstd_done, b + 1)
                if not isinstance(b, int) or b > 1:
                    dve.wait_ge(tr_done, KD * (b - 1))
                for j in range(2):
                    nc.vector.tensor_scalar(xn[par][:, j, :], raw[par][:, j, :], moments[:, j, 0:1], rstd[:, j:j + 1],
                                            ALU.subtract, ALU.mult).then_inc(xn_done, 1)

            def transposed(b, par, f):
                dve.wait_ge(xt_done, KD * b + f + 1)
                if f == 0:
                    if not isinstance(b, int) or b > 1:
                        dve.wait_ge(mm_done, NC * (b - 1))
                        if keep is not None:
                            dve.wait_ge(kept[par], 16 * (b - par) if not isinstance(b, int) else 32 * (b // 2))
                nc.vector.tensor_copy(xt_hi[par][:, f, :], xt[:, f, :]).then_inc(xt_hi_done, 1)
                dve.wait_ge(xt_hi_done, KD * b + f + 1)
                nc.vector.tensor_tensor(xt_lo[par][:, f, :], xt[:, f, :], xt_hi[par][:, f, :].bitcast(FP32),
                                        ALU.subtract).then_inc(xt_lo_done, 1)

            statistics(0, 0)
            normalise(0, 0)
            for k in range(KD):
                dve.wait_ge(w_hi_done, NW * (k + 1))
                if queries:
                    nc.vector.scalar_tensor_tensor(w_lo[:, k, 0:queries], w_raw[:, k, 0:queries], SCALE1, w_hi[:, k, 0:queries].bitcast(FP32),
                                                   ALU.mult, ALU.subtract).then_inc(w_split, 1)
                if width > queries:
                    nc.vector.tensor_tensor(w_lo[:, k, queries:], w_raw[:, k, queries:], w_hi[:, k, queries:].bitcast(FP32),
                                            ALU.subtract).then_inc(w_split, 1)
            for f in range(KD):
                transposed(0, 0, f)
            statistics(1, 1)
            normalise(1, 1)

            def step(b, par, has_next, has_second):
                for s in range(NC):
                    bank = (NC * par + s) % 4
                    if s < NF:
                        dve.wait_ge(f_hi_done, NF * b + s + 1)
                        nc.vector.scalar_tensor_tensor(f_lo[par][:, s, :], ps_m[:, bank, 0:T], fm[s][1],
                                                       f_hi[par][:, s, :].bitcast(FP32), ALU.add, ALU.subtract).then_inc(f_lo_done, 1)
                    for f in chunks_in(s) if has_next else ():
                        transposed(b + 1, 1 - par, f)
                    if has_second and s == NC - 2:
                        statistics(b + 2, par)
                    if has_second and s == NC - 1:
                        normalise(b + 2, par)

            batches(dve, step)

        @block.scalar
        def _(act):
            def transposed(b, par, f):
                act.wait_ge(tr_done, KD * b + f + 1)
                after_first(act, b, xt_lo_done, KD * (b - 1) + f + 1)
                scale, shift, per_batch = affine(f)
                if per_batch:
                    scale, shift = scale[:, bass.ds(b, 1)], shift[:, bass.ds(b, 1)]
                nc.scalar.activation(xt[:, f, :], ps_t[:, f, 0:T], ACT.Identity, bias=shift, scale=scale).then_inc(xt_done, 1)

            for k in range(KD):
                act.wait_ge(w_loaded[k], 16)
                if queries:
                    nc.scalar.activation(w_hi[:, k, 0:queries], w_raw[:, k, 0:queries], ACT.Copy, scale=SCALE1).then_inc(w_hi_done, 1)
                if width > queries:
                    nc.scalar.activation(w_hi[:, k, queries:], w_raw[:, k, queries:], ACT.Copy).then_inc(w_hi_done, 1)
            for f in range(KD):
                transposed(0, 0, f)

            def step(b, par, has_next, has_second):
                for s in range(NC):
                    bank = (NC * par + s) % 4
                    act.wait_ge(mm_done, NC * b + s + 1)
                    if s == 0 and (not isinstance(b, int) or b > 1):
                        act.wait_ge(stored[par], NS * (b // 2) if isinstance(b, int) else NS // 2 * (b - par))
                    if s < NF:
                        nc.scalar.activation(f_hi[par][:, s, :], ps_m[:, bank, 0:T], ACT.Identity, bias=fm[s][1]).then_inc(f_hi_done, 1)
                    else:
                        nc.scalar.activation(r_sb[par][:, s - NF, :], ps_m[:QT, bank, :], ACT.Copy).then_inc(r_done, 1)
                    for f in chunks_in(s) if has_next else ():
                        transposed(b + 1, 1 - par, f)

            batches(act, step)

        @block.tensor
        def _(pe):
            def transposes(b, par, f):
                if f == 0:
                    pe.wait_ge(xn_done, 2 * (b + 1))
                after_first(pe, b, xt_done, KD * (b - 1) + f + 1)
                for j in range(2):
                    last = nc.tensor.transpose(ps_t[:, f, j * QT:(j + 1) * QT], xn[par][:, j, f * P:(f + 1) * P], ident[:QT, :QT])
                last.then_inc(tr_done, 1)

            for f in range(KD):
                transposes(0, 0, f)
            pe.wait_ge(w_split, NW * KD)

            def step(b, par, has_next, has_second):
                pe.wait_ge(xt_lo_done, KD * (b + 1))
                for s in range(NC):
                    bank = (NC * par + s) % 4
                    ago = (s - 4) % NC
                    done, each = (f_lo_done, NF) if ago < NF else (r_done, NR)
                    nth = ago + 1 if ago < NF else ago - NF + 1
                    if s >= 4:
                        pe.wait_ge(done, each * b + nth)
                    else:
                        after_first(pe, b, done, each * (b - 1) + nth)
                    for k in range(KD):
                        if s < NF:
                            w = slice(fm[s][0], fm[s][0] + P)
                            last = three_passes(nc, ps_m[:, bank, 0:T], w_hi[:, k, w], w_lo[:, k, w], xt_hi[par][:, k, :],
                                                xt_lo[par][:, k, :], k == 0, k == KD - 1)
                        else:
                            r = slice((s - NF) * QT, (s - NF + 1) * QT)
                            last = three_passes(nc, ps_m[:QT, bank, :], xt_hi[par][:, k, r], xt_lo[par][:, k, r],
                                                w_hi[:, k, rm:rm + D], w_lo[:, k, rm:rm + D], k == 0, k == KD - 1)
                    last.then_inc(mm_done, 1)
                    for f in chunks_in(s) if has_next else ():
                        transposes(b + 1, 1 - par, f)

            batches(pe, step)


def project_scores0(nc, dram, const):
    gamma, beta = const["vecs"]["ln_gamma"], const["vecs"]["ln_beta"]
    project(nc, dram, const, "u", "x0", EPS0, dram["W_qk"], lambda f: (gamma[:, f:f + 1], beta[:, f:f + 1], False),
            [(n * P, 0.0, "u", n) for n in range(KD)], None, "comb")


def project_qkv(nc, dram, const):
    mod, bias = const["mod"], const["vecs"]["b_qkv"]
    project(nc, dram, const, "qkv", "x1", EPS1, dram["W_qkv"], lambda f: (mod[:, KD + f, :], mod[:, f, :], True),
            [(n * P, bias[:, n:n + 1], ("q", "k")[n // KD], n % KD) for n in range(2 * KD)], 2 * D, None, D)


def project_qc(nc, dram, const):
    bias = const["vecs"]["b_qc"]
    project(nc, dram, const, "qc", "x2", EPS1, dram["W_qc"], lambda f: (1.0, 0.0, False),
            [(n * P, bias[:, n:n + 1], "qc", n) for n in range(KD)], None, None, D)


def attention0(nc, dram, const):
    ident = const["ident"]
    ctx_view = dram["ctx"].rearrange("b (p c) d -> b p c d", c=KCH)
    w_view = dram["Wv"].rearrange("(k p) n -> p k n", p=P)
    NT = 2 * KD
    NP = KCH // 2
    NM = NP + 2 * KD
    with ExitStack() as ctx:
        sb = lambda name, shape, dt=FP32: ctx.enter_context(nc.sbuf_tensor("a0_" + name, shape, dt))
        sem = lambda name: ctx.enter_context(nc.semaphore("a0_" + name))
        w_raw = sb("w_raw", [P, KD, D])
        w_hi, w_lo = sb("w_hi", [P, KD, D], F32R), sb("w_lo", [P, KD, D], F32R)
        raw = [sb(f"raw{i}", [KC, KCH, D]) for i in range(2)]
        u_hi = [sb(f"u_hi{i}", [P, KD, T], F32R) for i in range(2)]
        u_lo = [sb(f"u_lo{i}", [P, KD, T], F32R) for i in range(2)]
        c_hi = [sb(f"c_hi{i}", [KC, KCH, D], F32R) for i in range(2)]
        c_lo = [sb(f"c_lo{i}", [KC, KCH, D], F32R) for i in range(2)]
        ct_hi = [sb(f"ct_hi{i}", [P, KD, S_E], F32R) for i in range(2)]
        ct_lo = [sb(f"ct_lo{i}", [P, KD, S_E], F32R) for i in range(2)]
        prob = [sb(f"prob{i}", [QT, 2, S]) for i in range(2)]
        neg_max, total, recip = sb("neg_max", [QT, 2]), sb("total", [QT, 2]), sb("recip", [QT, 2])
        pt_hi, pt_lo = sb("pt_hi", [KC, KCH, T], F32R), sb("pt_lo", [KC, KCH, T], F32R)
        e_hi, e_lo = sb("e_hi", [P, KD, T], F32R), sb("e_lo", [P, KD, T], F32R)
        ev_hi, ev_lo = sb("ev_hi", [P, KD, T], F32R), sb("ev_lo", [P, KD, T], F32R)
        ps_s = ctx.enter_context(nc.psum_tensor("a0_ps_s", [P, 2, 2, 512], FP32))
        ps_t = ctx.enter_context(nc.psum_tensor("a0_ps_t", [P, 2, 512], FP32))
        ps_m = ctx.enter_context(nc.psum_tensor("a0_ps_m", [P, 2, 512], FP32))
        padded = sem("padded")
        w_loaded, w_hi_done, w_split = sem("w_loaded"), sem("w_hi_done"), sem("w_split")
        raw_loaded = [sem("raw_loaded0"), sem("raw_loaded1")]
        u_loaded = [sem("u_loaded0"), sem("u_loaded1")]
        tr_done, ct_hi_done, ct_lo_done = sem("tr_done"), sem("ct_hi_done"), sem("ct_lo_done")
        c_hi_done, c_lo_done = sem("c_hi_done"), sem("c_lo_done")
        s_done, max_done, exp_done = sem("s_done"), sem("max_done"), sem("exp_done")
        recip_done, p_done = sem("recip_done"), sem("p_done")
        mm_done, m_hi_done, m_lo_done, stored = sem("mm_done"), sem("m_hi_done"), sem("m_lo_done"), sem("stored")
        block = ctx.enter_context(nc.Block())

        def fill(n, part):
            if n < NP:
                return (pt_hi, pt_lo)[part][:, 2 * n:2 * n + 2, :], KC, 2 * T
            if n < NP + KD:
                return (e_hi, e_lo)[part][:, n - NP, :], P, T
            return (ev_hi, ev_lo)[part][:, n - NP - KD, :], P, T

        def behind(n):
            tiles = {0: (0,), 1: (1,), 2: (2, 3, 4)}.get(n, (n + 2,) if n + 2 < NT else ())
            return tiles, (n - NP if 0 <= n - NP < KCH else None)

        def times(b, par):
            return 16 * (b // 2) + 16 if isinstance(b, int) else 8 * (b - par) + 16

        @block.sync
        def _(sp):
            def load(b, par):
                rows = bass.ds(T * b, T)
                sp.dma_start(raw[par][:, :, :], ctx_view[b, :, :, :]).then_inc(raw_loaded[par], 16)
                for part, name in ((u_hi, "u_hi"), (u_lo, "u_lo")):
                    sp.dma_start(part[par][:, :, :].bitcast(FP32), dram[name][:, :, rows].rearrange("k p r -> p k r")).then_inc(u_loaded[par], 16)

            load(0, 0)
            load(1, 1)
            sp.dma_start(w_raw[:, :, :], w_view).then_inc(w_loaded, 16)

            def step(b, par, has_next, has_second):
                rows = bass.ds(T * b, T)
                if has_second:
                    sp.wait_ge(c_lo_done, KCH * b + KCH)
                    sp.wait_ge(s_done, 2 * b + 2)
                    load(b + 2, par)
                sp.wait_ge(m_lo_done, NM * (b + 1))
                for part, name in ((ev_hi, "comb_hi"), (ev_lo, "comb_lo")):
                    sp.dma_start(dram[name][KD:, :, rows].rearrange("k p r -> p k r"), part[:, :, :].bitcast(FP32)).then_inc(stored, 16)

            batches(sp, step)
            sp.wait_ge(stored, 32 * B)

        @block.gpsimd
        def _(pool):
            for t in (*ct_hi, *ct_lo):
                nc.gpsimd.memset(t[:, :, S:].bitcast(FP32), 0.0).then_inc(padded, 1)

            def split_context(b, par):
                for c in range(KCH):
                    pool.wait_ge(c_hi_done, KCH * b + c + 1)
                    nc.gpsimd.tensor_tensor(c_lo[par][:, c, :], raw[par][:, c, :], c_hi[par][:, c, :].bitcast(FP32),
                                            ALU.subtract).then_inc(c_lo_done, 1)

            split_context(0, 0)
            batches(pool, lambda b, par, has_next, has_second: split_context(b + 1, 1 - par) if has_next else None)

        @block.vector
        def _(dve):
            def transposed(b, par, s):
                cols = slice(s // KD * HALF, (s // KD + 1) * HALF)
                dve.wait_ge(ct_hi_done, NT * b + s + 1)
                nc.vector.tensor_tensor(ct_lo[par][:, s % KD, cols], ps_t[:, s % 2, 0:HALF],
                                        ct_hi[par][:, s % KD, cols].bitcast(FP32), ALU.subtract).then_inc(ct_lo_done, 1)

            def maximum(b, q):
                dve.wait_ge(s_done, 2 * b + q + 1)
                after_first(dve, b, exp_done, 2 * b)
                nc.vector.tensor_reduce(neg_max[:, q:q + 1], ps_s[:QT, q, :, 0:HALF], AX.XY, ALU.max, negate=True).then_inc(max_done, 1)

            def normalise(b, par):
                for q in range(2):
                    dve.wait_ge(exp_done, 2 * b + q + 1)
                    after_first(dve, b, p_done, 2 * b)
                    nc.vector.reciprocal(recip[:, q:q + 1], total[:, q:q + 1]).then_inc(recip_done, 1)
                    dve.wait_ge(recip_done, 2 * b + q + 1)
                    nc.vector.tensor_scalar(prob[par][:, q, :], prob[par][:, q, :], recip[:, q:q + 1], None, ALU.mult).then_inc(p_done, 1)

            for s in range(NT):
                transposed(0, 0, s)
            for q in range(2):
                maximum(0, q)
            normalise(0, 0)
            for s in range(NT):
                transposed(1, 1, s)
            dve.wait_ge(w_hi_done, 1)
            nc.vector.tensor_tensor(w_lo[:, :, :], w_raw[:, :, :], w_hi[:, :, :].bitcast(FP32), ALU.subtract).then_inc(w_split, 1)

            def step(b, par, has_next, has_second):
                if has_next:
                    for q in range(2):
                        maximum(b + 1, q)
                for n in range(NM):
                    hi, rows, cols = fill(n, 0)
                    lo, _, _ = fill(n, 1)
                    dve.wait_ge(m_hi_done, NM * b + n + 1)
                    src = ps_m[:rows, (NM * par + n) % 2, 0:cols]
                    if n < NP:
                        src = src.rearrange("p (c r) -> p c r", c=2)
                    nc.vector.tensor_tensor(lo, src, hi.bitcast(FP32), ALU.subtract).then_inc(m_lo_done, 1)
                    if has_next and n == NP:
                        normalise(b + 1, 1 - par)
                    tiles, _ = behind(n)
                    for tile in tiles if has_second else ():
                        transposed(b + 2, par, tile)

            batches(dve, step)

        @block.scalar
        def _(act):
            def transposed(b, par, s):
                act.wait_ge(tr_done, NT * b + s + 1)
                nc.scalar.activation(ct_hi[par][:, s % KD, s // KD * HALF:(s // KD + 1) * HALF], ps_t[:, s % 2, 0:HALF],
                                     ACT.Copy).then_inc(ct_hi_done, 1)

            def split_context(b, par, c):
                if c == 0:
                    act.wait_ge(raw_loaded[par], times(b, par))
                    if not isinstance(b, int) or b > 1:
                        act.wait_ge(mm_done, NM * (b - 1))
                nc.scalar.activation(c_hi[par][:, c, :], raw[par][:, c, :], ACT.Copy).then_inc(c_hi_done, 1)

            def exponent(b, par, q):
                act.wait_ge(max_done, 2 * b + q + 1)
                if q == 0:
                    if not isinstance(b, int) or b > 1:
                        act.wait_ge(mm_done, NM * b - 2 * NM + NP)
                    after_first(act, b, recip_done, 2 * b)
                nc.scalar.activation(prob[par][:, q, :].rearrange("p (h s) -> p h s", h=2), ps_s[:QT, q, :, 0:HALF], ACT.Exp,
                                     bias=neg_max[:, q:q + 1], accum_out=total[:, q:q + 1]).then_inc(exp_done, 1)

            for s in range(NT):
                transposed(0, 0, s)
            for c in range(KCH):
                split_context(0, 0, c)
            for q in range(2):
                exponent(0, 0, q)
            for s in range(NT):
                transposed(1, 1, s)
            act.wait_ge(w_loaded, 16)
            nc.scalar.activation(w_hi[:, :, :], w_raw[:, :, :], ACT.Copy).then_inc(w_hi_done, 1)

            def step(b, par, has_next, has_second):
                if has_next:
                    exponent(b + 1, 1 - par, 0)
                for n in range(NM):
                    hi, rows, cols = fill(n, 0)
                    act.wait_ge(mm_done, NM * b + n + 1)
                    if n == NP + KD:
                        after_first(act, b, stored, 32 * b)
                    src = ps_m[:rows, (NM * par + n) % 2, 0:cols]
                    if n < NP:
                        src = src.rearrange("p (c r) -> p c r", c=2)
                    nc.scalar.activation(hi, src, ACT.Copy).then_inc(m_hi_done, 1)
                    if has_next and n == 0:
                        exponent(b + 1, 1 - par, 1)
                    tiles, c = behind(n)
                    for tile in tiles if has_second else ():
                        transposed(b + 2, par, tile)
                    if has_next and c is not None:
                        split_context(b + 1, 1 - par, c)

            batches(act, step)

        @block.tensor
        def _(pe):
            def transposes(b, par, s):
                if s == 0:
                    pe.wait_ge(raw_loaded[par], times(b, par))
                if not isinstance(b, int) or NT * b + s >= 2:
                    pe.wait_ge(ct_lo_done, NT * b + s - 1)
                half, f = s // KD, s % KD
                for j in range(3):
                    last = nc.tensor.transpose(ps_t[:, s % 2, j * KC:(j + 1) * KC],
                                               raw[par][:, 3 * half + j, f * P:(f + 1) * P], ident[:KC, :KC])
                last.then_inc(tr_done, 1)

            def scores(b, par):
                pe.wait_ge(u_loaded[par], 2 * times(b, par))
                pe.wait_ge(ct_lo_done, NT * (b + 1))
                for q in range(2):
                    after_first(pe, b, exp_done, 2 * (b - 1) + q + 1)
                    for half in range(2):
                        rows, cols = slice(q * QT, (q + 1) * QT), slice(half * HALF, half * HALF + HALF_E)
                        for k in range(KD):
                            last = three_passes(nc, ps_s[:QT, q, half, 0:HALF_E], u_hi[par][:, k, rows], u_lo[par][:, k, rows],
                                                ct_hi[par][:, k, cols], ct_lo[par][:, k, cols], k == 0, k == KD - 1)
                    last.then_inc(s_done, 1)

            for s in range(NT):
                transposes(0, 0, s)
            pe.wait_ge(padded, 4)
            scores(0, 0)
            for s in range(NT):
                transposes(1, 1, s)

            def step(b, par, has_next, has_second):
                if has_next:
                    scores(b + 1, 1 - par)
                for n in range(NM):
                    bank = (NM * par + n) % 2
                    if not isinstance(b, int) or NM * b + n >= 2:
                        pe.wait_ge(m_lo_done, NM * b + n - 1)
                    if n < NP:
                        if n == 0:
                            pe.wait_ge(p_done, 2 * (b + 1))
                        for c in range(2):
                            for q in range(2):
                                cols = slice((2 * n + c) * KC, (2 * n + c + 1) * KC)
                                last = nc.tensor.transpose(ps_m[:KC, bank, c * T + q * QT:c * T + (q + 1) * QT],
                                                           prob[par][:, q, cols], ident[:QT, :QT])
                    elif n < NP + KD:
                        if n == NP:
                            pe.wait_ge(m_lo_done, NM * b + NP)
                            pe.wait_ge(c_lo_done, KCH * (b + 1))
                        f = slice((n - NP) * P, (n - NP + 1) * P)
                        for c in range(KCH):
                            last = three_passes(nc, ps_m[:, bank, 0:T], c_hi[par][:, c, f], c_lo[par][:, c, f], pt_hi[:, c, :],
                                                pt_lo[:, c, :], c == 0, c == KCH - 1)
                    else:
                        if n == NP + KD:
                            pe.wait_ge(w_split, 1)
                            pe.wait_ge(m_lo_done, NM * b + NP + KD)
                        f = slice((n - NP - KD) * P, (n - NP - KD + 1) * P)
                        for k in range(KD):
                            last = three_passes(nc, ps_m[:, bank, 0:T], w_hi[:, k, f], w_lo[:, k, f], e_hi[:, k, :],
                                                e_lo[:, k, :], k == 0, k == KD - 1)
                    last.then_inc(mm_done, 1)
                    tiles, _ = behind(n)
                    for tile in tiles if has_second else ():
                        transposes(b + 2, par, tile)

            batches(pe, step)


RT = R // P


class HiddenUnits:

    def __init__(self, nc, ctx, tag, ki):
        sb = lambda name, shape, dt=FP32: ctx.enter_context(nc.sbuf_tensor(f"{tag}_{name}", shape, dt))
        sem = lambda name: ctx.enter_context(nc.semaphore(f"{tag}_{name}"))
        self.nc, self.ki, self.width = nc, ki, ki * P + D
        self.x_hi, self.x_lo = sb("x_hi", [P, ki, R], F32R), sb("x_lo", [P, ki, R], F32R)
        self.acc = sb("acc", [P, RT, D])
        self.w_raw = sb("w_raw", [P, self.width])
        self.w_hi = [sb(f"w_hi{i}", [P, self.width], F32R) for i in range(2)]
        self.w_lo = [sb(f"w_lo{i}", [P, self.width], F32R) for i in range(2)]
        self.h = [sb(f"h{i}", [P, GROUP]) for i in range(2)]
        self.h_hi = [sb(f"h_hi{i}", [P, R // 2], F32R) for i in range(2)]
        self.h_lo = [sb(f"h_lo{i}", [P, R // 2], F32R) for i in range(2)]
        self.ps_h = ctx.enter_context(nc.psum_tensor(tag + "_ps_h", [P, NG, 512], FP32))
        self.ps_y = ctx.enter_context(nc.psum_tensor(tag + "_ps_y", [P, 4, 512], FP32))
        self.w_loaded = [sem("w1_loaded"), sem("w2_loaded")]
        self.w_hi_done, self.w_lo_done = sem("w_hi_done"), sem("w_lo_done")
        self.h_mm, self.h_done, self.h_hi_done, self.h_lo_done = sem("h_mm"), sem("h_done"), sem("h_hi_done"), sem("h_lo_done")
        self.y_mm, self.y_done, self.acc_ready = sem("y_mm"), sem("y_done"), sem("acc_ready")

    def load(self, sp, n, w1, w2):
        after_first(sp, n, self.w_lo_done, n)
        sp.dma_start(self.w_raw[:, 0:self.ki * P].rearrange("p (k n) -> p k n", n=P),
                     w1.rearrange("(k p) n -> p k n", p=P)).then_inc(self.w_loaded[0], 16)
        sp.dma_start(self.w_raw[:, self.ki * P:], w2).then_inc(self.w_loaded[1], 16)

    def split_hi(self, act, n, slot):
        for s in self.w_loaded:
            act.wait_ge(s, 16 * (n + 1))
        if not isinstance(n, int) or n > 1:
            act.wait_ge(self.y_mm, RT * (n - 1))
        self.nc.scalar.activation(self.w_hi[slot][:, :], self.w_raw[:, :], ACT.Copy).then_inc(self.w_hi_done, 1)

    def split_lo(self, pool, n, slot):
        pool.wait_ge(self.w_hi_done, n + 1)
        self.nc.gpsimd.tensor_tensor(self.w_lo[slot][:, :], self.w_raw[:, :], self.w_hi[slot][:, :].bitcast(FP32),
                                     ALU.subtract).then_inc(self.w_lo_done, 1)

    def activate(self, act, n, func, bias, group):
        nc = self.nc
        act.wait_ge(self.h_mm, NG * n + group + 1)
        if not isinstance(n, int) or NG * n + group >= 2:
            act.wait_ge(self.h_lo_done, NG * n + group - 1)
        for j in range(2):
            cols = slice(j * T, (j + 1) * T)
            last = nc.scalar.activation(self.h[group % 2][:, cols], self.ps_h[:, group, cols], func, bias=bias(2 * group + j))
        last.then_inc(self.h_done, 1)

    def split_h(self, dve, n, group):
        nc, half = self.nc, group // 2
        cols = slice(group % 2 * GROUP, (group % 2 + 1) * GROUP)
        dve.wait_ge(self.h_done, NG * n + group + 1)
        after_first(dve, n, self.y_mm, RT * (n - 1) + RT // 2 * (half + 1))
        nc.vector.tensor_copy(self.h_hi[half][:, cols], self.h[group % 2][:, :]).then_inc(self.h_hi_done, 1)
        dve.wait_ge(self.h_hi_done, NG * n + group + 1)
        nc.vector.tensor_tensor(self.h_lo[half][:, cols], self.h[group % 2][:, :], self.h_hi[half][:, cols].bitcast(FP32),
                                ALU.subtract).then_inc(self.h_lo_done, 1)

    def accumulate(self, dve, n, tile, weight, par):
        nc = self.nc
        dve.wait_ge(self.y_mm, RT * n + tile + 1)
        after_first(dve, n, self.y_done, RT * (n - 1) + tile + 1)
        nc.vector.scalar_tensor_tensor(self.acc[:, tile, :], self.ps_y[:, (RT * par + tile) % 4, :], weight,
                                       self.acc[:, tile, :], ALU.mult, ALU.add).then_inc(self.y_done, 1)

    def multiply(self, pe, n, slot, par, x_ready=None):
        nc, ki = self.nc, self.ki
        w_hi, w_lo = self.w_hi[slot], self.w_lo[slot]
        pe.wait_ge(self.w_lo_done, n + 1)
        for g in range(NG):
            if x_ready is not None:
                x_ready(g)
            after_first(pe, n, self.h_done, NG * (n - 1) + g + 1)
            cols = slice(g * GROUP, (g + 1) * GROUP)
            for k in range(ki):
                w = slice(k * P, (k + 1) * P)
                last = three_passes(nc, self.ps_h[:, g, 0:GROUP], w_hi[:, w], w_lo[:, w], self.x_hi[:, k, cols],
                                    self.x_lo[:, k, cols], k == 0, k == ki - 1)
            last.then_inc(self.h_mm, 1)
        for i in range(RT):
            half, j = i // (RT // 2), i % (RT // 2)
            if j == 0:
                pe.wait_ge(self.h_lo_done, NG * n + 2 * (half + 1))
            if not isinstance(n, int) or RT * n + i >= 4:
                pe.wait_ge(self.y_done, RT * n + i - 3)
            r = slice(j * P, (j + 1) * P)
            three_passes(nc, self.ps_y[:, (RT * par + i) % 4, :], self.h_hi[half][:, r], self.h_lo[half][:, r],
                         w_hi[:, ki * P:], w_lo[:, ki * P:], True, True).then_inc(self.y_mm, 1)


def mixture(nc, dram, const):
    ident, anchor = const["ident"], const["anchor"]
    KI = 2 * KD
    EU, GU = E * HCH, D // P
    with ExitStack() as ctx:
        sb = lambda name, shape, dt=FP32: ctx.enter_context(nc.sbuf_tensor("mx_" + name, shape, dt))
        sem = lambda name: ctx.enter_context(nc.semaphore("mx_" + name))
        u = HiddenUnits(nc, ctx, "mx", KI)
        b2 = sb("b2", [P, E + 1, D])
        logits = u.acc[0:E, :, :].rearrange("e i d -> e (i d)")[:, 0:R]
        prob = sb("prob", [P, RT, E])
        top, total, recip = sb("top", [P, RT]), sb("total", [P, RT]), sb("recip", [P, RT])
        x_loaded = [sem(f"x_loaded{g}") for g in range(NG)]
        r_zeroed, r_loaded, b2_loaded = sem("r_zeroed"), sem("r_loaded"), sem("b2_loaded")
        r_hi_done, r_lo_done = sem("r_hi_done"), sem("r_lo_done")
        l_mm, l_done, l_tr, soft, soft_exp = sem("l_mm"), sem("l_done"), sem("l_tr"), sem("soft"), sem("soft_exp")
        routed_stored, stored = [sem("routed_stored0"), sem("routed_stored1")], sem("stored")
        block = ctx.enter_context(nc.Block())
        r_raw = u.w_raw[:, 0:KI * P].rearrange("p (k n) -> p k n", n=P)
        r_hi, r_lo = u.w_hi[1][:, 0:KI * P], u.w_lo[1][:, 0:KI * P]
        H = RT // 2

        def expert_units(eng, unit, begin=lambda e: None):
            unit(0, 0, 0, 0)
            unit(0, 1, 1, 1)
            with eng.Fori(1, HCH // 2) as i:
                for slot in range(2):
                    unit(0, 2 * i + slot, 2 * i + slot, slot)
            with eng.Fori(1, E) as e:
                begin(e)
                with eng.Fori(0, HCH // 2) as i:
                    for slot in range(2):
                        unit(e, 2 * i + slot, e * HCH + 2 * i + slot, slot)

        def gate_units(eng, unit, first=0):
            for k in range(first, 2):
                unit(k, EU + k, k)
            with eng.Fori(1, GU // 2) as i:
                for slot in range(2):
                    unit(2 * i + slot, 2 * i + slot + EU, slot)

        def chunk(k):
            return bass.ds(k * P, P)

        @block.sync
        def _(sp):
            for g in range(NG):
                rows = slice(g * GROUP, (g + 1) * GROUP)
                for part, name in ((u.x_hi, "comb_hi"), (u.x_lo, "comb_lo")):
                    sp.dma_start(part[:, :, rows].bitcast(FP32), dram[name][:, :, rows].rearrange("k p r -> p k r")).then_inc(x_loaded[g], 16)
                    if g == 0 and part is u.x_hi:
                        sp.wait_ge(r_zeroed, 1)
                        sp.dma_start(r_raw[:, :, 0:E], dram["router_W"][0:2 * D, :].rearrange("(k p) n -> p k n", p=P)).then_inc(r_loaded, 16)
                if g == 0:
                    sp.wait_ge(r_lo_done, 1)
                    u.load(sp, 0, dram["e_w1"][0, 0:2 * D, 0:P], dram["e_w2"][0, 0:P, :])
            for e in range(E):
                sp.dma_start(b2[:, e, :], dram["e_b2"][e].partition_broadcast(P)).then_inc(b2_loaded, 16)
            sp.dma_start(b2[:, E, :], dram["gate_b2"].partition_broadcast(P)).then_inc(b2_loaded, 16)
            expert_units(sp, lambda e, k, n, slot: None if isinstance(n, int) and n == 0 else
                         u.load(sp, n, dram["e_w1"][e, 0:2 * D, chunk(k)], dram["e_w2"][e, chunk(k), :]))
            gate = lambda k, n, slot: u.load(sp, n, dram["gate_w1"][0:2 * D, chunk(k)], dram["gate_w2"][chunk(k), :])
            gate(0, EU, 0)
            for h in range(2):
                tiles = slice(h * H, (h + 1) * H)
                sp.wait_ge(u.y_done, RT * (EU - 1) + H * (h + 1))
                sp.dma_start(dram["routed"].rearrange("(i p) d -> p i d", p=P)[:, tiles, :], u.acc[:, tiles, :]).then_inc(routed_stored[h], 16)
            gate_units(sp, gate, first=1)
            for h in range(2):
                tiles = slice(h * H, (h + 1) * H)
                sp.wait_ge(u.y_done, RT * (EU + GU - 1) + H * (h + 1))
                sp.dma_start(dram["gate"].rearrange("(i p) d -> p i d", p=P)[:, tiles, :], u.acc[:, tiles, :]).then_inc(stored, 16)
            sp.wait_ge(stored, 32)

        @block.gpsimd
        def _(pool):
            nc.gpsimd.memset(r_raw, 0.0).then_inc(r_zeroed, 1)
            pool.wait_ge(r_hi_done, 1)
            nc.gpsimd.tensor_tensor(r_lo, u.w_raw[:, 0:KI * P], r_hi.bitcast(FP32), ALU.subtract).then_inc(r_lo_done, 1)
            expert_units(pool, lambda e, k, n, slot: u.split_lo(pool, n, slot))
            gate_units(pool, lambda k, n, slot: u.split_lo(pool, n, slot))

        @block.scalar
        def _(act):
            act.wait_ge(r_loaded, 16)
            nc.scalar.activation(r_hi, u.w_raw[:, 0:KI * P], ACT.Copy).then_inc(r_hi_done, 1)
            for g in range(NG):
                act.wait_ge(l_mm, g + 1)
                for j in range(2):
                    last = nc.scalar.activation(logits[:, g * GROUP + j * T:g * GROUP + (j + 1) * T], u.ps_h[:E, g, j * T:(j + 1) * T], ACT.Identity,
                                                bias=const["router_anchor"][:, 2 * g + j:2 * g + j + 1])
                last.then_inc(l_done, 1)
                if g == 0:
                    u.split_hi(act, 0, 0)
            act.wait_ge(soft, 2)
            nc.scalar.activation(prob[:, :, :], prob[:, :, :], ACT.Exp).then_inc(soft_exp, 1)

            def expert(e, k, n, slot):
                if not isinstance(n, int) or n > 0:
                    u.split_hi(act, n, slot)
                for g in range(NG):
                    u.activate(act, n, ACT.Silu, lambda b: anchor[:, bass.ds(e * HCH + k, 1), b], g)

            def gate(k, n, slot):
                u.split_hi(act, n, slot)
                for g in range(NG):
                    u.activate(act, n, ACT.Silu, lambda b: anchor[:, bass.ds(k + EU, 1), b], g)

            expert_units(act, expert)
            gate_units(act, gate)

        @block.vector
        def _(dve):
            dve.wait_ge(l_tr, 1)
            raw = u.ps_y[:, 0, 0:4 * RT].rearrange("p (i e) -> p i e", e=4)[:, :, 0:E]
            wide = lambda v: v.unsqueeze(2).to_broadcast([P, RT, E])
            nc.vector.tensor_reduce(top[:, :], raw, AX.X, ALU.max).then_inc(soft, 1)
            dve.wait_ge(soft, 1)
            nc.vector.tensor_tensor(prob[:, :, :], raw, wide(top[:, :]), ALU.subtract).then_inc(soft, 1)
            dve.wait_ge(soft_exp, 1)
            nc.vector.tensor_reduce(total[:, :], prob[:, :, :], AX.X, ALU.add).then_inc(soft, 1)
            dve.wait_ge(soft, 3)
            nc.vector.reciprocal(recip[:, :], total[:, :]).then_inc(soft, 1)
            dve.wait_ge(soft, 4)
            nc.vector.tensor_tensor(prob[:, :, :], prob[:, :, :], wide(recip[:, :]), ALU.mult).then_inc(soft, 1)
            dve.wait_ge(soft, 5)
            dve.wait_ge(b2_loaded, 16 * (E + 1))
            for g in range(NG):
                u.split_h(dve, 0, g)
            for i in range(RT):
                nc.vector.tensor_scalar(u.acc[:, i, :], b2[:, 0, :], prob[:, i, 0:1], None, ALU.mult).then_inc(u.acc_ready, 1)

            def add_bias(e):
                for i in range(RT):
                    dve.wait_ge(u.y_done, e * (HCH * RT) + (i + 1 - RT))
                    nc.vector.scalar_tensor_tensor(u.acc[:, i, :], b2[:, bass.ds(e, 1), :].rearrange("p e d -> p (e d)"), prob[:, i, bass.ds(e, 1)],
                                                   u.acc[:, i, :], ALU.mult, ALU.add).then_inc(u.acc_ready, 1)

            def expert(e, k, n, slot):
                for g in range(NG):
                    if not isinstance(n, int) or n > 0:
                        u.split_h(dve, n, g)
                dve.wait_ge(u.acc_ready, RT * e + RT)
                for i in range(RT):
                    w = prob[:, i, e:e + 1] if isinstance(e, int) else prob[:, i, bass.ds(e, 1)]
                    u.accumulate(dve, n, i, w, slot)

            def gate(k, n, slot):
                for g in range(NG):
                    u.split_h(dve, n, g)
                for i in range(RT):
                    u.accumulate(dve, n, i, 1.0, slot)

            expert_units(dve, expert, add_bias)
            for i in range(RT):
                dve.wait_ge(routed_stored[i // H], 16)
                nc.vector.tensor_copy(u.acc[:, i, :], b2[:, E, :]).then_inc(u.acc_ready, 1)
            dve.wait_ge(u.acc_ready, (E + 1) * RT)
            gate_units(dve, gate)

        @block.tensor
        def _(pe):
            pe.wait_ge(r_lo_done, 1)
            for g in range(NG):
                pe.wait_ge(x_loaded[g], 32)
                cols = slice(g * GROUP, (g + 1) * GROUP)
                for k in range(KI):
                    w = slice(k * P, (k + 1) * P)
                    last = three_passes(nc, u.ps_h[:, g, 0:GROUP], r_hi[:, w], r_lo[:, w], u.x_hi[:, k, cols],
                                        u.x_lo[:, k, cols], k == 0, k == KI - 1)
                last.then_inc(l_mm, 1)
            pe.wait_ge(l_done, NG)
            for i in range(RT):
                last = nc.tensor.transpose(u.ps_y[:, 0, 4 * i:4 * i + E], logits[:, i * P:(i + 1) * P], ident[:E, :E])
            last.then_inc(l_tr, 1)
            pe.wait_ge(soft, 2)
            expert_units(pe, lambda e, k, n, slot: u.multiply(pe, n, slot, slot))
            gate_units(pe, lambda k, n, slot: u.multiply(pe, n, slot, slot))


def residual(nc, dram, const):
    ident = const["ident"]
    rows_of = lambda name: dram[name].rearrange("(b j p) d -> b p j d", p=QT, j=2)
    with ExitStack() as ctx:
        sb = lambda name, shape, dt=FP32: ctx.enter_context(nc.sbuf_tensor("rs_" + name, shape, dt))
        sem = lambda name: ctx.enter_context(nc.semaphore("rs_" + name))
        w_raw = sb("w_raw", [P, KD, D])
        w_hi, w_lo = sb("w_hi", [P, KD, D], F32R), sb("w_lo", [P, KD, D], F32R)
        bias = sb("bias", [QT, D])
        routed = [sb(f"routed{i}", [QT, 2, D]) for i in range(2)]
        gate = [sb(f"gate{i}", [QT, 2, D]) for i in range(2)]
        x = [sb(f"x{i}", [QT, 2, D]) for i in range(2)]
        r_hi = [sb(f"r_hi{i}", [P, KD, T], F32R) for i in range(2)]
        r_lo = [sb(f"r_lo{i}", [P, KD, T], F32R) for i in range(2)]
        y = [sb(f"y{i}", [QT, 2, D]) for i in range(2)]
        ps_t = ctx.enter_context(nc.psum_tensor("rs_ps_t", [P, KD, 512], FP32))
        ps_m = ctx.enter_context(nc.psum_tensor("rs_ps_m", [P, 4, 512], FP32))
        w_loaded, bias_loaded, w_hi_done, w_split = sem("w_loaded"), sem("bias_loaded"), sem("w_hi_done"), sem("w_split")
        routed_loaded = [sem("routed_loaded0"), sem("routed_loaded1")]
        side_loaded = [sem("side_loaded0"), sem("side_loaded1")]
        tr_done, r_hi_done, r_lo_done, mm_done = sem("tr_done"), sem("r_hi_done"), sem("r_lo_done"), sem("mm_done")
        gate_done, y_done, gated, y_added, stored = sem("gate_done"), sem("y_done"), sem("gated"), sem("y_added"), [sem("stored0"), sem("stored1")]
        block = ctx.enter_context(nc.Block())

        def nth(b, par, n=16):
            return n * (b // 2 + 1) if isinstance(b, int) else n // 2 * (b - par) + n

        @block.sync
        def _(sp):
            def load_side(b, par):
                sp.dma_start(gate[par][:, :, :], rows_of("gate")[b, :, :, :]).then_inc(side_loaded[par], 16)
                sp.dma_start(x[par][:, :, :], rows_of("x0")[b, :, :, :]).then_inc(side_loaded[par], 16)

            sp.dma_start(w_raw[:, :, :], dram["out_w"].rearrange("(k p) n -> p k n", p=P)).then_inc(w_loaded, 16)
            load_side(0, 0)
            sp.dma_start(bias[:, :], dram["out_b"].partition_broadcast(QT)).then_inc(bias_loaded, 16)
            load_side(1, 1)

            def step(b, par, has_next, has_second):
                sp.wait_ge(y_added, b + 1)
                sp.dma_start(rows_of("x1")[b, :, :, :], y[par][:, :, :]).then_inc(stored[par], 16)
                if has_second:
                    load_side(b + 2, par)

            batches(sp, step)
            for s in stored:
                sp.wait_ge(s, 16 * B // 2)

        @block.scalar
        def _(act):
            def load_routed(b, par):
                act.dma_start(routed[par][:, :, :], rows_of("routed")[b, :, :, :]).then_inc(routed_loaded[par], 16)

            load_routed(0, 0)
            load_routed(1, 1)
            act.wait_ge(w_loaded, 16)
            nc.scalar.activation(w_hi[:, :, :], w_raw[:, :, :], ACT.Copy).then_inc(w_hi_done, 1)

            def step(b, par, has_next, has_second):
                for f in range(KD):
                    act.wait_ge(tr_done, KD * b + f + 1)
                    if f == 0 and (not isinstance(b, int) or b > 1):
                        act.wait_ge(mm_done, 2 * (b - 1))
                    nc.scalar.activation(r_hi[par][:, f, :], ps_t[:, f, 0:T], ACT.Copy).then_inc(r_hi_done, 1)
                if has_second:
                    load_routed(b + 2, par)
                act.wait_ge(side_loaded[par], nth(b, par, 32))
                nc.scalar.activation(gate[par][:, :, :], gate[par][:, :, :], ACT.Sigmoid).then_inc(gate_done, 1)

            batches(act, step)

        @block.vector
        def _(dve):
            dve.wait_ge(w_hi_done, 1)
            nc.vector.tensor_tensor(w_lo[:, :, :], w_raw[:, :, :], w_hi[:, :, :].bitcast(FP32), ALU.subtract).then_inc(w_split, 1)
            dve.wait_ge(bias_loaded, 16)

            def transposed(b, par):
                for f in range(KD):
                    dve.wait_ge(r_hi_done, KD * b + f + 1)
                    nc.vector.tensor_tensor(r_lo[par][:, f, :], ps_t[:, f, 0:T], r_hi[par][:, f, :].bitcast(FP32),
                                            ALU.subtract).then_inc(r_lo_done, 1)

            transposed(0, 0)

            def step(b, par, has_next, has_second):
                if has_next:
                    transposed(b + 1, 1 - par)
                if not isinstance(b, int) or b > 1:
                    dve.wait_ge(stored[par], nth(b, par) - 16)
                for q in range(2):
                    dve.wait_ge(mm_done, 2 * b + q + 1)
                    nc.vector.tensor_tensor(y[par][:, q, :], ps_m[:QT, 2 * par + q, :], bias[:, :], ALU.add).then_inc(y_done, 1)
                dve.wait_ge(y_done, 2 * (b + 1))
                dve.wait_ge(gate_done, b + 1)
                nc.vector.tensor_tensor(y[par][:, :, :], y[par][:, :, :], gate[par][:, :, :], ALU.mult).then_inc(gated, 1)

            batches(dve, step)

        @block.gpsimd
        def _(pool):
            def step(b, par, has_next, has_second):
                pool.wait_ge(gated, b + 1)
                pool.wait_ge(side_loaded[par], nth(b, par, 32))
                nc.gpsimd.tensor_tensor(y[par][:, :, :], y[par][:, :, :], x[par][:, :, :], ALU.add).then_inc(y_added, 1)

            batches(pool, step)

        @block.tensor
        def _(pe):
            def transposes(b, par):
                pe.wait_ge(routed_loaded[par], nth(b, par))
                for f in range(KD):
                    after_first(pe, b, r_lo_done, KD * (b - 1) + f + 1)
                    for j in range(2):
                        last = nc.tensor.transpose(ps_t[:, f, j * QT:(j + 1) * QT], routed[par][:, j, f * P:(f + 1) * P], ident[:QT, :QT])
                    last.then_inc(tr_done, 1)

            transposes(0, 0)
            pe.wait_ge(w_split, 1)

            def step(b, par, has_next, has_second):
                if has_next:
                    transposes(b + 1, 1 - par)
                pe.wait_ge(r_lo_done, KD * (b + 1))
                if not isinstance(b, int) or b > 1:
                    pe.wait_ge(y_done, 2 * (b - 1))
                for q in range(2):
                    for k in range(KD):
                        r = slice(q * QT, (q + 1) * QT)
                        last = three_passes(nc, ps_m[:QT, 2 * par + q, :], r_hi[par][:, k, r], r_lo[par][:, k, r],
                                            w_hi[:, k, :], w_lo[:, k, :], k == 0, k == KD - 1)
                    last.then_inc(mm_done, 1)

            batches(pe, step)


def attention1(nc, dram, const, tag, chunks, kc, halves, q_name, k_parts, v_of, v_bias, w_name, b_name, gate, source, target, lag, per_load, gap):
    ident = const["ident"]
    keys = chunks * kc
    HN = keys // halves
    HN_E = HN + HN % 2
    NS = 4 // halves
    NPB = 2 * NS
    FPT = max(1, chunks // 3)
    CPF = chunks // FPT
    HPB = P // HD
    GPB = NH // HPB
    TPB, TPGR = 2 * NH, 2 * HPB
    LPB = NH // per_load
    RECIP, WIDE, VALUES = gap, 2 * gap, 2 * gap + 1
    chunk_turn = lambda c: VALUES + min(c // gap, 4)
    DIVIDE = chunk_turn(chunks - 1) + 1
    SPLIT, PROJECT = DIVIDE + 1, DIVIDE + gap
    ADD = PROJECT + KD // gap
    STORE = 20
    TAIL = lag + STORE + 1
    RC = slice(256, 256 + T)
    rows_of = lambda name: dram[name].rearrange("(b j p) d -> b p j d", p=QT, j=2)
    with ExitStack() as ctx:
        sb = lambda name, shape, dt=FP32: ctx.enter_context(nc.sbuf_tensor(f"{tag}_{name}", shape, dt))
        sem = lambda name: ctx.enter_context(nc.semaphore(f"{tag}_{name}"))
        w_raw = sb("w_raw", [P, KD, D])
        w_hi, w_lo = sb("w_hi", [P, KD, D], F32R), sb("w_lo", [P, KD, D], F32R)
        b_out = sb("b_out", [QT, D])
        pick = sb("pick", [HPB, P])
        q4 = [sb(f"q4_{i}", [P, per_load, T], F32R) for i in range(2)]
        k4 = [sb(f"k4_{i}", [P, per_load, keys + 2], F32R) for i in range(2)]
        v = [sb(f"v{i}", [kc, chunks, D]) for i in range(2)]
        x = [sb(f"x{i}", [QT, 2, D]) for i in range(2)]
        factor = [sb(f"factor{i}", [QT, D]) for i in range(2)]
        neg_max = sb("neg_max", [QT, NPB])
        total, recip = sb("total", [QT, 2, 2, HPB]), sb("recip", [QT, 2, HPB])
        prob = sb("prob", [QT, NPB, keys])
        pt = [sb(f"pt{i}", [kc, HPB, chunks, T]) for i in range(2)]
        recip_t, recip_wide = sb("recip_t", [HPB, T]), sb("recip_wide", [P, T])
        a = sb("a", [P, T])
        a_hi, a_lo = sb("a_hi", [P, GPB, T], F32R), sb("a_lo", [P, GPB, T], F32R)
        y = sb("y", [QT, 2, D])
        ps_s = ctx.enter_context(nc.psum_tensor(tag + "_ps_s", [P, NS, halves, 512], FP32))
        ps_t = ctx.enter_context(nc.psum_tensor(tag + "_ps_t", [P, 2, 512], FP32))
        ps_o = ctx.enter_context(nc.psum_tensor(tag + "_ps_o", [P, 2, 512], FP32))
        w_loaded, w_hi_done, w_split, side_loaded = sem("w_loaded"), sem("w_hi_done"), sem("w_split"), [sem("side_loaded0"), sem("side_loaded1")]
        padded = sem("padded")
        bias_loaded, pick_done = sem("bias_loaded"), sem("pick_done")
        qk_loaded = [sem("qk_loaded0"), sem("qk_loaded1")]
        v_loaded = [sem("v_loaded0"), sem("v_loaded1")]
        s_done, max_done, exp_done, tr_done = sem("s_done"), sem("max_done"), sem("exp_done"), sem("tr_done")
        pt_done = [sem("pt_done_dve"), sem("pt_done_act")]
        recip_done, rt_done, rt_copied, wide_done, wide_copied = sem("recip_done"), sem("rt_done"), sem("rt_copied"), sem("wide_done"), sem("wide_copied")
        pv_done, a_done, a_hi_done, a_lo_done = sem("pv_done"), sem("a_done"), sem("a_hi_done"), sem("a_lo_done")
        y_mm, y_done, y_gated, y_added, stored = sem("y_mm"), sem("y_done"), sem("y_gated"), sem("y_added"), sem("stored")
        block = ctx.enter_context(nc.Block())

        def turns(eng, turn):
            for b in range(2):
                for t in range(TPB):
                    turn(b, b, t)
            with eng.Fori(1, B // 2) as i:
                for par in range(2):
                    for t in range(TPB):
                        turn(2 * i + par, par, t)
            for t in range(TPB, TPB + TAIL):
                turn(B - 1, 1, t)

        def exists(b, t):
            return not isinstance(b, int) or 0 <= TPB * b + t < TPB * B

        def group_at(b, t, behind):
            last = t - lag - behind
            return last // TPGR if last % TPGR == TPGR - 1 and exists(b, last) else None

        def batch_at(b, t, behind):
            g = group_at(b, t, behind)
            return g // GPB if g is not None and g % GPB == GPB - 1 else None

        def wait(eng, s, b, per_batch, more):
            if not isinstance(b, int) or per_batch * b + more > 0:
                eng.wait_ge(s, per_batch * b + more)

        def every_second(b, par, n):
            return n * (b // 2 + 1) if isinstance(b, int) else n // 2 * (b - par) + n

        @block.sync
        def _(sp):
            def step(b, par):
                rows, keys_of = bass.ds(T * b, T), [k_parts(part, b) for part in range(2)]
                for n in range(LPB):
                    wait(sp, s_done, b, TPB, 2 * per_load * (n - 1))
                    if n == 0:
                        if not isinstance(b, int) or b > 1:
                            sp.wait_ge(pv_done, GPB * b - GPB)
                        if not isinstance(b, int) or b > 0:
                            sp.dma_start(v[par][:, :, :], v_of(b)).then_inc(v_loaded[par], 16)
                    side = (LPB * par + n) % 2
                    for strip in range(4):
                        part = slice(strip * HD, (strip + 1) * HD)
                        heads = slice(n * per_load * HD, (n + 1) * per_load * HD)
                        q = dram[q_name + ("_hi", "_lo")[strip % 2]].rearrange("k p r -> (k p) r")[heads, rows]
                        k = keys_of[strip // 2][heads, :]
                        sp.dma_start(q4[side][part, :, :].bitcast(FP32), q.rearrange("(h d) r -> d h r", d=HD)).then_inc(qk_loaded[side], 16)
                        sp.dma_start(k4[side][part, :, 0:keys].bitcast(FP32), k.rearrange("(h d) s -> d h s", d=HD)).then_inc(qk_loaded[side], 16)
                    if n == 0:
                        if isinstance(b, int) and b == 0:
                            sp.dma_start(v[par][:, :, :], v_of(b)).then_inc(v_loaded[par], 16)
                        if not isinstance(b, int) or b > 1:
                            sp.wait_ge(y_added, b - 1)
                        sp.dma_start(x[par][:, :, :], rows_of(source)[b, :, :, :]).then_inc(side_loaded[par], 16)
                        if gate is not None:
                            sp.dma_start(factor[par][:, :], dram["gates"][b, gate, :].partition_broadcast(QT)).then_inc(side_loaded[par], 16)
                    if isinstance(b, int) and b == 0 and n == min(1, LPB - 1):
                        sp.dma_start(w_raw[:, :, :], dram[w_name].rearrange("(k p) n -> p k n", p=P)).then_inc(w_loaded, 16)
                        sp.dma_start(b_out[:, :], dram[b_name].partition_broadcast(QT)).then_inc(bias_loaded, 16)

            step(0, 0)
            step(1, 1)
            with sp.Fori(1, B // 2) as i:
                step(2 * i, 0)
                step(2 * i + 1, 1)
            sp.wait_ge(stored, 16 * B)

        @block.gpsimd
        def _(pool):
            nc.gpsimd.memset(pick[:, :], 1.0).then_inc(pick_done, 1)
            for t in k4:
                nc.gpsimd.memset(t[:, :, keys:].bitcast(FP32), 0.0).then_inc(padded, 1)
            pool.wait_ge(pick_done, 1)
            nc.gpsimd.affine_select(out=pick[:, :], in_=pick[:, :], compare_op=ALU.is_ge, fill=0.0, base=0,
                                    pattern=[[1, P]], channel_multiplier=-HD).then_inc(pick_done, 1)
            pool.wait_ge(pick_done, 2)
            nc.gpsimd.affine_select(out=pick[:, :], in_=pick[:, :], compare_op=ALU.is_ge, fill=0.0, base=HD - 1,
                                    pattern=[[-1, P]], channel_multiplier=HD).then_inc(pick_done, 1)

            def turn(b, par, t):
                ago = batch_at(b, t, ADD + KD // gap)
                if ago is not None:
                    done, side = b + ago + 1, (par + ago) % 2
                    n_side = 32 if gate is not None else 16
                    pool.wait_ge(y_done, 2 * done)
                    pool.wait_ge(side_loaded[side], every_second(b + ago, side, n_side))
                    if gate is not None:
                        nc.gpsimd.tensor_tensor(y[:, :, :], y[:, :, :], factor[side][:, :].unsqueeze(1).to_broadcast([QT, 2, D]),
                                                ALU.mult).then_inc(y_gated, 1)
                        pool.wait_ge(y_gated, done)
                    nc.gpsimd.tensor_tensor(y[:, :, :], y[:, :, :], x[side][:, :, :], ALU.add).then_inc(y_added, 1)

            turns(pool, turn)

        def filled(b, t, f):
            n = FPT * t + f
            return n % 2, n // 2 + 1

        def empty(eng, own, b, t):
            for f in range(FPT):
                which, _ = filled(b, t, f)
                if which != own:
                    continue
                eng.wait_ge(tr_done, FPT * TPB * b + FPT * t + f + 1)
                group, h, q = t // TPGR, t // 2, t % 2
                wait(eng, pv_done, b, GPB, group - 1)
                out = pt[group % 2][:, h % HPB, CPF * f:CPF * (f + 1), q * QT:(q + 1) * QT]
                src = ps_t[:kc, own, 0:CPF * QT].rearrange("p (c r) -> p c r", c=CPF)
                if own == 0:
                    nc.vector.tensor_copy(out, src).then_inc(pt_done[0], 1)
                else:
                    nc.scalar.activation(out, src, ACT.Copy).then_inc(pt_done[1], 1)

        @block.vector
        def _(dve):
            def turn(b, par, t):
                for q in range(2):
                    ago = batch_at(b, t, ADD + q * KD // gap)
                    if ago is not None:
                        if q == 0:
                            wait(dve, stored, b + ago, 16, 0)
                        dve.wait_ge(y_mm, 2 * (b + ago) + q + 1)
                        nc.vector.tensor_tensor(y[:, q, :], ps_o[:QT, 1, :], b_out[:, :], ALU.add).then_inc(y_done, 1)
                if t < TPB:
                    dve.wait_ge(s_done, TPB * b + t + 1)
                    wait(dve, exp_done, b, TPB, t + 1 - NPB)
                    nc.vector.tensor_reduce(neg_max[:, t % NPB:t % NPB + 1], ps_s[:QT, t % NS, :, 0:HN], AX.XY, ALU.max,
                                            negate=True).then_inc(max_done, 1)
                if exists(b, t - lag):
                    empty(dve, 0, b, t - lag)
                g = group_at(b, t, 0)
                if g is not None:
                    dve.wait_ge(exp_done, TPB * b + TPGR * (g + 1))
                    wait(dve, rt_done, b, GPB, g)
                    nc.vector.reciprocal(recip[:, :, :], total[:, g % 2, :, :]).then_inc(recip_done, 1)
                g = group_at(b, t, DIVIDE)
                if g is not None:
                    dve.wait_ge(pv_done, GPB * b + g + 1)
                    dve.wait_ge(wide_copied, GPB * b + g + 1)
                    wait(dve, a_lo_done, b, GPB, g)
                    nc.vector.tensor_tensor(a[:, :], ps_o[:, 0, 0:T], recip_wide[:, :], ALU.mult).then_inc(a_done, 1)
                g = group_at(b, t, SPLIT)
                if g is not None:
                    dve.wait_ge(a_hi_done, GPB * b + g + 1)
                    nc.vector.scalar_tensor_tensor(a_lo[:, g % GPB, :], a[:, :], v_bias[:, g % GPB:g % GPB + 1],
                                                   a_hi[:, g % GPB, :].bitcast(FP32), ALU.add, ALU.subtract).then_inc(a_lo_done, 1)
                if isinstance(b, int) and b == 0 and t == NH:
                    dve.wait_ge(w_hi_done, 1)
                    nc.vector.tensor_tensor(w_lo[:, :, :], w_raw[:, :, :], w_hi[:, :, :].bitcast(FP32), ALU.subtract).then_inc(w_split, 1)
                    dve.wait_ge(bias_loaded, 16)

            turns(dve, turn)

        @block.scalar
        def _(act):
            def turn(b, par, t):
                if exists(b, t - lag):
                    empty(act, 1, b, t - lag)
                if t < TPB:
                    g = t // TPGR
                    act.wait_ge(max_done, TPB * b + t + 1)
                    wait(act, tr_done, b, FPT * TPB, FPT * (t + 1 - NPB))
                    if t % TPGR == 0:
                        wait(act, recip_done, b, GPB, g - 1)
                    nc.scalar.activation(prob[:, t % NPB, :].rearrange("p (h s) -> p h s", h=halves),
                                         ps_s[:QT, t % NS, :, 0:HN], ACT.Exp, bias=neg_max[:, t % NPB:t % NPB + 1],
                                         accum_out=total[:, g % 2, t % 2, t // 2 % HPB:t // 2 % HPB + 1]).then_inc(exp_done, 1)
                g = group_at(b, t, RECIP)
                if g is not None:
                    act.wait_ge(rt_done, GPB * b + g + 1)
                    nc.scalar.activation(recip_t[:, :], ps_o[:HPB, 0, RC], ACT.Copy).then_inc(rt_copied, 1)
                g = group_at(b, t, WIDE)
                if g is not None:
                    act.wait_ge(wide_done, GPB * b + g + 1)
                    wait(act, a_done, b, GPB, g)
                    nc.scalar.activation(recip_wide[:, :], ps_o[:, 0, RC], ACT.Copy).then_inc(wide_copied, 1)
                g = group_at(b, t, DIVIDE)
                if g is not None:
                    act.wait_ge(a_done, GPB * b + g + 1)
                    wait(act, y_mm, b + g // GPB, 2, 0)
                    nc.scalar.activation(a_hi[:, g % GPB, :], a[:, :], ACT.Identity, bias=v_bias[:, g % GPB:g % GPB + 1]).then_inc(a_hi_done, 1)
                ago = batch_at(b, t, STORE)
                if ago is not None:
                    act.wait_ge(y_added, b + ago + 1)
                    act.dma_start(rows_of(target)[b + ago, :, :, :], y[:, :, :]).then_inc(stored, 16)
                if isinstance(b, int) and b == 0 and t == NH:
                    act.wait_ge(w_loaded, 16)
                    nc.scalar.activation(w_hi[:, :, :], w_raw[:, :, :], ACT.Copy).then_inc(w_hi_done, 1)

            turns(act, turn)

        @block.tensor
        def _(pe):
            pe.wait_ge(pick_done, 3)
            pe.wait_ge(padded, 2)

            def turn(b, par, t):
                if t < TPB:
                    h, q = t // 2, t % 2
                    n, j = h // per_load, h % per_load
                    side = (LPB * par + n) % 2
                    if j == q == 0:
                        pe.wait_ge(qk_loaded[side], every_second(b, par, 128) if LPB == 1 else 128 * (LPB // 2) * b + 128 * (n // 2 + 1))
                    wait(pe, exp_done, b, TPB, t + 1 - NS)
                    for half in range(halves):
                        last = nc.tensor.matmul(ps_s[:QT, t % NS, half, 0:HN_E], q4[side][:, j, q * QT:(q + 1) * QT],
                                                k4[side][:, j, half * HN:half * HN + HN_E], start=True, stop=True)
                    last.then_inc(s_done, 1)
                old = t - lag
                if exists(b, old):
                    for f in range(FPT):
                        which, nth = filled(b, old, f)
                        wait(pe, pt_done[which], b, FPT * TPB // 2, nth - 1)
                        if f == 0:
                            wait(pe, exp_done, b, TPB, old + 1)
                        for c in range(CPF):
                            chunk = slice((CPF * f + c) * kc, (CPF * f + c + 1) * kc)
                            last = nc.tensor.transpose(ps_t[:kc, which, c * QT:(c + 1) * QT], prob[:, old % NPB, chunk],
                                                       ident[:QT, :QT])
                        last.then_inc(tr_done, 1)
                g = group_at(b, t, RECIP)
                if g is not None:
                    pe.wait_ge(recip_done, GPB * b + g + 1)
                    wait(pe, a_done, b, GPB, g)
                    for q in range(2):
                        last = nc.tensor.transpose(ps_o[:HPB, 0, RC.start + q * QT:RC.start + (q + 1) * QT], recip[:, q, :], ident[:QT, :QT])
                    last.then_inc(rt_done, 1)
                g = group_at(b, t, WIDE)
                if g is not None:
                    pe.wait_ge(rt_copied, GPB * b + g + 1)
                    nc.tensor.matmul(ps_o[:, 0, RC], pick[:, :], recip_t[:, :], start=True, stop=True).then_inc(wide_done, 1)
                for c in range(chunks):
                    g = group_at(b, t, chunk_turn(c))
                    if g is None:
                        continue
                    side = (par + g // GPB) % 2
                    if c == 0:
                        pe.wait_ge(wide_copied, GPB * b + g + 1)
                        for which in range(2):
                            pe.wait_ge(pt_done[which], FPT * TPB // 2 * b + FPT * HPB * (g + 1))
                        if g % GPB == 0:
                            pe.wait_ge(v_loaded[side], every_second(b + g // GPB, side, 16))
                    for j in range(HPB):
                        cols = slice((g % GPB * HPB + j) * HD, (g % GPB * HPB + j + 1) * HD)
                        last = nc.tensor.matmul(ps_o[j * HD:(j + 1) * HD, 0, 0:T], v[side][:, c, cols], pt[g % 2][:, j, c, :],
                                                start=c == 0, stop=c == chunks - 1)
                    if c == chunks - 1:
                        last.then_inc(pv_done, 1)
                for q in range(2):
                    for k in range(KD):
                        ago = batch_at(b, t, PROJECT + (q * KD + k) // gap)
                        if ago is None:
                            continue
                        if q == k == 0:
                            pe.wait_ge(a_lo_done, GPB * (b + ago + 1))
                            if isinstance(b, int):
                                pe.wait_ge(w_split, 1)
                        if k == 0:
                            wait(pe, y_done, b + ago, 2, q)
                        r = slice(q * QT, (q + 1) * QT)
                        last = three_passes(nc, ps_o[:QT, 1, :], a_hi[:, k, r], a_lo[:, k, r], w_hi[:, k, :], w_lo[:, k, :],
                                            k == 0, k == KD - 1)
                        if k == KD - 1:
                            last.then_inc(y_mm, 1)

            turns(pe, turn)


def self_attention(nc, dram, const):
    keys = lambda part, b: dram[("k_hi", "k_lo")[part]].rearrange("k p r -> (k p) r")[:, bass.ds(T * b, T)]
    values = lambda b: dram["v_s"][bass.ds(T * b, T), :].rearrange("(c p) d -> p c d", p=QT)
    attention1(nc, dram, const, "sa", 2, QT, 1, "q", keys, values, const["vecs"]["b_qkv"][:, 2 * KD:3 * KD], "W_proj", "b_proj",
               0, "x1", "x2", 3, NH // 2, 2)


def cross_attention(nc, dram, const):
    keys = lambda part, b: dram[("kT_hi", "kT_lo")[part]][b, :, :]
    attention1(nc, dram, const, "ca", KCH, KC, 2, "qc", keys, lambda b: dram["v_c"][b, :, :, :],
               const["vecs"]["b_kvc"][:, KD:2 * KD], "W_cproj", "b_cproj", None, "x2", "x3", 2, P // HD, 1)


def mlp(nc, dram, const):
    ident, mod = const["ident"], const["mod"]
    NU = MLP // P
    N_SIDE = 1 + RT + sum(T * b % P > 0 for b in range(B))
    x_view = dram["x3"].rearrange("(b j p) d -> b p j d", p=QT, j=2)
    by_tile = lambda name: dram[name].rearrange("(i p) d -> p i d", p=P)
    with ExitStack() as ctx:
        sb = lambda name, shape, dt=FP32: ctx.enter_context(nc.sbuf_tensor("ml_" + name, shape, dt))
        sem = lambda name: ctx.enter_context(nc.semaphore("ml_" + name))
        u = HiddenUnits(nc, ctx, "ml", KD)
        raw = [sb(f"raw{i}", [QT, 2, D]) for i in range(2)]
        xn = [sb(f"xn{i}", [QT, 2, D]) for i in range(2)]
        stats, moments = sb("stats", [QT, 2, 6]), sb("moments", [QT, 2, 2])
        rstd, power, eps_tile = sb("rstd", [QT, 2]), sb("power", [QT, 2]), sb("eps_tile", [QT, 2])
        spare = sb("spare", [QT, 1])
        xt = sb("xt", [P, KD, T])
        b2 = sb("b2", [P, D])
        bias = sb("bias", [P, 2])
        x3 = sb("x3", [P, RT, D])
        factor = sb("factor", [P, RT, D])
        raw_loaded = [sem("raw_loaded0"), sem("raw_loaded1")]
        stats_done, aggr_done, rstd_add, rstd_done = sem("stats_done"), sem("aggr_done"), sem("rstd_add"), sem("rstd_done")
        xn_done, tr_done, xt_done, xt_hi_done, xt_lo_done = sem("xn_done"), sem("tr_done"), sem("xt_done"), sem("xt_hi_done"), sem("xt_lo_done")
        bias_done = sem("bias_done")
        side_loaded, b2_loaded, scaled, summed, stored = sem("side_loaded"), sem("b2_loaded"), sem("scaled"), sem("summed"), sem("stored")
        block = ctx.enter_context(nc.Block())

        def units(eng, unit):
            unit(0, 0)
            unit(1, 1)
            with eng.Fori(1, NU // 2) as i:
                for slot in range(2):
                    unit(2 * i + slot, slot)

        @block.sync
        def _(sp):
            def load(b, par):
                sp.dma_start(raw[par][:, :, :], x_view[b, :, :, :]).then_inc(raw_loaded[par], 16)

            weights = lambda n, slot: u.load(sp, n, dram["W_mlp1"][:, bass.ds(n * P, P)], dram["W_mlp2"][bass.ds(n * P, P), :])
            load(0, 0)
            load(1, 1)
            weights(0, 0)
            sp.dma_start(b2[:, :], dram["b_mlp2"].partition_broadcast(P)).then_inc(b2_loaded, 16)

            def step(b, par, has_next, has_second):
                if has_second:
                    sp.wait_ge(xn_done, 2 * (b + 1))
                    load(b + 2, par)

            batches(sp, step)
            n_side = 1
            sp.dma_start(x3[:, :, :], by_tile("x3")).then_inc(side_loaded, 16)
            for i in range(RT):
                at = i * P
                while at < (i + 1) * P:
                    b = at // T
                    end = min((i + 1) * P, (b + 1) * T)
                    sp.dma_start(factor[at - i * P:end - i * P, i, :], dram["gates"][b, 1, :].partition_broadcast(end - at)).then_inc(side_loaded, 16)
                    n_side += 1
                    at = end
            assert n_side == N_SIDE
            units(sp, lambda n, slot: None if isinstance(n, int) and n == 0 else weights(n, slot))
            for i in range(RT):
                sp.wait_ge(summed, i + 1)
                sp.dma_start(by_tile("y")[:, i, :], u.acc[:, i, :]).then_inc(stored, 16)
            sp.wait_ge(stored, 16 * RT)

        @block.gpsimd
        def _(pool):
            nc.gpsimd.memset(power[:, :], -0.5).then_inc(rstd_add, 1)
            nc.gpsimd.memset(eps_tile[:, :], EPS1).then_inc(rstd_add, 1)
            pool.wait_ge(rstd_add, 2)

            def step(b):
                pool.wait_ge(aggr_done, b + 1)
                after_first(pool, b, xn_done, 2 * b)
                nc.gpsimd.tensor_tensor(rstd[:, :], moments[:, :, 1], eps_tile[:, :], ALU.add).then_inc(rstd_add, 1)
                pool.wait_ge(rstd_add, b + 3)
                nc.gpsimd.tensor_tensor(rstd[:, :], rstd[:, :], power[:, :], ALU.pow).then_inc(rstd_done, 1)

            step(0)
            u.split_lo(pool, 0, 0)
            with pool.Fori(1, B) as b:
                step(b)
            units(pool, lambda n, slot: None if isinstance(n, int) and n == 0 else u.split_lo(pool, n, slot))

        @block.vector
        def _(dve):
            def statistics(b, par):
                dve.wait_ge(raw_loaded[par], 16 * (b // 2) + 16 if isinstance(b, int) else 8 * (b - par) + 16)
                after_first(dve, b, rstd_done, b)
                for j in range(2):
                    nc.vector.bn_stats(stats[:, j, :], raw[par][:, j, :]).then_inc(stats_done, 1)
                dve.wait_ge(stats_done, 2 * (b + 1))
                after_first(dve, b, xn_done, 2 * b)
                nc.vector.memset(spare[:, :], 0.0)
                for j in range(2):
                    last = nc.vector.bn_aggr(moments[:, j, :], stats[:, j, :])
                last.then_inc(aggr_done, 1)

            def normalise(b, par):
                dve.wait_ge(rstd_done, b + 1)
                if not isinstance(b, int) or b > 1:
                    dve.wait_ge(tr_done, KD * (b - 1))
                for j in range(2):
                    nc.vector.tensor_scalar(xn[par][:, j, :], raw[par][:, j, :], moments[:, j, 0:1], rstd[:, j:j + 1],
                                            ALU.subtract, ALU.mult).then_inc(xn_done, 1)

            def step(b, par, has_next, has_second):
                cols = bass.ds(T * b, T)
                for f in range(KD):
                    dve.wait_ge(xt_done, KD * b + f + 1)
                    nc.vector.tensor_copy(u.x_hi[:, f, cols], xt[:, f, :]).then_inc(xt_hi_done, 1)
                    dve.wait_ge(xt_hi_done, KD * b + f + 1)
                    nc.vector.tensor_tensor(u.x_lo[:, f, cols], xt[:, f, :], u.x_hi[:, f, cols].bitcast(FP32),
                                            ALU.subtract).then_inc(xt_lo_done, 1)
                    if has_second and f == 0:
                        statistics(b + 2, par)
                    if has_second and f == 2:
                        normalise(b + 2, par)

            for b in range(2):
                statistics(b, b)
                normalise(b, b)
            batches(dve, step)
            dve.wait_ge(b2_loaded, 16)
            for g in range(NG):
                u.split_h(dve, 0, g)
            for i in range(RT):
                nc.vector.tensor_copy(u.acc[:, i, :], b2[:, :]).then_inc(u.acc_ready, 1)
            dve.wait_ge(u.acc_ready, RT)

            def unit(n, slot):
                for g in range(NG):
                    if not isinstance(n, int) or n > 0:
                        u.split_h(dve, n, g)
                for i in range(RT):
                    u.accumulate(dve, n, i, 1.0, slot)

            units(dve, unit)
            dve.wait_ge(side_loaded, 16 * N_SIDE)
            for i in range(RT):
                dve.wait_ge(u.y_done, RT * (NU - 1) + i + 1)
                nc.vector.tensor_tensor(u.acc[:, i, :], u.acc[:, i, :], factor[:, i, :], ALU.mult).then_inc(scaled, 1)
                dve.wait_ge(scaled, i + 1)
                nc.vector.tensor_tensor(u.acc[:, i, :], u.acc[:, i, :], x3[:, i, :], ALU.add).then_inc(summed, 1)

        @block.scalar
        def _(act):
            def transposed(b, f):
                act.wait_ge(tr_done, KD * b + f + 1)
                after_first(act, b, xt_lo_done, KD * (b - 1) + f + 1)
                one = bass.ds(b, 1)
                nc.scalar.activation(xt[:, f, :], u.ps_y[:, f, 0:T], ACT.Identity, bias=mod[:, 3 * KD + f, one],
                                     scale=mod[:, 4 * KD + f, one]).then_inc(xt_done, 1)

            for f in range(KD):
                transposed(0, f)
            u.split_hi(act, 0, 0)
            with act.Fori(1, B) as b:
                for f in range(KD):
                    transposed(b, f)

            def unit(n, slot):
                if not isinstance(n, int) or n > 0:
                    u.split_hi(act, n, slot)
                nc.scalar.activation(bias[:, slot:slot + 1], const["vecs"]["b_mlp1"][:, bass.ds(n, 1)], ACT.Copy).then_inc(bias_done, 1)
                act.wait_ge(bias_done, n + 1)
                for g in range(NG):
                    u.activate(act, n, ACT.Gelu_apprx_tanh, lambda b: bias[:, slot:slot + 1], g)

            units(act, unit)

        @block.tensor
        def _(pe):
            def transposes(b, par):
                pe.wait_ge(xn_done, 2 * (b + 1))
                for f in range(KD):
                    after_first(pe, b, xt_done, KD * (b - 1) + f + 1)
                    for j in range(2):
                        last = nc.tensor.transpose(u.ps_y[:, f, j * QT:(j + 1) * QT], xn[par][:, j, f * P:(f + 1) * P], ident[:QT, :QT])
                    last.then_inc(tr_done, 1)

            def x_ready(g):
                for par in range(2):
                    if g + 1 < NG:
                        transposes(2 * (g + 1) + par, par)
                pe.wait_ge(xt_lo_done, KD * 2 * (g + 1))

            for par in range(2):
                transposes(par, par)

            units(pe, lambda n, slot: u.multiply(pe, n, slot, slot, x_ready if isinstance(n, int) and n == 0 else None))


STAGES = [conditioning, context_kv, project_scores0, attention0, mixture, residual, project_qkv, self_attention,
          project_qc, cross_attention, mlp]


VECS = 100


def program(nc, io, out, stages=None):
    dram = dict(io)
    dram["out"] = out

    def scratch(name, shape, dt=FP32):
        dram[name] = nc.dram_tensor(name, shape, dt, kind="Internal").ap()

    for name in ("b_mod", "e_b1", "gate_b1", "ln_gamma", "ln_beta", "b_qkv", "b_qc", "b_kvc", "b_mlp1"):
        v = dram[name]
        dram["rows_" + name] = v.rearrange("e (k p) -> (e k) p", p=P) if name == "e_b1" else v.rearrange("(k p) -> k p", p=P)
    scratch("W_qk", (D, D))
    scratch("gates", (B, 2, D))
    for name in ("comb_hi", "comb_lo"):
        scratch(name, (2 * KD, P, R))
    for name in ("u_hi", "u_lo", "q_hi", "q_lo", "k_hi", "k_lo", "qc_hi", "qc_lo"):
        scratch(name, (KD, P, R))
    scratch("v_s", (R, D))
    scratch("routed", (R, D))
    scratch("gate", (R, D))
    for name in ("x1", "x2", "x3"):
        scratch(name, (R, D))
    scratch("kT_hi", (B, D, S))
    scratch("kT_lo", (B, D, S))
    scratch("v_c", (B, KC, KCH, D))
    dram["x0"] = dram["x"].rearrange("b t d -> (b t) d")
    dram["y"] = out.rearrange("b t d -> (b t) d")
    with ExitStack() as ctx:
        sb = lambda name, shape, dt=FP32: ctx.enter_context(nc.sbuf_tensor(name, shape, dt))
        const = {
            "ident": sb("ident", [P, P]),
            "mod": sb("mod", [P, 6 * KD, B]),
            "anchor": sb("anchor", [P, E * HCH + KD, B]),
            "router_anchor": sb("router_anchor", [E, B]),
        }
        columns = sb("columns", [P, VECS])
        vecs = {"all": columns, "hidden": columns[:, 24:52]}
        at = 0
        for name, k in (("b_mod", 24), ("e_b1", 24), ("gate_b1", 4), ("ln_gamma", 4), ("ln_beta", 4), ("b_qkv", 12),
                        ("b_qc", 4), ("b_kvc", 8), ("b_mlp1", 16)):
            vecs[name] = columns[:, at:at + k]
            at += k
        const["vecs"] = vecs
        for stage in STAGES if stages is None else stages:
            if stage is project_qkv:
                used = list(nc.released_uncleared_semaphores)
                nc.gpsimd.sem_clear(range(min(used), max(used) + 1))
                nc.all_engine_barrier()
            stage(nc, dram, const)


NAMES = {
    "x": "x", "cond": "cond_1024", "ctx": "ctx_1024", "ln_gamma": "L0_xcond_ln_gamma", "ln_beta": "L0_xcond_ln_beta",
    "Wq": "L0_xcond_Wq", "Wk": "L0_xcond_Wk", "Wv": "L0_xcond_Wv", "router_W": "L0_xcond_router_W",
    "router_b": "L0_xcond_router_b", "e_w1": "L0_xcond_e_w1", "e_b1": "L0_xcond_e_b1", "e_w2": "L0_xcond_e_w2",
    "e_b2": "L0_xcond_e_b2", "gate_w1": "L0_xcond_gate_w1", "gate_b1": "L0_xcond_gate_b1",
    "gate_w2": "L0_xcond_gate_w2", "gate_b2": "L0_xcond_gate_b2", "out_w": "L0_xcond_out_w",
    "out_b": "L0_xcond_out_b", "W_mod": "L1_xcond_W_mod", "b_mod": "L1_xcond_b_mod", "W_qkv": "L1_xcond_W_qkv",
    "b_qkv": "L1_xcond_b_qkv", "W_proj": "L1_xcond_W_proj", "b_proj": "L1_xcond_b_proj", "W_qc": "L1_xcond_W_qc",
    "b_qc": "L1_xcond_b_qc", "W_kvc": "L1_xcond_W_kvc", "b_kvc": "L1_xcond_b_kvc", "W_cproj": "L1_xcond_W_cproj",
    "b_cproj": "L1_xcond_b_cproj", "W_mlp1": "L1_xcond_W_mlp1", "b_mlp1": "L1_xcond_b_mlp1",
    "W_mlp2": "L1_xcond_W_mlp2", "b_mlp2": "L1_xcond_b_mlp2",
}


def kernel(**inputs):
    import numpy as np
    import concourse.bacc as bacc
    from concourse.bass_utils import run_bass_kernel_spmd

    nc = bacc.Bacc("TRN2", target_bir_lowering=False, num_devices=1)
    arrays, io = {}, {}
    for name, given in NAMES.items():
        a = np.ascontiguousarray(inputs[given])
        arrays["in_" + name] = a
        io[name] = nc.dram_tensor("in_" + name, a.shape, mybir.dt.from_np(a.dtype), kind="ExternalInput").ap()
    out = nc.dram_tensor("out", (B, T, D), FP32, kind="ExternalOutput").ap()
    program(nc, io, out)
    result = run_bass_kernel_spmd(nc, [arrays], core_ids=[0])
    return result.results[0]["out"]
```
